# Optimizing a Trainium2 kernel written in Bass

```python
import numpy as np
import jax
import jax.numpy as jnp

def _softmax(x, axis=-1):
    return jax.nn.softmax(x, axis=axis)

def _gelu(x):
    return jax.nn.gelu(x, approximate=True)

def _silu(x):
    return jax.nn.silu(x)

def _sigmoid(x):
    return jax.nn.sigmoid(x)

def _layernorm(x, axis=-1, eps=1e-05):
    m = jnp.mean(x, axis=axis, keepdims=True)
    v = jnp.var(x, axis=axis, keepdims=True)
    return (x - m) / jnp.sqrt(v + eps)

def _scatter_add(tgt, idx, src, axis=0):
    return tgt.at[idx].add(src)

def _segment_sum(src, seg, n):
    return jax.ops.segment_sum(src, seg, n)
kernel_name = 'mk_prb_d1_jaxref_r8_0198f3'

def setup_inputs(seed: int=0):
    np.random.seed(seed)
    _w = jnp.asarray

    def _L0_attn_setup():
        import jax, jax.numpy as jnp
        import numpy as np
        CHUNK = 64
        HEADS = 16

        def _chunk_mask(T, cs):
            idx = jnp.arange(T)
            blk = idx // cs * cs
            qb = blk[:, None]
            kb = blk[None, :]
            masked = (qb >= kb) & (idx[None, :] - idx[:, None] - 2 * (kb - qb) >= 1)
            return masked
        key = jax.random.key(seed)
        ks = jax.random.split(key, 6)
        B, T, C = (2, 256, 128)
        w = 0.02
        return {'x': jax.random.normal(ks[0], (B, T, C), jnp.float32), 'Wq': jax.random.normal(ks[1], (C, C), jnp.float32) * w, 'bq': jnp.zeros((C,), jnp.float32), 'Wk': jax.random.normal(ks[2], (C, C), jnp.float32) * w, 'bk': jnp.zeros((C,), jnp.float32), 'Wv': jax.random.normal(ks[3], (C, C), jnp.float32) * w, 'bv': jnp.zeros((C,), jnp.float32), 'Wo': jax.random.normal(ks[4], (C, C), jnp.float32) * w, 'bo': jnp.zeros((C,), jnp.float32), 'attn_scale': jnp.full((1,), 1.0 / np.sqrt(C // HEADS), jnp.float32)}
    _L0_attn_in = _L0_attn_setup()

    def _L0_ffn_setup():
        import jax, jax.numpy as jnp
        import numpy as np
        B, S = (4, 256)
        D_MODEL, D_FF, N_EXPERTS, TOP_K = (128, 512, 8, 2)
        T = B * S
        CAPACITY_FACTOR, MIN_CAP = (1.25, 4)
        CAP = max(int(CAPACITY_FACTOR * (T * TOP_K / N_EXPERTS)), MIN_CAP)
        key = jax.random.key(seed)
        ks = jax.random.split(key, 6)

        def w(k, shape, fan):
            return jax.random.normal(k, shape, jnp.float32) * fan ** (-0.5)
        return {'x': jax.random.normal(ks[0], (B, S, D_MODEL), jnp.float32), 'Wr': w(ks[1], (D_MODEL, N_EXPERTS), D_MODEL), 'W1': w(ks[2], (N_EXPERTS, D_MODEL, D_FF), D_MODEL), 'b1': jnp.zeros((N_EXPERTS, D_FF), jnp.float32), 'W2': w(ks[3], (N_EXPERTS, D_FF, D_MODEL), D_FF), 'b2': jnp.zeros((N_EXPERTS, D_MODEL), jnp.float32), 'fw1': w(ks[4], (D_MODEL, D_FF), D_MODEL), 'fb1': jnp.zeros((D_FF,), jnp.float32), 'fw2': w(ks[5], (D_FF, D_MODEL), D_FF), 'fb2': jnp.zeros((D_MODEL,), jnp.float32)}
    _L0_ffn_in = _L0_ffn_setup()
    _d = {'L0_attn_x': _L0_attn_in['x'], 'L0_attn_Wq': _L0_attn_in['Wq'], 'L0_attn_bq': _L0_attn_in['bq'], 'L0_attn_Wk': _L0_attn_in['Wk'], 'L0_attn_bk': _L0_attn_in['bk'], 'L0_attn_Wv': _L0_attn_in['Wv'], 'L0_attn_bv': _L0_attn_in['bv'], 'L0_attn_Wo': _L0_attn_in['Wo'], 'L0_attn_bo': _L0_attn_in['bo'], 'L0_attn_attn_scale': _L0_attn_in['attn_scale'], 'L0_ffn_Wr': _L0_ffn_in['Wr'], 'L0_ffn_W1': _L0_ffn_in['W1'], 'L0_ffn_b1': _L0_ffn_in['b1'], 'L0_ffn_W2': _L0_ffn_in['W2'], 'L0_ffn_b2': _L0_ffn_in['b2'], 'L0_ffn_fw1': _L0_ffn_in['fw1'], 'L0_ffn_fb1': _L0_ffn_in['fb1'], 'L0_ffn_fw2': _L0_ffn_in['fw2'], 'L0_ffn_fb2': _L0_ffn_in['fb2']}
    _x0 = _d['L0_attn_x']
    _d['L0_attn_x'] = jax.random.normal(jax.random.fold_in(jax.random.key(seed), 1), (8, 512, 128), dtype=_x0.dtype)
    del _x0
    return _d

def reference(L0_attn_x, L0_attn_Wq, L0_attn_bq, L0_attn_Wk, L0_attn_bk, L0_attn_Wv, L0_attn_bv, L0_attn_Wo, L0_attn_bo, L0_attn_attn_scale, L0_ffn_Wr, L0_ffn_W1, L0_ffn_b1, L0_ffn_W2, L0_ffn_b2, L0_ffn_fw1, L0_ffn_fb1, L0_ffn_fw2, L0_ffn_fb2):

    def _L0_attn_ref(x, Wq, bq, Wk, bk, Wv, bv, Wo, bo, attn_scale):
        import jax, jax.numpy as jnp
        import numpy as np
        CHUNK = 64
        HEADS = 16

        def _chunk_mask(T, cs):
            idx = jnp.arange(T)
            blk = idx // cs * cs
            qb = blk[:, None]
            kb = blk[None, :]
            masked = (qb >= kb) & (idx[None, :] - idx[:, None] - 2 * (kb - qb) >= 1)
            return masked
        B, T, C = x.shape
        H = HEADS
        D = C // H
        q = (x @ Wq.T + bq).reshape(B, T, H, D)
        k = (x @ Wk.T + bk).reshape(B, T, H, D)
        v = (x @ Wv.T + bv).reshape(B, T, H, D)
        scores = jnp.einsum('bqhd,bkhd->bhqk', q, k) * attn_scale[0]
        mask = _chunk_mask(T, CHUNK)
        scores = jnp.where(mask[None, None], -jnp.inf, scores)
        attn = jax.nn.softmax(scores, axis=-1)
        out = jnp.einsum('bhqk,bkhd->bqhd', attn, v).reshape(B, T, C)
        return out @ Wo.T + bo

    def _L0_ffn_ref(x, Wr, W1, b1, W2, b2, fw1, fb1, fw2, fb2):
        import jax, jax.numpy as jnp
        import numpy as np
        B, S = (4, 256)
        D_MODEL, D_FF, N_EXPERTS, TOP_K = (128, 512, 8, 2)
        T = B * S
        CAPACITY_FACTOR, MIN_CAP = (1.25, 4)
        CAP = max(int(CAPACITY_FACTOR * (T * TOP_K / N_EXPERTS)), MIN_CAP)
        Bx, Sx, D = x.shape
        Tn = Bx * Sx
        xf = x.reshape(Tn, D)
        logits = xf @ Wr
        probs = jax.nn.softmax(logits, axis=-1)
        scores, experts = jax.lax.top_k(probs, TOP_K)
        scores = scores / jnp.maximum(scores.sum(-1, keepdims=True), 1e-09)
        y_fb = jax.nn.gelu(xf @ fw1 + fb1, approximate=False) @ fw2 + fb2
        y = jnp.zeros_like(xf)
        fb_mask = jnp.zeros((Tn,), bool)
        for e in range(N_EXPERTS):
            assign = experts == e
            w_e = jnp.where(assign, scores, 0.0).sum(-1)
            eligible = assign.any(-1) & ~fb_mask
            rank = jnp.cumsum(eligible.astype(jnp.int32)) - 1
            keep = eligible & (rank < CAP)
            overflow = eligible & ~keep
            fb_mask = fb_mask | overflow
            y = jnp.where(overflow[:, None], y_fb, y)
            idx = jnp.nonzero(keep, size=CAP, fill_value=0)[0]
            valid = jnp.arange(CAP) < keep.sum()
            h = jax.nn.gelu(xf[idx] @ W1[e] + b1[e], approximate=False)
            y_e = h @ W2[e] + b2[e]
            y = y.at[idx].add(y_e * (w_e[idx] * valid)[:, None])
        return y.reshape(Bx, Sx, D)
    x = L0_attn_x
    xn = _layernorm(x, axis=-1)
    x = x + _L0_attn_ref(xn, L0_attn_Wq, L0_attn_bq, L0_attn_Wk, L0_attn_bk, L0_attn_Wv, L0_attn_bv, L0_attn_Wo, L0_attn_bo, L0_attn_attn_scale) + _L0_ffn_ref(xn, L0_ffn_Wr, L0_ffn_W1, L0_ffn_b1, L0_ffn_W2, L0_ffn_b2, L0_ffn_fw1, L0_ffn_fb1, L0_ffn_fw2, L0_ffn_fb2)
    return x

_drawn_inputs = setup_inputs


def setup_inputs(seed=0):
    import zlib

    import numpy as np

    out = dict(_drawn_inputs(seed))
    spreads = {'L0_attn_bq': (0.0, 0.8),
     'L0_attn_bk': (0.0, 2.0),
     'L0_attn_bv': (0.0, 0.449),
     'L0_attn_bo': (0.0, 0.1),
     'L0_ffn_b1': (0.0, 0.343),
     'L0_ffn_b2': (0.0, 0.281),
     'L0_ffn_fb1': (0.0, 0.1),
     'L0_ffn_fb2': (0.0, 0.1)}
    factors = {'L0_attn_Wq': 8.0, 'L0_attn_Wk': 8.0, 'L0_attn_Wv': 8.0, 'L0_attn_Wo': 3.034}
    for name, (base, spread) in spreads.items():
        noise = np.random.default_rng([zlib.crc32(name.encode()), seed]).standard_normal(out[name].shape)
        drawn = base * np.exp(spread * noise) if base else spread * noise
        out[name] = jnp.asarray(drawn.astype(out[name].dtype))
    for name, factor in factors.items():
        out[name] = (out[name] * factor).astype(out[name].dtype)
    return out
```

```python
from contextlib import ExitStack

import concourse.bass as bass
from concourse import mybir

ALU = mybir.AluOpType
ACT = mybir.ActivationFunctionType
AX = mybir.AxisListType
F32 = mybir.dt.float32
BF16 = mybir.dt.bfloat16
I32 = mybir.dt.int32

P = 128
B, T = 8, 512
TOK = B * T
TPB = T // P
NT = TOK // P
H, D = 16, 8
G = 4
W = 32
CHUNK = 64
F = 512
FC = F // P
E, TOPK = 8, 2
CAP = max(int(1.25 * (1024 * TOPK / E)), 4)
SLOTS = E * CAP
ST = [(0, P), (P, P), (2 * P, CAP - 2 * P)]
NPARTS = 3
QROWS = 3 * 32
EPS = 1e-5
FAR = 1.0e6
HUGE = 3.0e38
MASKED = -1.0e30
SROWS = QROWS + 2
SLOT = 1024
UNIT = 1024
RING = 10


class Count:

    def __init__(self, sem, base=0):
        self.sem, self.base, self.n = sem, base, 0

    def inc(self, ins):
        self.n += 1
        ins.then_inc(self.sem, 1)
        return ins

    def wait(self, eng):
        eng.wait_ge(self.sem, self.base + self.n)


def moe_attention_kernel(nc, x, Wq, bq, Wk, bk, Wv, bv, Wo, bo, attn_scale,
                         Wr, W1, b1, W2, b2, fw1, fb1, fw2, fb2, out):
    qp_d = nc.dram_tensor("qp_d", (NPARTS, P, TOK), BF16, kind="Internal").ap()
    kp_d = nc.dram_tensor("kp_d", (NPARTS, P, TOK), BF16, kind="Internal").ap()
    xnT_d = nc.dram_tensor("xnT_d", (P, TOK), F32, kind="Internal").ap()
    xg_d = nc.dram_tensor("xg_d", (SLOTS, P), F32, kind="Internal").ap()
    sh_d = nc.dram_tensor("sh_d", (B, P, P), BF16, kind="Internal").ap()
    y_d = nc.dram_tensor("y_d", (SLOTS, P), F32, kind="Internal").ap()

    x_rows = x.rearrange("b t c -> (b t) c")
    out_rows = out.rearrange("b t c -> (b t) c")

    ctx = ExitStack()
    with ctx:
        def sb(name, shape, dt=F32, c=ctx):
            return c.enter_context(nc.sbuf_tensor(name, shape, dt))

        def banks(name, n, c, dt=F32):
            return c.enter_context(nc.psum_tensor(name, [P, n, 512], dt))

        def sem(name):
            return ctx.enter_context(nc.semaphore(name))

        s_pass = sem("waits_passed")

        x_all = sb("x_all", [P, NT, P])
        yfb_all = sb("yfb_all", [P, NT, P])
        wT = sb("wT", [P, 4, P])
        ident = sb("ident", [P, P])
        keep_min = sb("keep_min", [P, P])
        BC = [("b2", E * P), ("fb2", P), ("bv", P), ("bo", P), ("scale", 1)]
        bc_at, w0 = {}, 0
        for name, n in BC:
            bc_at[name] = w0
            w0 += n
        NBC = w0
        bc = sb("bc", [P, NBC])
        NBR = E * FC + FC + 2
        bT = sb("bT", [P, NBR])
        idx = sb("idx", [P, TOPK, NT], I32)
        wgt = sb("wgt", [P, TOPK + 1, NT])

        c12 = ctx.enter_context(ExitStack())
        xn_all = sb("xn_all", [P, NT, P], c=c12)
        c1 = ExitStack()
        xn_s = sb("xn_s", [P, 2, TPB, P], c=c1)
        xnT = sb("xnT", [P, 2, T], c=c1)
        wn = sb("wn", [P, 4, P], c=c1)
        wr_s = sb("wr_s", [P, E], c=c1)
        brows = sb("brows", [NBR, P], c=c1)
        bcrow = sb("bcrow", [1, NBC], c=c1)
        ones_row = sb("ones_row", [1, P], c=c1)
        ones_bf = sb("ones_bf", [P, P], BF16, c=c1)
        after_bf = sb("after_bf", [P, P], BF16, c=c1)
        stats = sb("stats", [P, NT, 6], c=c1)
        mv = sb("mv", [P, NT, 2], c=c1)
        vare = sb("vare", [P, NT], c=c1)
        rstd = sb("rstd", [P, NT], c=c1)
        mhalf = sb("mhalf", [P, NT], c=c1)
        qs = sb("qs", [P, 2, T], c=c1)
        rem = sb("rem", [P, 2, T], c=c1)
        parts = sb("parts", [P, 2, 2, NPARTS, T], BF16, c=c1)
        logits = sb("logits", [P, NT, E], c=c1)
        pr = sb("pr", [P, NT, E], c=c1)
        tmp = sb("tmp", [P, NT, E], c=c1)
        tmp2 = sb("tmp2", [P, NT, E], c=c1)
        m1 = sb("m1", [P, NT, E], c=c1)
        m2 = sb("m2", [P, NT, E], c=c1)
        assign = sb("assign", [P, NT, E], c=c1)
        slotk = sb("slotk", [P, NT, E], c=c1)
        w8 = sb("w8", [P, E], c=c1)
        rsm = sb("rsm", [P, 8, NT], c=c1)
        elig = sb("elig", [P, 2, NT], BF16, c=c1)
        escan = sb("escan", [P, 2, NT], BF16, c=c1)
        ones_nt = sb("ones_nt", [P, NT], c=c1)
        rank = sb("rank", [P, NT], c=c1)
        ovf = sb("ovf", [P, NT], c=c1)
        zero = sb("zero", [P, SLOTS // P * P], c=c1)
        pt = banks("pt", 1, c1)
        pq = banks("pq", 2, c1)
        pl = banks("pl", 1, c1)
        ph = banks("ph", 2, c1)
        pw = banks("pw", 1, c1)

        s_x = [sem(f"x_loaded{i}") for i in range(4)]
        s_wn = sem("wn_loaded")
        s_wl = sem("weights_loaded")
        s_rows = sem("rows_loaded")
        s_const = sem("consts_ready")
        s_c0 = sem("const_chain")
        s_c1 = sem("mask_chain")
        s_xl = [sem(f"xnT_loaded{i}") for i in range(2)]
        s_zero = sem("zero_ready")
        s_xgz = sem("xg_zeroed")
        s_wt = sem("wt_in_psum")
        s_wtc = sem("wt_copied")
        s_dv = sem("dve_chain")
        s_bs = sem("x_statistics")
        s_rs = sem("rstd_ready")
        s_xn = sem("xn_ready")
        s_xnc = sem("xn_kept")
        s_tr = sem("xnT_in_psum")
        s_xnT = sem("xnT_ready")
        s_qk = sem("qk_in_psum")
        s_qs = sem("qs_ready")
        s_p1 = sem("part1_ready")
        s_r1 = sem("rem_ready")
        s_p2 = sem("part2_ready")
        s_p3 = sem("part3_ready")
        s_st = [sem(f"parts_stored{i}") for i in range(2)]
        s_lg = sem("logits_in_psum")
        s_lc = sem("logits_copied")
        s_h = sem("h_in_psum")
        s_g = sem("gelu_done")
        s_y = sem("yfb_in_psum")
        s_yc = sem("yfb_copied")
        s_z = sem("shifted_logits")
        s_e = sem("exp_logits")
        s_el = sem("eligible_ready")
        s_rk = sem("rank_in_psum")
        s_ix = sem("slots_ready")
        s_sc = sem("rows_scattered")
        s_we = [sem(f"expert_loaded{i}") for i in range(2)]
        s_xt = sem("xgT_in_psum")
        s_xtc = sem("xgT_ready")
        s_h2 = sem("expert_h_in_psum")
        s_g2 = sem("expert_gelu_done")
        s_y2 = sem("expert_y_in_psum")
        s_y2c = sem("expert_y_ready")
        s_yst = sem("expert_y_stores_done")
        s_ys = [sem(f"expert_y_stored{i}") for i in range(2)]

        def bcast(name, n=P):
            return bc[:, bc_at[name]:bc_at[name] + n]

        B1C, FB1C, BQC, BKC = 0, E * FC, E * FC + FC, E * FC + FC + 1
        NG1 = 4

        with c1, nc.Block() as block:

            @block.sync
            def _(sp):
                sp.sem_inc(s_st[0], 1)
                sp.sem_inc(s_st[1], 1)
                for c in range(4):
                    t0 = c * NT // 4
                    sp.dma_start(x_all[:, t0:t0 + NT // 4, :],
                                 x_rows[t0 * P:(t0 + NT // 4) * P, :].rearrange("(n p) c -> p n c", p=P)).then_inc(s_x[c], 16)
                    if c == 0:
                        for n, w in enumerate((Wq, Wk, Wv, Wo)):
                            sp.dma_start(wn[:, n, :], w).then_inc(s_wn, 16)
                        sp.dma_start(brows[0:E * FC, :], b1.rearrange("e (c p) -> (e c) p", p=P)).then_inc(s_rows, 16)
                        sp.dma_start(brows[FB1C:FB1C + FC, :], fb1.rearrange("(c p) -> c p", p=P)).then_inc(s_rows, 16)
                        sp.dma_start(brows[BQC:BQC + 1, :], bq.rearrange("(a p) -> a p", a=1)).then_inc(s_rows, 16)
                        sp.dma_start(brows[BKC:BKC + 1, :], bk.rearrange("(a p) -> a p", a=1)).then_inc(s_rows, 16)
                        sp.dma_start(bcrow[:, 0:E * P], b2.rearrange("(a e) p -> a (e p)", a=1)).then_inc(s_rows, 16)
                        for name, v in (("fb2", fb2), ("bv", bv), ("bo", bo), ("scale", attn_scale)):
                            n = v.shape[0]
                            sp.dma_start(bcrow[:, bc_at[name]:bc_at[name] + n],
                                         v.rearrange("(a p) -> a p", a=1)).then_inc(s_rows, 16)
                        sp.dma_start(wr_s[:, :], Wr).then_inc(s_wl, 16)
                sp.wait_ge(s_zero, 1)
                sp.dma_start(xg_d.rearrange("(p n) c -> p (n c)", p=P), zero[:, :]).then_inc(s_xgz, 16)

                with sp.Fori(0, B // 2) as i:
                    for k in range(2):
                        n = 2 * i + k
                        sp.wait_ge(s_xnT, n + 1)
                        sp.sem_inc(s_pass, 1)
                        sp.dma_start(xnT_d[:, bass.ds(n * T, T)], xnT[:, k, :]).then_inc(s_st[k], 16)
                        sp.wait_ge(s_p3, 2 * n + 2)
                        sp.wait_ge(s_p2, 2 * n + 2)
                        sp.wait_ge(s_p1, 2 * n + 2)
                        sp.sem_inc(s_pass, 1)
                        for m, d in enumerate((qp_d, kp_d)):
                            sp.dma_start(d.rearrange("j p t -> p j t")[:, :, bass.ds(n * T, T)],
                                         parts[:, k, m, :, :]).then_inc(s_st[k], 16)
                for k in range(2):
                    sp.wait_ge(s_st[k], 16 * 3 * (B // 2) + 1)
                sp.wait_ge(s_xgz, 16)

            @block.gpsimd
            def _(pool):
                ch = Count(s_c0)
                pool.sem_inc(s_xnc, 1)
                ch.inc(pool.memset(ident[:, :], 0.0))
                ch.inc(pool.memset(after_bf[:, :], 0.0))
                ch.inc(pool.memset(keep_min[:, :], HUGE))
                pool.memset(zero[:, :], 0.0).then_inc(s_zero, 1)
                pool.memset(ones_row[:, :], 1.0).then_inc(s_const, 1)
                pool.memset(ones_bf[:, :], 1.0).then_inc(s_const, 1)
                pool.memset(ones_nt[:, :], 1.0).then_inc(s_const, 1)
                ch.wait(pool)
                pool.affine_select(out=ident[:, :], in_=ident[:, :], compare_op=ALU.not_equal, fill=1.0,
                                   base=0, pattern=[[-1, P]], channel_multiplier=1).then_inc(s_const, 1)
                pool.affine_select(out=after_bf[:, :], in_=after_bf[:, :], compare_op=ALU.is_ge, fill=-1.0,
                                   base=0, pattern=[[1, P]], channel_multiplier=-1).then_inc(s_const, 1)
                for lo, base, step, channel, fill in ((CHUNK, -CHUNK, 0, 1, 0.0), (CHUNK, CHUNK, 1, -1, 0.0),
                                                      (0, 0, 1, -1, 0.0), (0, CHUNK - 1, 0, -1, HUGE)):
                    half = keep_min[:, lo:lo + CHUNK]
                    ch.inc(pool.affine_select(out=half, in_=half, compare_op=ALU.is_ge, fill=fill, base=base,
                                              pattern=[[step, CHUNK]], channel_multiplier=channel))
                    ch.wait(pool)
                for e in range(E):
                    ins = pool.memset(w8[:, e:e + 1], float(E - e))
                ins.then_inc(s_const, 1)
                ch.inc(pool.memset(mhalf[:, :], -0.5))
                ch.wait(pool)
                for c in range(4):
                    pool.wait_ge(s_bs, 3 * c + 3)
                    tiles = slice(c * NT // 4, (c + 1) * NT // 4)
                    pool.tensor_tensor(rstd[:, tiles], vare[:, tiles], mhalf[:, tiles], ALU.pow).then_inc(s_rs, 1)
                with pool.Fori(0, B // 2) as i:
                    for k in range(2):
                        n = 2 * i + k
                        pool.wait_ge(s_xn, n + 1)
                        pool.tensor_copy(xn_all[:, bass.ds(n * TPB, TPB), :], xn_s[:, k, :, :]).then_inc(s_xnc, 1)
                pool.wait_ge(s_xnc, B + 1)

            @block.vector
            def _(dve):
                dve.sem_inc(s_qs, 1)
                dve.sem_inc(s_lc, 1)

                def layer_norm(n, k, ch):
                    if not isinstance(n, int) or n >= 2:
                        dve.wait_ge(s_tr, n)
                        dve.wait_ge(s_xnc, n)
                    for j in range(TPB):
                        ins = dve.tensor_scalar(xn_s[:, k, j, :],
                                                x_all[:, n * TPB + j, :] if isinstance(n, int)
                                                else x_all[:, bass.ds(n * TPB + j, 1), :].rearrange("p a c -> p (a c)"),
                                                mv[:, n * TPB + j, 0:1] if isinstance(n, int) else mv[:, bass.ds(n * TPB + j, 1), 0],
                                                rstd[:, n * TPB + j:n * TPB + j + 1] if isinstance(n, int)
                                                else rstd[:, bass.ds(n * TPB + j, 1)], ALU.subtract, ALU.mult)
                        ch.inc(ins)
                    ch.wait(dve)
                    dve.sem_inc(s_xn, 1)

                def statistics(c):
                    tiles = range(c * NT // 4, (c + 1) * NT // 4)
                    dve.wait_ge(s_x[c], 16)
                    for t in tiles:
                        ins = dve.bn_stats(stats[:, t, :], x_all[:, t, :])
                    ins.then_inc(s_bs, 1)
                    dve.wait_ge(s_bs, 3 * c + 1)
                    for t in tiles:
                        ins = dve.bn_aggr(mv[:, t, :], stats[:, t, :])
                    ins.then_inc(s_bs, 1)
                    dve.wait_ge(s_bs, 3 * c + 2)
                    dve.tensor_scalar(vare[:, tiles[0]:tiles[-1] + 1], mv[:, tiles[0]:tiles[-1] + 1, 1], EPS, None,
                                      ALU.add).then_inc(s_bs, 1)

                def batch(i, k, ch, last=False):
                    n = 2 * i + k
                    for m, col in ((0, BQC), (1, BKC)):
                        dve.wait_ge(s_qk, 2 * n + m + 1)
                        if m == 0:
                            dve.tensor_scalar(qs[:, m, :], pq[:, m, :], bT[:, col:col + 1], bcast("scale", 1),
                                              ALU.add, ALU.mult).then_inc(s_qs, 1)
                        else:
                            dve.tensor_scalar(qs[:, m, :], pq[:, m, :], bT[:, col:col + 1], None,
                                              ALU.add).then_inc(s_qs, 1)
                    for m in range(2):
                        dve.wait_ge(s_p1, 2 * n + m + 1)
                        dve.tensor_tensor(rem[:, m, :], qs[:, m, :], parts[:, k, m, 0, :], ALU.subtract).then_inc(s_r1, 1)
                    dve.wait_ge(s_lg, n + 1)
                    dve.tensor_copy(logits[:, bass.ds(n * TPB, TPB), :],
                                    pl[:, 0, 0:TPB * E].rearrange("p (j e) -> p j e", e=E)).then_inc(s_lc, 1)
                    for m in range(2):
                        dve.wait_ge(s_p2, 2 * n + m + 1)
                        dve.tensor_tensor(parts[:, k, m, 2, :], rem[:, m, :], parts[:, k, m, 1, :],
                                          ALU.subtract).then_inc(s_p3, 1)
                    if not last:
                        layer_norm(n + 1, 1 - k, ch)

                PER = 2 * TPB
                ch = Count(s_dv)
                statistics(0)
                dve.wait_ge(s_rs, 1)
                layer_norm(0, 0, ch)
                assert ch.n == PER // 2
                for c in range(1, 4):
                    statistics(c)
                dve.wait_ge(s_rs, 4)
                dve.wait_ge(s_wtc, NG1 + 2)
                with dve.Fori(0, B // 2 - 1) as i:
                    cl = Count(s_dv, PER // 2 + i * PER)
                    batch(i, 0, cl)
                    batch(i, 1, cl)
                    assert cl.n == PER
                i = B // 2 - 1
                cl = Count(s_dv, PER // 2 + i * PER)
                batch(i, 0, cl)
                batch(i, 1, cl, last=True)
                ch = Count(s_dv, PER * (B // 2))
                dve.wait_ge(s_lc, B + 1)
                dve.wait_ge(s_const, 6)

                def bc8(a):
                    return a.unsqueeze(2).to_broadcast([P, NT, E])

                mx, sm, p1, p2, fb, fbn, t1, t2 = (rsm[:, j, :] for j in range(8))
                w8b = w8[:, :].unsqueeze(1).to_broadcast([P, NT, E])

                def step(ins):
                    ch.inc(ins)
                    ch.wait(dve)

                step(dve.tensor_reduce(mx, logits[:, :, :], AX.X, ALU.max))
                dve.tensor_tensor(tmp[:, :, :], logits[:, :, :], bc8(mx), ALU.subtract).then_inc(s_z, 1)
                dve.wait_ge(s_e, 1)
                step(dve.tensor_reduce(sm, pr[:, :, :], AX.X, ALU.add))
                step(dve.reciprocal(sm, sm))
                step(dve.tensor_tensor(pr[:, :, :], pr[:, :, :], bc8(sm), ALU.mult))
                for m, p, mask in ((0, p1, m1), (1, p2, m2)):
                    step(dve.tensor_reduce(p, pr[:, :, :], AX.X, ALU.max))
                    step(dve.tensor_tensor(tmp[:, :, :], pr[:, :, :], bc8(p), ALU.is_equal))
                    step(dve.tensor_tensor(tmp[:, :, :], tmp[:, :, :], w8b, ALU.mult))
                    step(dve.tensor_reduce(t1, tmp[:, :, :], AX.X, ALU.max))
                    step(dve.tensor_tensor(mask[:, :, :], tmp[:, :, :], bc8(t1), ALU.is_equal))
                    if m == 0:
                        step(dve.scalar_tensor_tensor(out=pr[:, :, :], in0=mask[:, :, :], scalar=-2.0,
                                                      in1=pr[:, :, :], op0=ALU.mult, op1=ALU.add))
                step(dve.tensor_tensor(assign[:, :, :], m1[:, :, :], m2[:, :, :], ALU.add))
                step(dve.tensor_tensor(t1, p1, p2, ALU.add))
                step(dve.tensor_scalar(t1, t1, 1e-9, None, ALU.max))
                step(dve.reciprocal(t1, t1))
                step(dve.tensor_tensor(p1, p1, t1, ALU.mult))
                step(dve.tensor_tensor(p2, p2, t1, ALU.mult))
                step(dve.memset(fb, 0.0))
                for e in range(E):
                    a = e % 2
                    step(dve.scalar_tensor_tensor(out=elig[:, a, :], in0=fb, scalar=0.0, in1=assign[:, :, e],
                                                  op0=ALU.is_equal, op1=ALU.mult))
                    dve.tensor_tensor_scan(escan[:, a, :], ones_nt[:, :], elig[:, a, :], 0.0,
                                           ALU.mult, ALU.add).then_inc(s_el, 1)
                    dve.wait_ge(s_rk, e + 1)
                    step(dve.tensor_copy(rank[:, :], pw[:, 0, 0:NT]))
                    step(dve.scalar_tensor_tensor(out=ovf[:, :], in0=rank[:, :], scalar=float(CAP),
                                                  in1=elig[:, a, :], op0=ALU.is_gt, op1=ALU.mult))
                    step(dve.tensor_tensor(fb, fb, ovf[:, :], ALU.max))
                    step(dve.tensor_scalar(slotk[:, :, e], rank[:, :], float(e * CAP - 1), None, ALU.add))
                step(dve.tensor_scalar(fbn, fb, -1.0, 1.0, ALU.mult, ALU.add))
                step(dve.tensor_copy(wgt[:, 2, :], fb))
                for m, p, mask in ((0, p1, m1), (1, p2, m2)):
                    step(dve.tensor_tensor(tmp[:, :, :], slotk[:, :, :], mask[:, :, :], ALU.mult))
                    step(dve.tensor_reduce(t1, tmp[:, :, :], AX.X, ALU.add))
                    step(dve.tensor_tensor(t1, t1, fbn, ALU.mult))
                    step(dve.scalar_tensor_tensor(out=t2, in0=fb, scalar=FAR, in1=t1, op0=ALU.mult, op1=ALU.add))
                    step(dve.tensor_copy(idx[:, m, :], t2))
                    step(dve.tensor_tensor(wgt[:, m, :], p, fbn, ALU.mult))
                dve.sem_inc(s_ix, 1)

            @block.scalar
            def _(act):
                act.wait_ge(s_wt, 1)
                act.activation(wT[:, :, :], pq[:, 0, :].rearrange("p (w c) -> p w c", c=P), ACT.Copy).then_inc(s_wtc, 1)
                act.wait_ge(s_wt, 2)
                act.activation(bT[:, :], pl[:, 0, 0:NBR], ACT.Copy).then_inc(s_wtc, 1)
                for c, bank in enumerate((pq[:, 1, :], ph[:, 0, :], ph[:, 1, :])):
                    act.wait_ge(s_wt, 3 + c)
                    n = min(512, NBC - c * 512)
                    act.activation(bc[:, c * 512:c * 512 + n], bank[:, 0:n], ACT.Copy).then_inc(s_wtc, 1)
                act.wait_ge(s_wtc, 5)
                act.sem_inc(s_wtc, 1)
                with act.Fori(0, B // 2) as i:
                    for k in range(2):
                        n = 2 * i + k
                        act.wait_ge(s_tr, n + 2)
                        act.wait_ge(s_st[k], 48 * i + 1)
                        act.activation(xnT[:, k, :], pt[:, 0, :], ACT.Copy).then_inc(s_xnT, 1)
                        for m in range(2):
                            act.wait_ge(s_qs, 2 * n + m + 2)
                            act.activation(parts[:, k, m, 0, :], qs[:, m, :], ACT.Copy).then_inc(s_p1, 1)
                        for m in range(2):
                            act.wait_ge(s_r1, 2 * n + m + 1)
                            act.activation(parts[:, k, m, 1, :], rem[:, m, :], ACT.Copy).then_inc(s_p2, 1)
                act.wait_ge(s_z, 1)
                act.activation(pr[:, :, :], tmp[:, :, :], ACT.Exp).then_inc(s_e, 1)

            @block.tensor
            def _(pe):
                pe.sem_inc(s_tr, 1)
                pe.wait_ge(s_const, 6)
                pe.wait_ge(s_wn, 64)
                for w in range(4):
                    mm = pe.transpose(pq[:, 0, w * P:(w + 1) * P], wn[:, w, :], ident[:, :])
                mm.then_inc(s_wt, 1)
                pe.wait_ge(s_rows, 16 * 9)
                pe.transpose(pl[:, 0, 0:NBR], brows[:, :], ident[0:NBR, 0:NBR]).then_inc(s_wt, 1)
                for c, bank in enumerate((pq[:, 1, :], ph[:, 0, :], ph[:, 1, :])):
                    n = min(512, NBC - c * 512)
                    pe.matmul(bank[:, 0:n], ones_row[:, :], bcrow[:, c * 512:c * 512 + n],
                              start=True, stop=True).then_inc(s_wt, 1)
                pe.wait_ge(s_wl, 16)
                pe.wait_ge(s_wtc, NG1 + 2)
                with pe.Fori(0, B // 2) as i:
                    for k in range(2):
                        n = 2 * i + k
                        pe.wait_ge(s_xn, n + 1)
                        for j in range(TPB):
                            mm = pe.transpose(pt[:, 0, j * P:(j + 1) * P], xn_s[:, k, j, :], ident[:, :])
                        mm.then_inc(s_tr, 1)
                        pe.wait_ge(s_xnT, n + 1)
                        pe.wait_ge(s_qs, 2 * n + 1)
                        for m in range(2):
                            pe.matmul(pq[:, m, :], wT[:, m, :], xnT[:, k, :], start=True, stop=True).then_inc(s_qk, 1)
                        pe.wait_ge(s_lc, n + 1)
                        for j in range(TPB):
                            mm = pe.matmul(pl[:, 0, j * E:(j + 1) * E], xnT[:, k, j * P:(j + 1) * P], wr_s[:, :],
                                           start=True, stop=True)
                        mm.then_inc(s_lg, 1)
                for e in range(E):
                    a = e % 2
                    pe.wait_ge(s_el, e + 1)
                    pe.matmul(pw[:, 0, 0:NT], ones_bf[:, :], escan[:, a, :], start=True, stop=False)
                    pe.matmul(pw[:, 0, 0:NT], after_bf[:, :], elig[:, a, :], start=False, stop=True).then_inc(s_rk, 1)

        cm = ExitStack()
        qm = sb("qm", [P, 2, H, T], BF16, c=cm)
        km = sb("km", [P, 2, H, T], BF16, c=cm)
        xT1 = sb("xT1", [P, 2, T], c=cm)
        fw1_s = sb("fw1_s", [P, F], c=cm)
        fw2_s = sb("fw2_s", [P, FC, P], c=cm)
        hT = sb("hT", [P, 2, FC, T], c=cm)
        w1_s = sb("w1_s", [P, 2, F], c=cm)
        w2_s = sb("w2_s", [P, 2, FC, P], c=cm)
        xg_s = sb("xg_s", [P, 2, 3, P], c=cm)
        xgT = sb("xgT", [P, 2, CAP], c=cm)
        y_s = sb("y_s", [P, 2, 3, P], c=cm)
        hide = sb("hide", [P, P], BF16, c=cm)
        ident_bf = sb("ident_bf", [P, P], BF16, c=cm)
        blkmax = sb("blkmax", [P, 2, H * 10], c=cm)
        negm = sb("negm", [P, H, TPB], c=cm)
        shift = sb("shift", [P, 2, H, TPB], BF16, c=cm)
        shT = sb("shT", [P, 2, P], BF16, c=cm)
        pm = banks("pm", 4, cm)
        ph = banks("ph2", 2, cm)
        py = banks("py", 1, cm)
        pt2 = banks("pt2", 1, cm)

        b_c = sem("b_consts")
        b_w = sem("b_weights_loaded")
        b_ld = [sem(f"b_qk_loaded{i}") for i in range(2)]
        b_s = sem("b_scores_in_psum")
        b_m = sem("b_block_maxima")
        b_n = sem("b_negated_maxima")
        b_hi = sem("b_shift_high")
        b_sh = sem("b_shift_ready")
        b_t = sem("b_shift_in_psum")
        b_tc = sem("b_shiftT_ready")
        b_st = [sem(f"b_shift_stored{i}") for i in range(2)]

        def slot_pieces(s):
            out, at = [], 0
            for h in range(H):
                for qt in range(TPB):
                    done, n = 0, TPB - qt
                    while done < n:
                        g = at // 8
                        m = min(n - done, 4 - at % 4)
                        if g == s:
                            out.append((h, qt, qt + done, m, at % 8))
                        at += m
                        done += m
            return out

        NS = H * 10 // 8

        with cm, nc.Block() as block:

            @block.sync
            def _(sp):
                sp.dma_start(fw1_s[:, :], fw1).then_inc(b_w, 16)
                sp.dma_start(fw2_s[:, :, :], fw2.rearrange("(c p) n -> p c n", p=P)).then_inc(b_w, 16)
                sp.wait_ge(b_c, 4)

                def load_qk(n, k, i):
                    sp.wait_ge(b_s, n * NS + NS)
                    sp.sem_inc(s_pass, 1)
                    for a in range(NPARTS):
                        for c in range(NPARTS):
                            r = 32 * a + D * c
                            sp.dma_start(qm[r:r + D, k, :, :],
                                         qp_d[a].rearrange("(h d) t -> d h t", d=D)[:, :, bass.ds(n * T, T)]).then_inc(b_ld[k], 16)
                            sp.dma_start(km[r:r + D, k, :, :],
                                         kp_d[c].rearrange("(h d) t -> d h t", d=D)[:, :, bass.ds(n * T, T)]).then_inc(b_ld[k], 16)

                HB = B // 4
                with sp.Fori(0, HB) as i:
                    for k in range(2):
                        n = 2 * i + k
                        load_qk(n, k, i)
                        for j in range(2):
                            sp.wait_ge(s_y, 2 * n + j + 1)
                            sp.sem_inc(s_pass, 1)
                            sp.dma_start(xT1[:, j, :], xnT_d[:, bass.ds((2 * n + j) * T, T)]).then_inc(s_xl[j], 16)
                sp.wait_ge(s_sc, 16 * TOPK * NT)
                with sp.Fori(0, HB) as i:
                    for k in range(2):
                        n = B // 2 + 2 * i + k
                        load_qk(n, k, i)
                        for j in range(2):
                            e = 2 * (2 * i + k) + j
                            sp.wait_ge(s_y2, e + 1)
                            sp.sem_inc(s_pass, 1)
                            sp.dma_start(w1_s[:, j, :], W1.rearrange("e d f -> (e d) f")[bass.ds(e * P, P), :]).then_inc(s_we[j], 16)
                            sp.dma_start(w2_s[:, j, :, :],
                                         W2.rearrange("e f d -> (e f) d")[bass.ds(e * F, F), :].rearrange("(c p) n -> p c n", p=P)).then_inc(s_we[j], 16)
                            sp.dma_start(xg_s[:, j, 0:2, :],
                                         xg_d[bass.ds(e * CAP, 2 * P), :].rearrange("(s p) c -> p s c", p=P)).then_inc(s_we[j], 16)
                            sp.dma_start(xg_s[0:CAP - 2 * P, j, 2, :],
                                         xg_d[bass.ds(e * CAP + 2 * P, CAP - 2 * P), :]).then_inc(s_we[j], 16)

            @block.gpsimd
            def _(pool):
                ch = Count(s_c1)
                pool.sem_inc(s_yst, 2)
                ch.inc(pool.memset(hide[:, :], 0.0))
                ch.inc(pool.memset(ident_bf[:, :], 0.0))
                ch.wait(pool)
                pool.affine_select(out=ident_bf[:, :], in_=ident_bf[:, :], compare_op=ALU.not_equal, fill=1.0,
                                   base=0, pattern=[[-1, P]], channel_multiplier=1).then_inc(b_c, 1)
                for lo, base, step, channel, fill in ((0, 0, -1, 1, MASKED), (0, CHUNK - 1, 0, -1, MASKED),
                                                      (CHUNK, -CHUNK, -1, 1, MASKED), (CHUNK, -CHUNK, 0, 1, 0.0)):
                    half = hide[:, lo:lo + CHUNK]
                    ch.inc(pool.affine_select(out=half, in_=half, compare_op=ALU.is_ge, fill=fill, base=base,
                                              pattern=[[step, CHUNK]], channel_multiplier=channel))
                    ch.wait(pool)
                pool.sem_inc(b_c, 1)
                for t in range(NT):
                    for a in range(TOPK):
                        pool.indirect_dma_start(
                            out=xg_d[:, :], out_offset=bass.IndirectOffsetOnAxis(ap=idx[:, a, t:t + 1], axis=0),
                            in_=xn_all[:, t, :], in_offset=None,
                            bounds_check=SLOTS - 1, oob_is_err=False).then_inc(s_sc, 16)
                with pool.Fori(0, E // 2) as i:
                    for k in range(2):
                        e = 2 * i + k
                        pool.wait_ge(s_y2c, e + 2)
                        pool.dma_start(y_d[bass.ds(e * CAP, 2 * P), :].rearrange("(s p) c -> p s c", p=P),
                                       y_s[:, k, 0:2, :]).then_inc(s_ys[k], 16)
                        pool.dma_start(y_d[bass.ds(e * CAP + 2 * P, CAP - 2 * P), :],
                                       y_s[0:CAP - 2 * P, k, 2, :]).then_inc(s_ys[k], 16)
                        pool.wait_ge(s_ys[k], 32 * i + 32)
                        pool.sem_inc(s_yst, 1)

            @block.vector
            def _(dve):
                dve.memset(qm[:, :, :, :], 0.0).then_inc(b_c, 1)
                dve.memset(km[:, :, :, :], 0.0).then_inc(b_c, 1)
                dve.sem_inc(b_m, 1)
                dve.sem_inc(b_sh, 1)
                dve.sem_inc(s_yc, 1)
                dve.sem_inc(s_y2c, 1)

                def maxima(n, k, extra):
                    for s in range(NS):
                        dve.wait_ge(b_s, 2 * NS + n * NS + s + 1)
                        dve.tensor_reduce(blkmax[:, k, s * 8:s * 8 + 8],
                                          pm[:, 2 * (s % 2):2 * (s % 2) + 2, :].rearrange("p a (b c) -> p (a b) c", c=P),
                                          AX.X, ALU.max).then_inc(b_m, 1)
                        if s in extra:
                            extra[s]()
                    dve.wait_ge(b_m, n * NS + NS + 1)
                    dve.wait_ge(b_sh, n + 1)
                    v, at = blkmax[:, k, :].rearrange("p (h b) -> p h b", h=H), 0
                    for qt in range(TPB):
                        ins = dve.tensor_reduce(negm[:, :, qt], v[:, :, at:at + TPB - qt], AX.X, ALU.max, negate=True)
                        at += TPB - qt
                        ins.then_inc(b_n, 1)
                    dve.wait_ge(b_n, TPB * n + TPB)
                    dve.wait_ge(b_t, n + 1)
                    dve.tensor_copy(shift[:, 0, :, :], negm[:, :, :]).then_inc(b_hi, 1)
                    dve.wait_ge(b_hi, n + 1)
                    dve.tensor_tensor(shift[:, 1, :, :], negm[:, :, :], shift[:, 0, :, :], ALU.subtract).then_inc(b_sh, 1)

                def fallback_out(m):
                    dve.wait_ge(s_y, m + 3)
                    dve.tensor_tensor(yfb_all[:, bass.ds(m * TPB, TPB), :],
                                      py[:, 0, :].rearrange("p (j c) -> p j c", c=P),
                                      bcast("fb2").unsqueeze(1).to_broadcast([P, TPB, P]), ALU.add).then_inc(s_yc, 1)

                def expert_out(e, j, i2):
                    dve.wait_ge(s_y2, e + 3)
                    dve.wait_ge(s_yst, e + 1)
                    dve.tensor_tensor(y_s[:, j, 0:2, :], py[:, 0, 0:2 * P].rearrange("p (s c) -> p s c", c=P),
                                      bc[:, bass.ds(e * P, P)].unsqueeze(1).to_broadcast([P, 2, P]), ALU.add)
                    dve.tensor_tensor(y_s[0:CAP - 2 * P, j, 2, :], py[0:CAP - 2 * P, 0, 2 * P:3 * P],
                                      bc[0:CAP - 2 * P, bass.ds(e * P, P)], ALU.add).then_inc(s_y2c, 1)

                with dve.Fori(0, B // 4) as i:
                    for k in range(2):
                        n = 2 * i + k
                        maxima(n, k, {8: lambda: fallback_out(2 * n), 18: lambda: fallback_out(2 * n + 1)})
                with dve.Fori(0, B // 4) as i:
                    for k in range(2):
                        n = 2 * i + k
                        maxima(B // 2 + n, k, {9: lambda: expert_out(2 * n, 0, n),
                                               19: lambda: expert_out(2 * n + 1, 1, n)})

            @block.scalar
            def _(act):
                act.sem_inc(b_tc, 1)
                act.sem_inc(s_g, 1)
                act.sem_inc(s_g2, 1)
                act.sem_inc(b_st[0], 1)
                act.sem_inc(b_st[1], 1)

                def shift_rows(n, k, i):
                    act.wait_ge(b_t, n + 2)
                    act.activation(shT[:, k, :], pt2[:, 0, 0:P // 2].bitcast(BF16), ACT.Copy).then_inc(b_tc, 1)
                    act.wait_ge(b_tc, n + 2)
                    act.dma_start(sh_d.rearrange("b r t -> (b r) t")[bass.ds(n * P, P), :], shT[:, k, :]).then_inc(b_st[k], 16)

                with act.Fori(0, B // 4) as i:
                    for k in range(2):
                        n = 2 * i + k
                        for j in range(2):
                            m = 2 * n + j
                            for c in range(FC):
                                act.wait_ge(s_h, FC * m + c + 1)
                                act.activation(hT[:, j, c, :], ph[:, c % 2, :], ACT.Gelu,
                                               bias=bT[:, FB1C + c:FB1C + c + 1]).then_inc(s_g, 1)
                        act.wait_ge(b_st[k], 16 * i + 1)
                        shift_rows(n, k, i)
                with act.Fori(0, B // 4) as i:
                    for k in range(2):
                        n = 2 * i + k
                        for j in range(2):
                            e = 2 * n + j
                            act.wait_ge(s_xt, e + 1)
                            act.activation(xgT[:, j, :], pt2[:, 0, 0:CAP], ACT.Copy).then_inc(s_xtc, 1)
                            for c in range(FC):
                                act.wait_ge(s_h2, FC * e + c + 1)
                                act.activation(hT[:, j, c, 0:CAP], ph[:, c % 2, 0:CAP], ACT.Gelu,
                                               bias=bT[:, bass.ds(B1C + e * FC + c, 1)]).then_inc(s_g2, 1)
                        act.wait_ge(b_st[k], 16 * (B // 4) + 16 * i + 1)
                        shift_rows(B // 2 + n, k, i)
                for k in range(2):
                    act.wait_ge(b_st[k], 16 * (B // 2) + 1)

            @block.tensor
            def _(pe):
                pe.sem_inc(b_s, 2 * NS)
                pe.sem_inc(b_t, 1)
                pe.sem_inc(s_y, 2)
                pe.sem_inc(s_y2, 2)
                pe.wait_ge(b_c, 4)
                pe.wait_ge(b_w, 32)

                def scores(n, k, s, i):
                    if isinstance(n, int) or k or s >= 2:
                        pe.wait_ge(b_m, n * NS + s)
                    else:
                        pe.wait_ge(b_m, n * NS + 1)
                    fresh = set()
                    for h, qt, kt, m, at in slot_pieces(s):
                        bank, c0 = 2 * (s % 2) + at // 4, (at % 4) * P
                        pe.matmul(pm[:, bank, c0:c0 + m * P], qm[0:QROWS, k, h, qt * P:(qt + 1) * P],
                                  km[0:QROWS, k, h, kt * P:(kt + m) * P],
                                  start=bank not in fresh, stop=False, skip_group_check=True)
                        fresh.add(bank)
                    for h, qt, kt, m, at in slot_pieces(s):
                        bank, c0 = 2 * (s % 2) + at // 4, (at % 4) * P
                        if kt == qt:
                            mm = pe.matmul(pm[:, bank, c0:c0 + P], ident_bf[:, :], hide[:, :],
                                           start=False, stop=True, skip_group_check=True)
                    mm.then_inc(b_s, 1)

                def batch_maxima(n, k, i, between):
                    pe.wait_ge(b_ld[k], 16 * 18 * (i + 1))
                    for s in range(NS):
                        scores(n, k, s, i)
                        for piece in between.get(s, ()):
                            piece()
                    pe.wait_ge(b_sh, n + 2)
                    pe.wait_ge(b_tc, n + 1)
                    pe.transpose(pt2[:, 0, 0:P // 2].bitcast(BF16), shift[:, :, :, :].rearrange("p a h q -> p (a h q)"),
                                 ident_bf[:, :]).then_inc(b_t, 1)

                def fb_first(m, j, i, c):
                    if c == 0:
                        pe.wait_ge(s_xl[j], 16 * i + 16)
                    pe.wait_ge(s_g, FC * m + max(c - 1, 0) + 1)
                    pe.matmul(ph[:, c % 2, :], fw1_s[:, c * P:(c + 1) * P], xT1[:, j, :],
                              start=True, stop=True).then_inc(s_h, 1)

                def fb_second(m, j, tiles):
                    if 0 in tiles:
                        pe.wait_ge(s_g, FC * m + FC + 1)
                        pe.wait_ge(s_yc, m + 1)
                    for t in tiles:
                        for c in range(FC):
                            mm = pe.matmul(py[:, 0, t * P:(t + 1) * P], hT[:, j, c, t * P:(t + 1) * P],
                                           fw2_s[:, c, :], start=(c == 0), stop=(c == FC - 1))
                    if TPB - 1 in tiles:
                        mm.then_inc(s_y, 1)

                def ex_turn(e, j, i):
                    pe.wait_ge(s_we[j], 64 * i + 64)
                    pe.wait_ge(b_tc, B // 2 + i + 1)
                    for s, (s0, n) in enumerate(ST):
                        mm = pe.transpose(pt2[:, 0, s0:s0 + n], xg_s[0:n, j, s, :], ident[0:n, 0:n])
                    mm.then_inc(s_xt, 1)

                def ex_first(e, j, c):
                    if c == 0:
                        pe.wait_ge(s_xtc, e + 1)
                    pe.wait_ge(s_g2, FC * e + max(c - 1, 0) + 1)
                    pe.matmul(ph[:, c % 2, 0:CAP], w1_s[:, j, c * P:(c + 1) * P], xgT[:, j, :],
                              start=True, stop=True).then_inc(s_h2, 1)

                def ex_second(e, j, s):
                    if s == 0:
                        pe.wait_ge(s_g2, FC * e + FC + 1)
                        pe.wait_ge(s_y2c, e + 1)
                    s0, n = ST[s]
                    for c in range(FC):
                        mm = pe.matmul(py[0:n, 0, s * P:(s + 1) * P], hT[:, j, c, s0:s0 + n],
                                       w2_s[:, j, c, :], start=(c == 0), stop=(c == FC - 1))
                    if s == len(ST) - 1:
                        mm.then_inc(s_y2, 1)

                with pe.Fori(0, B // 4) as i:
                    for k in range(2):
                        n = 2 * i + k
                        between = {}
                        for j in range(2):
                            m, o = 2 * n + j, 10 * j
                            for c in range(FC):
                                between.setdefault(o + c, []).append(lambda m=m, j=j, c=c: fb_first(m, j, n, c))
                            for t in range(TPB):
                                between.setdefault(o + 5 + t // 2, []).append(lambda m=m, j=j, t=t: fb_second(m, j, (t,)))
                        batch_maxima(n, k, i, between)
                pe.wait_ge(s_yc, B + 1)
                with pe.Fori(0, B // 4) as i:
                    for k in range(2):
                        n = 2 * i + k
                        between = {}
                        for j in range(2):
                            e, o = 2 * n + j, 10 * j
                            between.setdefault(o, []).append(lambda e=e, j=j: ex_turn(e, j, n))
                            for c in range(FC):
                                between.setdefault(o + 1 + c, []).append(lambda e=e, j=j, c=c: ex_first(e, j, c))
                            for s in range(len(ST)):
                                between.setdefault(o + 6 + s, []).append(lambda e=e, j=j, s=s: ex_second(e, j, s))
                        batch_maxima(B // 2 + n, k, i + B // 4, between)

        c12.close()
        c2 = ExitStack()
        qT = sb("qT", [P, 2, H, T], BF16, c=c2)
        kT = sb("kT", [P, 2, H, T], BF16, c=c2)
        xT2 = sb("xT2", [P, 2, T], c=c2)
        v_s = sb("v_s", [P, 2, TPB, H, W], c=c2)
        pb = sb("pb", [P, RING, UNIT], c=c2)
        o_raw = sb("o_raw", [P, 2, T], c=c2)
        rd = sb("rd", [P, 2, TPB, G], c=c2)
        oq = sb("oq", [P, 2, TPB, H, D], c=c2)
        oT = sb("oT", [P, T], c=c2)
        g1 = sb("g1", [P, 2, TOPK, TPB, P], c=c2)
        idx_s = sb("idx_s", [P, 2, TOPK, TPB], I32, c=c2)
        acc = sb("acc", [P, 2, TPB, P], c=c2)
        acc2 = sb("acc2", [P, 2, TPB, P], c=c2)
        res = sb("res", [P, 2, TPB, P], c=c2)
        ps = banks("ps", 4, c2)
        po = banks("po", 2, c2)
        pv = banks("pv", 1, c2)
        px = banks("px", 1, c2)

        a_ld = [sem(f"qkx_loaded{i}") for i in range(2)]
        a_z = sem("buffers_cleared")
        a_v = sem("v_in_psum")
        a_vc = sem("v_ready")
        a_s = sem("scores_in_psum")
        a_e = sem("probs_ready")
        a_m = sem("probs_masked")
        a_pv = sem("pv_done")
        a_oc = sem("o_raw_ready")
        a_t = sem("o_transposed")
        a_rd = sem("recip_ready")
        a_oq = sem("o_normalised")
        a_ot = sem("oT_in_psum")
        a_otc = sem("oT_ready")
        a_op = sem("attn_in_psum")
        a_g = [sem(f"gathered{i}") for i in range(2)]
        a_pc = sem("pool_chain")
        a_acc = sem("rest_summed")
        a_res = sem("result_ready")
        a_ost = sem("results_stored")
        a_out = [sem(f"out_stored{i}") for i in range(2)]

        NU = 5
        NGR = H // G
        UB = NU * NGR

        def pieces(u):
            if u < 2:
                return [(2 * u + a, 3, a * 512, 512) for a in range(2)]
            if u < 4:
                return [x for a in range(2) for x in ((2 * (u - 2) + a, 2, a * 512, 384),
                                                       (2 * (u - 2) + a, 0, a * 512 + 384, 128))]
            return [(a, 1, a * 256, 256) for a in range(4)]

        with c2, nc.Block() as block:

            @block.sync
            def _(sp):
                sp.wait_ge(a_z, 6)
                with sp.Fori(0, B // 2) as i:
                    for k in range(2):
                        n = 2 * i + k
                        sp.wait_ge(a_s, n * UB + UB)
                        sp.sem_inc(s_pass, 1)
                        sp.wait_ge(a_v, n + 1)
                        sp.sem_inc(s_pass, 1)
                        for a in range(NPARTS):
                            for c in range(NPARTS):
                                r = 32 * a + D * c
                                sp.dma_start(qT[r:r + D, k, :, :],
                                             qp_d[a].rearrange("(h d) t -> d h t", d=D)[:, :, bass.ds(n * T, T)]).then_inc(a_ld[k], 16)
                                sp.dma_start(kT[r:r + D, k, :, :],
                                             kp_d[c].rearrange("(h d) t -> d h t", d=D)[:, :, bass.ds(n * T, T)]).then_inc(a_ld[k], 16)
                        sp.dma_start(qT[QROWS:SROWS, k, :, :],
                                     sh_d.rearrange("b (a r) t -> (b a) (r t)", a=2)[bass.ds(2 * n, 2), :].rearrange("a (h t) -> a h t", h=H)).then_inc(a_ld[k], 16)
                        sp.dma_start(xT2[:, k, :], xnT_d[:, bass.ds(n * T, T)]).then_inc(a_ld[k], 16)

            @block.gpsimd
            def _(pool):
                pool.memset(g1[:, :, :, :, :], 0.0).then_inc(a_z, 1)
                pool.sem_inc(a_ost, 2)
                pool.wait_ge(a_z, 6)
                cnt = 8
                with pool.Fori(0, B // 2) as i:
                    for k in range(2):
                        n = 2 * i + k
                        ch = Count(a_pc, i * 2 * cnt + k * cnt)
                        ch.inc(pool.tensor_copy(idx_s[:, k, :, :], idx[:, :, bass.ds(n * TPB, TPB)]))
                        ch.wait(pool)
                        pool.sem_inc(s_pass, 1)
                        for j in range(TPB):
                            for a in range(TOPK):
                                pool.indirect_dma_start(
                                    out=g1[:, k, a, j, :], out_offset=None,
                                    in_=y_d[:, :],
                                    in_offset=bass.IndirectOffsetOnAxis(ap=idx_s[:, k, a, j:j + 1], axis=0),
                                    bounds_check=SLOTS - 1, oob_is_err=False).then_inc(a_g[k], 16)
                        pool.wait_ge(a_g[k], 16 * TOPK * TPB * (i + 1))
                        pool.wait_ge(a_res, n + 1)

                        def wb(a):
                            return wgt[:, a, bass.ds(n * TPB, TPB)].unsqueeze(2).to_broadcast([P, TPB, P])

                        tiles = bass.ds(n * TPB, TPB)
                        ch.inc(pool.tensor_tensor(acc[:, k, :, :], g1[:, k, 0, :, :], wb(0), ALU.mult))
                        ch.inc(pool.tensor_tensor(acc2[:, k, :, :], g1[:, k, 1, :, :], wb(1), ALU.mult))
                        ch.wait(pool)
                        ch.inc(pool.tensor_tensor(acc[:, k, :, :], acc[:, k, :, :], acc2[:, k, :, :], ALU.add))
                        ch.wait(pool)
                        ch.inc(pool.tensor_tensor(acc2[:, k, :, :], yfb_all[:, tiles, :], wb(2), ALU.mult))
                        ch.wait(pool)
                        ch.inc(pool.tensor_tensor(acc[:, k, :, :], acc[:, k, :, :], acc2[:, k, :, :], ALU.add))
                        ch.wait(pool)
                        ch.inc(pool.tensor_tensor(acc[:, k, :, :], acc[:, k, :, :], x_all[:, tiles, :], ALU.add))
                        ch.wait(pool)
                        ch.inc(pool.tensor_tensor(acc[:, k, :, :], acc[:, k, :, :],
                                                  bcast("bo").unsqueeze(1).to_broadcast([P, TPB, P]), ALU.add))
                        assert ch.n == cnt
                        ch.wait(pool)
                        pool.sem_inc(a_acc, 1)
                        pool.wait_ge(a_res, n + 3)
                        pool.dma_start(out_rows[bass.ds(n * T, T), :].rearrange("(j p) c -> p j c", p=P),
                                       res[:, k, :, :]).then_inc(a_out[k], 16)
                        pool.wait_ge(a_out[k], 16 * i + 16)
                        pool.sem_inc(a_ost, 1)

            @block.scalar
            def _(act):
                act.sem_inc(a_e, 1)
                with act.Fori(0, B // 2) as i:
                    for k in range(2):
                        for u in range(UB):
                            n = i * 2 * UB + k * UB + u
                            act.wait_ge(a_s, 2 * UB + n + 1)
                            act.wait_ge(a_pv, n + 1)
                            r = (k * UB + u) % RING
                            s = 2 * (u % 2)
                            act.activation(pb[:, r, :], ps[:, s:s + 2, :].rearrange("p a c -> p (a c)"),
                                           ACT.Exp).then_inc(a_e, 1)

            @block.vector
            def _(dve):
                dve.memset(qT[:, :, :, :], 0.0).then_inc(a_z, 1)
                dve.memset(kT[:, :, :, :], 0.0).then_inc(a_z, 1)
                dve.memset(v_s[:, :, :, :, :], 0.0).then_inc(a_z, 1)
                dve.wait_ge(a_z, 4)
                dve.memset(kT[QROWS:P, :, :, :], 1.0).then_inc(a_z, 1)
                dve.memset(v_s[:, :, :, :, D:D + 1], 1.0).then_inc(a_z, 1)
                dve.sem_inc(a_res, 2)
                dve.sem_inc(a_oq, 1)
                dve.sem_inc(a_otc, 1)
                dve.sem_inc(a_oc, 1)
                dve.wait_ge(a_z, 6)

                def finish_group(gg, k, g):
                    dve.wait_ge(a_pv, RING + (gg + 1) * NU)
                    dve.wait_ge(a_t, gg + 1)
                    dve.tensor_copy(o_raw[:, g % 2, :], po[:, g % 2, :]).then_inc(a_oc, 1)
                    dve.wait_ge(a_t, gg + 3)
                    o4 = px[:, 0, :].rearrange("p (j h w) -> p j h w", h=G, w=W)
                    dve.wait_ge(a_oq, gg + 1)
                    dve.reciprocal(rd[:, g % 2, :, :], o4[:, :, :, D]).then_inc(a_rd, 1)
                    dve.wait_ge(a_rd, gg + 1)
                    for j in range(TPB):
                        ins = dve.tensor_tensor(oq[:, k, j, g * G:(g + 1) * G, :], o4[:, j, :, 0:D],
                                                rd[:, g % 2, j, :].unsqueeze(2).to_broadcast([P, G, D]), ALU.mult)
                    ins.then_inc(a_oq, 1)

                with dve.Fori(0, B // 2) as i:
                    for k in range(2):
                        n = 2 * i + k
                        dve.wait_ge(a_v, n + 3)
                        dve.tensor_tensor(v_s[:, k, :, :, 0:D],
                                          pv[:, 0, :].rearrange("p (j h d) -> p j h d", h=H, d=D),
                                          bcast("bv").rearrange("p (h d) -> p h d", d=D).unsqueeze(1).to_broadcast([P, TPB, H, D]),
                                          ALU.add).then_inc(a_vc, 1)
                        for g in range(NGR):
                            for u in range(NU):
                                un = n * UB + g * NU + u
                                r = (k * UB + g * NU + u) % RING
                                dve.wait_ge(a_e, un + 2)
                                if u < 2:
                                    v = pb[:, r, :].rearrange("p (a c) -> p a c", a=2)[:, :, 384:512]
                                    m = keep_min[:, :].unsqueeze(1).to_broadcast([P, 2, P])
                                elif u < 4:
                                    v = pb[:, r, :].rearrange("p (a b c) -> p a b c", a=2, c=P)[:, :, 2:4, :]
                                    m = keep_min[:, :].unsqueeze(1).unsqueeze(1).to_broadcast([P, 2, 2, P])
                                else:
                                    v = pb[:, r, :].rearrange("p (a c) -> p a c", a=4)[:, :, P:2 * P]
                                    m = keep_min[:, :].unsqueeze(1).to_broadcast([P, 4, P])
                                dve.tensor_tensor(v, v, m, ALU.min).then_inc(a_m, 1)
                                if u == 3 and g > 0:
                                    finish_group(n * NGR + g - 1, k, g - 1)
                        finish_group(n * NGR + NGR - 1, k, NGR - 1)
                        dve.wait_ge(a_ot, n + 1)
                        dve.tensor_copy(oT[:, :], px[:, 0, :]).then_inc(a_otc, 1)
                        dve.wait_ge(a_op, n + 1)
                        dve.wait_ge(a_acc, n + 1)
                        dve.wait_ge(a_ost, n + 1)
                        dve.tensor_tensor(res[:, k, :, :], pv[:, 0, :].rearrange("p (j c) -> p j c", c=P),
                                          acc[:, k, :, :], ALU.add).then_inc(a_res, 1)

            @block.tensor
            def _(pe):
                pe.sem_inc(a_s, 2 * UB)
                pe.sem_inc(a_v, 2)
                pe.sem_inc(a_pv, RING)
                pe.sem_inc(a_t, 2)

                with pe.Fori(0, B // 2) as i:

                    def scores(k, g, u):
                        n = (2 * i + k) * UB + g * NU + u
                        if k * UB + g * NU + u >= 2:
                            pe.wait_ge(a_e, n)
                        else:
                            pe.wait_ge(a_e, i * 2 * UB + 1)
                        s = 2 * ((g * NU + u) % 2)
                        for a, kt, c0, nq in pieces(u):
                            h = g * G + a
                            o = ps[:, s + c0 // 512, c0 % 512:c0 % 512 + nq]
                            mm = pe.matmul(o, kT[0:SROWS, k, h, kt * P:(kt + 1) * P], qT[0:SROWS, k, h, 0:nq],
                                           start=(c0 % 512 == 0), stop=True, skip_group_check=True)
                        mm.then_inc(a_s, 1)

                    def weighted(k, g, us):
                        gg = (2 * i + k) * NGR + g
                        if us[0] == 0:
                            pe.wait_ge(a_vc, 2 * i + k + 1)
                            if k * NGR + g >= 2:
                                pe.wait_ge(a_oc, gg)
                            else:
                                pe.wait_ge(a_oc, i * 2 * NGR + 1)
                        un = (2 * i + k) * UB + g * NU + us[-1]
                        pe.wait_ge(a_m, un + 1)
                        todo = sorted(((kt, a, c0, nq, u) for u in us for a, kt, c0, nq in pieces(u)), reverse=True)
                        todo.sort(key=lambda t: (-t[0], t[1]))
                        for m, (kt, a, c0, nq, u) in enumerate(todo):
                            r = (k * UB + g * NU + u) % RING
                            mm = pe.matmul(po[W * a:W * (a + 1), g % 2, 0:nq], v_s[:, k, kt, g * G + a, :],
                                           pb[:, r, c0:c0 + nq], start=(kt == 3), stop=(kt == 1),
                                           skip_group_check=True)
                            if m >= len(todo) - len(us):
                                mm.then_inc(a_pv, 1)

                    def transposes(k, g):
                        gg = (2 * i + k) * NGR + g
                        pe.wait_ge(a_oc, gg + 2)
                        pe.wait_ge(a_oq, gg + 1)
                        pe.wait_ge(a_otc, 2 * i + k + 1)
                        for j in range(TPB):
                            mm = pe.transpose(px[:, 0, j * P:(j + 1) * P], o_raw[:, g % 2, j * P:(j + 1) * P], ident[:, :])
                        mm.then_inc(a_t, 1)

                    def project(k):
                        n = 2 * i + k
                        pe.wait_ge(a_oq, NGR * n + NGR + 1)
                        for j in range(TPB):
                            mm = pe.transpose(px[:, 0, j * P:(j + 1) * P],
                                              oq[:, k, j, :, :].rearrange("p h d -> p (h d)"), ident[:, :])
                        mm.then_inc(a_ot, 1)
                        pe.wait_ge(a_otc, n + 2)
                        for j in range(TPB):
                            mm = pe.matmul(pv[:, 0, j * P:(j + 1) * P], oT[:, j * P:(j + 1) * P], wT[:, 3, :],
                                           start=True, stop=True)
                        mm.then_inc(a_op, 1)

                    for k in range(2):
                        pe.wait_ge(a_ld[k], 16 * 20 * (i + 1))
                        pe.wait_ge(a_res, 2 * i + k + 2)
                        for j in range(TPB):
                            mm = pe.matmul(pv[:, 0, j * P:(j + 1) * P], xT2[:, k, j * P:(j + 1) * P], wT[:, 2, :],
                                           start=True, stop=True)
                        mm.then_inc(a_v, 1)
                        for g in range(NGR):
                            for u in range(NU):
                                scores(k, g, u)
                                if u == 3:
                                    weighted(k, g, (0, 1))
                                if u == 0 and g > 0:
                                    weighted(k, g - 1, (2, 3))
                                if u == 1 and g > 0:
                                    weighted(k, g - 1, (4,))
                                if u == 4 and g > 0:
                                    transposes(k, g - 1)
                        weighted(k, NGR - 1, (2, 3))
                        weighted(k, NGR - 1, (4,))
                        transposes(k, NGR - 1)
                        project(k)


_INS = ['L0_attn_x', 'L0_attn_Wq', 'L0_attn_bq', 'L0_attn_Wk', 'L0_attn_bk', 'L0_attn_Wv', 'L0_attn_bv',
        'L0_attn_Wo', 'L0_attn_bo', 'L0_attn_attn_scale', 'L0_ffn_Wr', 'L0_ffn_W1', 'L0_ffn_b1', 'L0_ffn_W2',
        'L0_ffn_b2', 'L0_ffn_fw1', 'L0_ffn_fb1', 'L0_ffn_fw2', 'L0_ffn_fb2']
_OUTS = [((B, T, P), 'float32')]


def kernel(**inputs):
    import numpy as _np
    import concourse.bacc as _bacc
    from concourse import mybir as _mybir
    from concourse.bass_utils import run_bass_kernel_spmd as _run

    nc = _bacc.Bacc("TRN2", target_bir_lowering=False, num_devices=1)
    arrays, args = {}, []
    for name in _INS:
        a = _np.ascontiguousarray(inputs[name])
        arrays[f"in_{name}_dram"] = a
        args.append(nc.dram_tensor(f"in_{name}_dram", a.shape, _mybir.dt.from_np(a.dtype), kind="ExternalInput").ap())
    for i, (shape, dtype) in enumerate(_OUTS):
        dt = _mybir.dt.from_np(_np.dtype(dtype))
        args.append(nc.dram_tensor(f"out_{i}_dram", shape, dt, kind="ExternalOutput").ap())
    moe_attention_kernel(nc, *args)
    r = _run(nc, [arrays], core_ids=[0])
    return r.results[0]["out_0_dram"]
```

```python
from contextlib import ExitStack

import concourse.bass as bass
from concourse import mybir

ALU = mybir.AluOpType
ACT = mybir.ActivationFunctionType
AX = mybir.AxisListType
F32 = mybir.dt.float32
BF16 = mybir.dt.bfloat16
I32 = mybir.dt.int32

P = 128
B, T = 8, 512
TOK = B * T
TPB = T // P
NT = TOK // P
H, D = 16, 8
G = 4
W = 32
CHUNK = 64
F = 512
FC = F // P
E, TOPK = 8, 2
CAP = max(int(1.25 * (1024 * TOPK / E)), 4)
SLOTS = E * CAP
ST = [(0, P), (P, P), (2 * P, CAP - 2 * P)]
NPARTS = 3
QROWS = 3 * 32
EPS = 1e-5
FAR = 1.0e6
HUGE = 3.0e38
MASKED = -1.0e30
SROWS = QROWS + 2
SLOT = 1024
UNIT = 1024
RING = 10


class Count:

    def __init__(self, sem, base=0):
        self.sem, self.base, self.n = sem, base, 0

    def inc(self, ins):
        self.n += 1
        ins.then_inc(self.sem, 1)
        return ins

    def wait(self, eng):
        eng.wait_ge(self.sem, self.base + self.n)


def moe_attention_kernel(nc, x, Wq, bq, Wk, bk, Wv, bv, Wo, bo, attn_scale,
                         Wr, W1, b1, W2, b2, fw1, fb1, fw2, fb2, out):
    qp_d = nc.dram_tensor("qp_d", (NPARTS, P, TOK), BF16, kind="Internal").ap()
    kp_d = nc.dram_tensor("kp_d", (NPARTS, P, TOK), BF16, kind="Internal").ap()
    xnT_d = nc.dram_tensor("xnT_d", (P, TOK), F32, kind="Internal").ap()
    xg_d = nc.dram_tensor("xg_d", (SLOTS, P), F32, kind="Internal").ap()
    sh_d = nc.dram_tensor("sh_d", (B + 2, P, P), BF16, kind="Internal").ap()
    y_d = nc.dram_tensor("y_d", (SLOTS, P), F32, kind="Internal").ap()

    x_rows = x.rearrange("b t c -> (b t) c")
    out_rows = out.rearrange("b t c -> (b t) c")

    ctx = ExitStack()
    with ctx:
        def sb(name, shape, dt=F32, c=ctx):
            return c.enter_context(nc.sbuf_tensor(name, shape, dt))

        def banks(name, n, c, dt=F32):
            return c.enter_context(nc.psum_tensor(name, [P, n, 512], dt))

        def sem(name):
            return ctx.enter_context(nc.semaphore(name))

        s_pass = sem("waits_passed")

        x_all = sb("x_all", [P, NT, P])
        yfb_all = sb("yfb_all", [P, NT, P])
        wT = sb("wT", [P, 4, P])
        ident = sb("ident", [P, P])
        keep_min = sb("keep_min", [P, P])
        BC = [("b2", E * P), ("fb2", P), ("bv", P), ("bo", P), ("scale", 1)]
        bc_at, w0 = {}, 0
        for name, n in BC:
            bc_at[name] = w0
            w0 += n
        NBC = w0
        bc = sb("bc", [P, NBC])
        NBR = E * FC + FC + 2
        bT = sb("bT", [P, NBR])
        idx = sb("idx", [P, TOPK, NT], I32)
        wgt = sb("wgt", [P, TOPK + 1, NT])

        qT = sb("qT", [P, 2, H, T], BF16)
        kT = sb("kT", [P, 2, H, T], BF16)
        v_s = sb("v_s", [P, 2, TPB, H, W])
        g1 = sb("g1", [P, 2, TOPK, TPB, P])

        xT2 = sb("xT2", [P, 2, T])

        c12 = ctx.enter_context(ExitStack())
        xn_all = sb("xn_all", [P, NT, P], c=c12)
        xT1 = sb("xT1", [P, 2, T], c=c12)
        fw1_s = sb("fw1_s", [P, F], c=c12)
        fw2_s = sb("fw2_s", [P, FC, P], c=c12)
        hide = sb("hide", [P, P], BF16, c=c12)
        ident_bf = sb("ident_bf", [P, P], BF16, c=c12)
        c1 = ExitStack()
        hfb = sb("hfb", [P, FC, T], c=c1)
        xn_s = sb("xn_s", [P, 2, TPB, P], c=c1)
        xnT = sb("xnT", [P, 2, T], c=c1)
        wr_s = sb("wr_s", [P, E], c=c1)
        brows = sb("brows", [NBR, P], c=c1)
        bcrow = hfb[0:1, :, :].rearrange("p c t -> p (c t)")[:, 0:NBC]
        ones_row = sb("ones_row", [1, P], c=c1)
        ones_bf = sb("ones_bf", [P, P], BF16, c=c1)
        after_bf = sb("after_bf", [P, P], BF16, c=c1)
        stats = sb("stats", [P, NT, 6], c=c1)
        mv = sb("mv", [P, NT, 2], c=c1)
        vare = sb("vare", [P, NT], c=c1)
        rstd = sb("rstd", [P, NT], c=c1)
        mhalf = sb("mhalf", [P, NT], c=c1)
        qs = sb("qs", [P, 2, T], c=c1)
        rem = sb("rem", [P, 2, T], c=c1)
        wn = rem[:, 0, :].rearrange("p (w c) -> p w c", w=4)
        parts = sb("parts", [P, 2, 2, NPARTS, T], BF16, c=c1)
        logits = sb("logits", [P, NT, E], c=c1)
        pr = sb("pr", [P, NT, E], c=c1)
        tmp = sb("tmp", [P, NT, E], c=c1)
        tmp2 = sb("tmp2", [P, NT, E], c=c1)
        m1 = sb("m1", [P, NT, E], c=c1)
        m2 = sb("m2", [P, NT, E], c=c1)
        assign = sb("assign", [P, NT, E], c=c1)
        slotk = sb("slotk", [P, NT, E], c=c1)
        w8 = sb("w8", [P, E], c=c1)
        rsm = sb("rsm", [P, 8, NT], c=c1)
        elig = sb("elig", [P, 2, NT], BF16, c=c1)
        escan = sb("escan", [P, 2, NT], BF16, c=c1)
        ones_nt = sb("ones_nt", [P, NT], c=c1)
        ovf = sb("ovf", [P, NT], c=c1)
        pt = banks("pt", 1, c1)
        pq = banks("pq", 2, c1)
        pl = banks("pl", 1, c1)
        ph = banks("ph", 2, c1)
        pw = banks("pw", 1, c1)
        py = banks("py", 1, c1)

        s_x = [sem(f"x_loaded{i}") for i in range(4)]
        s_wn = sem("wn_loaded")
        s_wl = sem("weights_loaded")
        s_rows = sem("rows_loaded")
        s_const = sem("consts_ready")
        s_c0 = sem("const_chain")
        s_c1 = sem("mask_chain")
        s_clr = sem("buffers_cleared")
        s_clq = sem("spare_rows_filled")
        b_w = sem("b_weights_loaded")
        b_c = sem("b_consts")
        b_ld = [sem(f"b_qk_loaded{i}") for i in range(2)]
        a_ld = [sem(f"qkx_loaded{i}") for i in range(2)]
        s_zero = sem("zero_ready")
        s_xgz = sem("xg_zeroed")
        s_wt = sem("wt_in_psum")
        s_wtc = sem("wt_copied")
        s_dv = sem("dve_chain")
        s_bs = sem("x_statistics")
        s_rs = sem("rstd_ready")
        s_xn = sem("xn_ready")
        s_xnc = sem("xn_kept")
        s_tr = sem("xnT_in_psum")
        s_xnT = sem("xnT_ready")
        s_qk = sem("qk_in_psum")
        s_qs = sem("qs_ready")
        s_p1 = sem("part1_ready")
        s_r1 = sem("rem_ready")
        s_p2 = sem("part2_ready")
        s_p3 = sem("part3_ready")
        s_xst = [sem(f"xnT_stored{i}") for i in range(2)]
        s_xl = [sem(f"xnT_loaded{i}") for i in range(2)]
        s_st = [sem(f"parts_stored{i}") for i in range(2)]
        s_lg = sem("logits_in_psum")
        s_lc = sem("logits_copied")
        s_h = sem("h_in_psum")
        s_g = sem("gelu_done")
        s_y = sem("yfb_in_psum")
        s_yc = sem("yfb_copied")
        s_z = sem("shifted_logits")
        s_e = sem("exp_logits")
        s_el = sem("eligible_ready")
        s_rk = sem("rank_in_psum")
        s_ix = sem("slots_ready")
        s_sc = sem("rows_scattered")
        s_we = [sem(f"expert_loaded{i}") for i in range(2)]
        s_xt = sem("xgT_in_psum")
        s_xtc = sem("xgT_ready")
        s_h2 = sem("expert_h_in_psum")
        s_g2 = sem("expert_gelu_done")
        s_y2 = sem("expert_y_in_psum")
        s_y2c = sem("expert_y_ready")
        s_yst = sem("expert_y_stores_done")
        s_ys = [sem(f"expert_y_stored{i}") for i in range(2)]

        def bcast(name, n=P):
            return bc[:, bc_at[name]:bc_at[name] + n]

        def load_qk(sp, nb, slot, sem):
            for a in range(NPARTS):
                for c in range(NPARTS):
                    r = 32 * a + D * c
                    sp.dma_start(qT[r:r + D, slot, :, :],
                                 qp_d[a].rearrange("(h d) t -> d h t", d=D)[:, :, bass.ds(nb * T, T)]).then_inc(sem, 16)
                    sp.dma_start(kT[r:r + D, slot, :, :],
                                 kp_d[c].rearrange("(h d) t -> d h t", d=D)[:, :, bass.ds(nb * T, T)]).then_inc(sem, 16)

        def load_shifts(sp, n, k):
            sp.dma_start(qT[QROWS:SROWS, k, :, :],
                         sh_d.rearrange("b (a r) t -> (b a) (r t)", a=2)[bass.ds(2 * n, 2), :].rearrange("a (h t) -> a h t", h=H)).then_inc(a_ld[k], 16)

        def rank_bank(e):
            return (pl if e % 2 else pw)[:, 0, 0:NT]

        B1C, FB1C, BQC, BKC = 0, E * FC, E * FC + FC, E * FC + FC + 1
        NG1 = 4

        with c1, nc.Block() as block:

            @block.sync
            def _(sp):
                sp.sem_inc(s_st[0], 1)
                sp.sem_inc(s_st[1], 1)
                sp.sem_inc(s_xst[0], 1)
                sp.sem_inc(s_xst[1], 1)
                for c in range(4):
                    t0 = c * NT // 4
                    sp.dma_start(x_all[:, t0:t0 + NT // 4, :],
                                 x_rows[t0 * P:(t0 + NT // 4) * P, :].rearrange("(n p) c -> p n c", p=P)).then_inc(s_x[c], 16)
                    if c == 0:
                        for n, w in enumerate((Wq, Wk, Wv, Wo)):
                            sp.dma_start(wn[:, n, :], w).then_inc(s_wn, 16)
                        sp.dma_start(brows[0:E * FC, :], b1.rearrange("e (c p) -> (e c) p", p=P)).then_inc(s_rows, 16)
                        sp.dma_start(brows[FB1C:FB1C + FC, :], fb1.rearrange("(c p) -> c p", p=P)).then_inc(s_rows, 16)
                        sp.dma_start(brows[BQC:BQC + 1, :], bq.rearrange("(a p) -> a p", a=1)).then_inc(s_rows, 16)
                        sp.dma_start(brows[BKC:BKC + 1, :], bk.rearrange("(a p) -> a p", a=1)).then_inc(s_rows, 16)
                        sp.dma_start(bcrow[:, 0:E * P], b2.rearrange("(a e) p -> a (e p)", a=1)).then_inc(s_rows, 16)
                        for name, v in (("fb2", fb2), ("bv", bv), ("bo", bo), ("scale", attn_scale)):
                            n = v.shape[0]
                            sp.dma_start(bcrow[:, bc_at[name]:bc_at[name] + n],
                                         v.rearrange("(a p) -> a p", a=1)).then_inc(s_rows, 16)
                        sp.dma_start(wr_s[:, :], Wr).then_inc(s_wl, 16)
                    if c == 1:
                        sp.dma_start(fw1_s[:, :], fw1).then_inc(b_w, 16)
                        sp.dma_start(fw2_s[:, :, :], fw2.rearrange("(c p) n -> p c n", p=P)).then_inc(b_w, 16)
                sp.wait_ge(s_zero, 1)
                for half in range(2):
                    sp.dma_start(xg_d.rearrange("(a p n) c -> a p (n c)", a=2, p=P)[half],
                                 g1[:, :, :, :, :].rearrange("p k a j c -> p (k a j c)")[:, 0:SLOTS // 2]).then_inc(s_xgz, 16)

                zeros = v_s[0:D, :, :, :, :].rearrange("p k j h w -> p (k j h w)").bitcast(BF16).rearrange("p (h t) -> p h t", t=T)
                sp.wait_ge(s_clr, 1)
                for buf in (qT, kT):
                    for a in range(NPARTS):
                        r = 32 * a + 3 * D
                        for k in range(2):
                            sp.dma_start(buf[r:r + D, k, :, :], zeros).then_inc(s_clq, 16)
                sp.wait_ge(s_const, 6)
                for k in range(2):
                    sp.dma_start(kT[QROWS:SROWS, k, :, :].rearrange("p h (a t) -> p (h a) t", t=P),
                                 ones_bf[0:2, :].unsqueeze(1).to_broadcast([2, H * T // P, P])).then_inc(s_clq, 16)

                with sp.Fori(0, B // 2) as i:
                    for k in range(2):
                        n = 2 * i + k
                        sp.wait_ge(s_xnT, n + 1)
                        sp.sem_inc(s_pass, 1)
                        sp.dma_start(xnT_d[:, bass.ds(n * T, T)], xnT[:, k, :]).then_inc(s_xst[k], 16)
                        sp.wait_ge(s_p3, 2 * n + 2)
                        sp.wait_ge(s_p2, 2 * n + 2)
                        sp.wait_ge(s_p1, 2 * n + 2)
                        sp.sem_inc(s_pass, 1)
                        for m, d in enumerate((qp_d, kp_d)):
                            sp.dma_start(d.rearrange("j p t -> p j t")[:, :, bass.ds(n * T, T)],
                                         parts[:, k, m, :, :]).then_inc(s_st[k], 16)
                for k in range(2):
                    sp.wait_ge(s_st[k], 32 * (B // 2) + 1)
                    sp.wait_ge(s_xst[k], 16 * (B // 2) + 1)
                for j in range(2):
                    sp.dma_start(xT1[:, j, :], xnT_d[:, 2 * j * T:(2 * j + 1) * T]).then_inc(s_xl[j], 16)
                sp.wait_ge(s_clq, 16 * (2 * NPARTS * 2 + 2))
                for slot in range(2):
                    load_qk(sp, B - 2 + slot, slot, b_ld[slot])
                for k in range(2):
                    sp.dma_start(xT2[:, k, :], xnT_d[:, k * T:(k + 1) * T]).then_inc(a_ld[k], 16)
                sp.wait_ge(s_xgz, 32)

            @block.gpsimd
            def _(pool):
                ch = Count(s_c0)
                pool.sem_inc(s_xnc, 1)
                ch.inc(pool.memset(ident[:, :], 0.0))
                ch.inc(pool.memset(after_bf[:, :], 0.0))
                ch.inc(pool.memset(keep_min[:, :], HUGE))
                pool.memset(g1[:, :, :, :, :], 0.0).then_inc(s_zero, 1)
                pool.memset(ones_row[:, :], 1.0).then_inc(s_const, 1)
                pool.memset(ones_bf[:, :], 1.0).then_inc(s_const, 1)
                pool.memset(ones_nt[:, :], 1.0).then_inc(s_const, 1)
                ch.wait(pool)
                pool.affine_select(out=ident[:, :], in_=ident[:, :], compare_op=ALU.not_equal, fill=1.0,
                                   base=0, pattern=[[-1, P]], channel_multiplier=1).then_inc(s_const, 1)
                pool.affine_select(out=after_bf[:, :], in_=after_bf[:, :], compare_op=ALU.is_ge, fill=-1.0,
                                   base=0, pattern=[[1, P]], channel_multiplier=-1).then_inc(s_const, 1)
                for lo, base, step, channel, fill in ((CHUNK, -CHUNK, 0, 1, 0.0), (CHUNK, CHUNK, 1, -1, 0.0),
                                                      (0, 0, 1, -1, 0.0), (0, CHUNK - 1, 0, -1, HUGE)):
                    half = keep_min[:, lo:lo + CHUNK]
                    ch.inc(pool.affine_select(out=half, in_=half, compare_op=ALU.is_ge, fill=fill, base=base,
                                              pattern=[[step, CHUNK]], channel_multiplier=channel))
                    ch.wait(pool)
                for e in range(E):
                    ins = pool.memset(w8[:, e:e + 1], float(E - e))
                ins.then_inc(s_const, 1)
                ch.inc(pool.memset(mhalf[:, :], -0.5))
                ch.wait(pool)
                pool.memset(v_s[:, :, :, :, :], 0.0).then_inc(s_clr, 1)
                for c in range(4):
                    pool.wait_ge(s_bs, 3 * c + 3)
                    tiles = slice(c * NT // 4, (c + 1) * NT // 4)
                    pool.tensor_tensor(rstd[:, tiles], vare[:, tiles], mhalf[:, tiles], ALU.pow).then_inc(s_rs, 1)
                with pool.Fori(0, B // 2) as i:
                    for k in range(2):
                        n = 2 * i + k
                        pool.wait_ge(s_xn, n + 1)
                        pool.tensor_copy(xn_all[:, bass.ds(n * TPB, TPB), :], xn_s[:, k, :, :]).then_inc(s_xnc, 1)
                ch = Count(s_c1)
                ch.inc(pool.memset(hide[:, :], 0.0))
                ch.inc(pool.memset(ident_bf[:, :], 0.0))
                ch.wait(pool)
                pool.affine_select(out=ident_bf[:, :], in_=ident_bf[:, :], compare_op=ALU.not_equal, fill=1.0,
                                   base=0, pattern=[[-1, P]], channel_multiplier=1).then_inc(b_c, 1)
                for lo, base, step, channel, fill in ((0, 0, -1, 1, MASKED), (0, CHUNK - 1, 0, -1, MASKED),
                                                      (CHUNK, -CHUNK, -1, 1, MASKED), (CHUNK, -CHUNK, 0, 1, 0.0)):
                    chunk = hide[:, lo:lo + CHUNK]
                    ch.inc(pool.affine_select(out=chunk, in_=chunk, compare_op=ALU.is_ge, fill=fill, base=base,
                                              pattern=[[step, CHUNK]], channel_multiplier=channel))
                    ch.wait(pool)
                pool.sem_inc(b_c, 1)
                pool.wait_ge(s_clq, 16 * (2 * NPARTS * 2 + 2))
                pool.memset(v_s[:, :, :, :, D:D + 1], 1.0).then_inc(s_clr, 1)
                pool.wait_ge(s_clr, 2)
                pool.wait_ge(s_xnc, B + 1)

            @block.vector
            def _(dve):
                dve.sem_inc(s_qs, 1)
                dve.sem_inc(s_lc, 1)
                dve.sem_inc(s_yc, 1)

                def layer_norm(n, k, ch):
                    if not isinstance(n, int) or n >= 2:
                        dve.wait_ge(s_tr, n)
                        dve.wait_ge(s_xnc, n)
                    for j in range(TPB):
                        ins = dve.tensor_scalar(xn_s[:, k, j, :],
                                                x_all[:, n * TPB + j, :] if isinstance(n, int)
                                                else x_all[:, bass.ds(n * TPB + j, 1), :].rearrange("p a c -> p (a c)"),
                                                mv[:, n * TPB + j, 0:1] if isinstance(n, int) else mv[:, bass.ds(n * TPB + j, 1), 0],
                                                rstd[:, n * TPB + j:n * TPB + j + 1] if isinstance(n, int)
                                                else rstd[:, bass.ds(n * TPB + j, 1)], ALU.subtract, ALU.mult)
                        ch.inc(ins)
                    ch.wait(dve)
                    dve.sem_inc(s_xn, 1)

                def statistics(c):
                    tiles = range(c * NT // 4, (c + 1) * NT // 4)
                    dve.wait_ge(s_x[c], 16)
                    for t in tiles:
                        ins = dve.bn_stats(stats[:, t, :], x_all[:, t, :])
                    ins.then_inc(s_bs, 1)
                    dve.wait_ge(s_bs, 3 * c + 1)
                    for t in tiles:
                        ins = dve.bn_aggr(mv[:, t, :], stats[:, t, :])
                    ins.then_inc(s_bs, 1)
                    dve.wait_ge(s_bs, 3 * c + 2)
                    dve.tensor_scalar(vare[:, tiles[0]:tiles[-1] + 1], mv[:, tiles[0]:tiles[-1] + 1, 1], EPS, None,
                                      ALU.add).then_inc(s_bs, 1)

                def batch(i, k, ch, last=False):
                    n = 2 * i + k
                    for m, col in ((0, BQC), (1, BKC)):
                        dve.wait_ge(s_qk, 2 * n + m + 1)
                        if m == 0:
                            dve.tensor_scalar(qs[:, m, :], pq[:, m, :], bT[:, col:col + 1], bcast("scale", 1),
                                              ALU.add, ALU.mult).then_inc(s_qs, 1)
                        else:
                            dve.tensor_scalar(qs[:, m, :], pq[:, m, :], bT[:, col:col + 1], None,
                                              ALU.add).then_inc(s_qs, 1)
                    if not last:
                        layer_norm(n + 1, (k + 1) % 2, ch)
                    for m in range(2):
                        dve.wait_ge(s_p1, 2 * n + m + 1)
                        dve.tensor_tensor(rem[:, m, :], qs[:, m, :], parts[:, k % 2, m, 0, :], ALU.subtract).then_inc(s_r1, 1)
                    dve.wait_ge(s_lg, n + 1)
                    dve.tensor_copy(logits[:, bass.ds(n * TPB, TPB), :],
                                    pl[:, 0, 0:TPB * E].rearrange("p (j e) -> p j e", e=E)).then_inc(s_lc, 1)
                    for m in range(2):
                        dve.wait_ge(s_p2, 2 * n + m + 1)
                        dve.tensor_tensor(parts[:, k % 2, m, 2, :], rem[:, m, :], parts[:, k % 2, m, 1, :],
                                          ALU.subtract).then_inc(s_p3, 1)
                    if k == 2:
                        fallback_out(i)

                def fallback_out(f):
                    dve.wait_ge(s_y, f + 1)
                    dve.tensor_tensor(yfb_all[:, bass.ds((2 * f + 1) * TPB, TPB), :],
                                      py[:, 0, :].rearrange("p (j c) -> p j c", c=P),
                                      bcast("fb2").unsqueeze(1).to_broadcast([P, TPB, P]), ALU.add).then_inc(s_yc, 1)

                PER = 2 * TPB
                ch = Count(s_dv)
                statistics(0)
                dve.wait_ge(s_rs, 1)
                layer_norm(0, 0, ch)
                assert ch.n == PER // 2
                for c in range(1, 4):
                    statistics(c)
                dve.wait_ge(s_rs, 4)
                dve.wait_ge(s_wtc, NG1 + 2)
                batch(0, 0, Count(s_dv, PER // 2))
                with dve.Fori(0, B // 2 - 1) as i:
                    cl = Count(s_dv, PER + i * PER)
                    batch(i, 1, cl)
                    batch(i, 2, cl)
                    assert cl.n == PER
                batch(B // 2 - 1, 1, None, last=True)
                ch = Count(s_dv, PER * (B // 2))
                dve.wait_ge(s_lc, B + 1)
                dve.wait_ge(s_const, 6)

                def bc8(a):
                    return a.unsqueeze(2).to_broadcast([P, NT, E])

                mx, sm, p1, p2, fb, fbn, t1, t2 = (rsm[:, j, :] for j in range(8))
                w8b = w8[:, :].unsqueeze(1).to_broadcast([P, NT, E])

                def step(ins):
                    ch.inc(ins)
                    ch.wait(dve)

                ch.inc(dve.memset(fb, 0.0))
                step(dve.tensor_reduce(mx, logits[:, :, :], AX.X, ALU.max))
                dve.tensor_tensor(tmp[:, :, :], logits[:, :, :], bc8(mx), ALU.subtract).then_inc(s_z, 1)
                fallback_out(B // 2 - 1)
                dve.wait_ge(s_e, 1)
                step(dve.tensor_reduce(sm, pr[:, :, :], AX.X, ALU.add))
                step(dve.reciprocal(sm, sm))
                step(dve.tensor_tensor(pr[:, :, :], pr[:, :, :], bc8(sm), ALU.mult))
                for m, p, mask in ((0, p1, m1), (1, p2, m2)):
                    step(dve.tensor_reduce(p, pr[:, :, :], AX.X, ALU.max))
                    step(dve.tensor_tensor(tmp[:, :, :], pr[:, :, :], bc8(p), ALU.is_equal))
                    step(dve.tensor_tensor(tmp[:, :, :], tmp[:, :, :], w8b, ALU.mult))
                    step(dve.tensor_reduce(t1, tmp[:, :, :], AX.X, ALU.max))
                    step(dve.tensor_tensor(mask[:, :, :], tmp[:, :, :], bc8(t1), ALU.is_equal))
                    if m == 0:
                        step(dve.scalar_tensor_tensor(out=pr[:, :, :], in0=mask[:, :, :], scalar=-2.0,
                                                      in1=pr[:, :, :], op0=ALU.mult, op1=ALU.add))
                step(dve.tensor_tensor(assign[:, :, :], m1[:, :, :], m2[:, :, :], ALU.add))
                step(dve.tensor_tensor(t1, p1, p2, ALU.add))
                step(dve.tensor_scalar(t1, t1, 1e-9, None, ALU.max))
                step(dve.reciprocal(t1, t1))
                ch.inc(dve.tensor_tensor(p1, p1, t1, ALU.mult))
                ch.inc(dve.tensor_tensor(p2, p2, t1, ALU.mult))
                def slots_of(e):
                    ch.inc(dve.tensor_scalar(slotk[:, :, e], rank_bank(e), float(e * CAP - 1), None, ALU.add))

                for e in range(E):
                    a = e % 2
                    step(dve.scalar_tensor_tensor(out=elig[:, a, :], in0=fb, scalar=0.0, in1=assign[:, :, e],
                                                  op0=ALU.is_equal, op1=ALU.mult))
                    dve.tensor_tensor_scan(escan[:, a, :], ones_nt[:, :], elig[:, a, :], 0.0,
                                           ALU.mult, ALU.add).then_inc(s_el, 1)
                    if e > 0:
                        slots_of(e - 1)
                    dve.wait_ge(s_rk, e + 1)
                    step(dve.scalar_tensor_tensor(out=ovf[:, :], in0=rank_bank(e), scalar=float(CAP),
                                                  in1=elig[:, a, :], op0=ALU.is_gt, op1=ALU.mult))
                    step(dve.tensor_tensor(fb, fb, ovf[:, :], ALU.max))
                slots_of(E - 1)
                ch.inc(dve.tensor_scalar(fbn, fb, -1.0, 1.0, ALU.mult, ALU.add))
                step(dve.tensor_copy(wgt[:, 2, :], fb))
                both = ((0, p1, m1, tmp, t1), (1, p2, m2, tmp2, t2))
                for m, p, mask, prod, t in both:
                    ch.inc(dve.tensor_tensor(prod[:, :, :], slotk[:, :, :], mask[:, :, :], ALU.mult))
                ch.wait(dve)
                for m, p, mask, prod, t in both:
                    ch.inc(dve.tensor_reduce(t, prod[:, :, :], AX.X, ALU.add))
                    ch.inc(dve.tensor_tensor(wgt[:, m, :], p, fbn, ALU.mult))
                ch.wait(dve)
                for m, p, mask, prod, t in both:
                    ch.inc(dve.tensor_tensor(t, t, fbn, ALU.mult))
                ch.wait(dve)
                for m, p, mask, prod, t in both:
                    ch.inc(dve.scalar_tensor_tensor(out=t, in0=fb, scalar=FAR, in1=t, op0=ALU.mult, op1=ALU.add))
                ch.wait(dve)
                for m, p, mask, prod, t in both:
                    ch.inc(dve.tensor_copy(idx[:, m, :], t))
                ch.wait(dve)
                dve.sem_inc(s_ix, 1)

            @block.scalar
            def _(act):
                act.wait_ge(s_wt, 1)
                act.activation(wT[:, :, :], pq[:, 0, :].rearrange("p (w c) -> p w c", c=P), ACT.Copy).then_inc(s_wtc, 1)
                act.wait_ge(s_wt, 2)
                act.activation(bT[:, :], pl[:, 0, 0:NBR], ACT.Copy).then_inc(s_wtc, 1)
                for c, bank in enumerate((pq[:, 1, :], ph[:, 0, :], ph[:, 1, :])):
                    act.wait_ge(s_wt, 3 + c)
                    n = min(512, NBC - c * 512)
                    act.activation(bc[:, c * 512:c * 512 + n], bank[:, 0:n], ACT.Copy).then_inc(s_wtc, 1)
                act.sem_inc(s_g, 1)
                act.wait_ge(s_wtc, 5)
                act.sem_inc(s_wtc, 1)

                def copy_xnT(i, k):
                    act.wait_ge(s_tr, 2 * i + k + 2)
                    act.wait_ge(s_xst[k % 2], 16 * (i + k // 2) + 1)
                    act.activation(xnT[:, k % 2, :], pt[:, 0, :], ACT.Copy).then_inc(s_xnT, 1)

                def gelus(i, k, chunks):
                    for c in chunks if k == 1 else ():
                        act.wait_ge(s_h, FC * i + c + 1)
                        act.activation(hfb[:, c, :], ph[:, c % 2, :], ACT.Gelu,
                                       bias=bT[:, FB1C + c:FB1C + c + 1]).then_inc(s_g, 1)

                def batch(i, k, last=False):
                    n = 2 * i + k
                    act.wait_ge(s_st[k % 2], 32 * (i + k // 2) + 1)
                    for m in range(2):
                        act.wait_ge(s_qs, 2 * n + m + 2)
                        act.activation(parts[:, k % 2, m, 0, :], qs[:, m, :], ACT.Copy).then_inc(s_p1, 1)
                    gelus(i, k, (0, 1))
                    if not last:
                        copy_xnT(i, k + 1)
                    for m in range(2):
                        act.wait_ge(s_r1, 2 * n + m + 1)
                        act.activation(parts[:, k % 2, m, 1, :], rem[:, m, :], ACT.Copy).then_inc(s_p2, 1)
                    gelus(i, k, (2, 3))

                copy_xnT(0, 0)
                batch(0, 0)
                with act.Fori(0, B // 2 - 1) as i:
                    for k in (1, 2):
                        batch(i, k)
                batch(B // 2 - 1, 1, last=True)
                act.wait_ge(s_z, 1)
                act.activation(pr[:, :, :], tmp[:, :, :], ACT.Exp).then_inc(s_e, 1)

            @block.tensor
            def _(pe):
                pe.sem_inc(s_tr, 1)
                pe.wait_ge(s_const, 6)
                pe.wait_ge(s_wn, 64)
                for w in range(4):
                    mm = pe.transpose(pq[:, 0, w * P:(w + 1) * P], wn[:, w, :], ident[:, :])
                mm.then_inc(s_wt, 1)
                pe.wait_ge(s_rows, 16 * 9)
                pe.transpose(pl[:, 0, 0:NBR], brows[:, :], ident[0:NBR, 0:NBR]).then_inc(s_wt, 1)
                for c, bank in enumerate((pq[:, 1, :], ph[:, 0, :], ph[:, 1, :])):
                    n = min(512, NBC - c * 512)
                    pe.matmul(bank[:, 0:n], ones_row[:, :], bcrow[:, c * 512:c * 512 + n],
                              start=True, stop=True).then_inc(s_wt, 1)
                pe.wait_ge(s_wl, 16)
                pe.wait_ge(s_wtc, NG1 + 2)
                pe.wait_ge(b_w, 32)

                def fb_first(f, chunks):
                    for c in chunks:
                        if c >= 2:
                            pe.wait_ge(s_g, FC * f + c)
                        pe.matmul(ph[:, c % 2, :], fw1_s[:, c * P:(c + 1) * P], xnT[:, 1, :],
                                  start=True, stop=True).then_inc(s_h, 1)

                def fb_second(f, tiles):
                    if 0 in tiles:
                        pe.wait_ge(s_g, FC * f + FC + 1)
                        pe.wait_ge(s_yc, f + 1)
                    for t in tiles:
                        for c in range(FC):
                            mm = pe.matmul(py[:, 0, t * P:(t + 1) * P], hfb[:, c, t * P:(t + 1) * P],
                                           fw2_s[:, c, :], start=(c == 0), stop=(c == FC - 1))
                    if TPB - 1 in tiles:
                        mm.then_inc(s_y, 1)

                def transpose_xn(n, k):
                    pe.wait_ge(s_xn, n + 1)
                    for j in range(TPB):
                        mm = pe.transpose(pt[:, 0, j * P:(j + 1) * P], xn_s[:, k % 2, j, :], ident[:, :])
                    mm.then_inc(s_tr, 1)

                def batch(i, k, last=False):
                    n = 2 * i + k
                    pe.wait_ge(s_xnT, n + 1)
                    pe.wait_ge(s_qs, 2 * n + 1)
                    for m in range(2):
                        pe.matmul(pq[:, m, :], wT[:, m, :], xnT[:, k % 2, :], start=True, stop=True).then_inc(s_qk, 1)
                    pe.wait_ge(s_lc, n + 1)
                    for j in range(TPB):
                        mm = pe.matmul(pl[:, 0, j * E:(j + 1) * E], xnT[:, k % 2, j * P:(j + 1) * P], wr_s[:, :],
                                       start=True, stop=True)
                    mm.then_inc(s_lg, 1)
                    if k == 1:
                        fb_first(i, (0, 1))
                    elif k == 2:
                        fb_second(i, (0, 1))
                    if not last:
                        transpose_xn(n + 1, k + 1)
                    if k == 1:
                        fb_first(i, (2, 3))
                    elif k == 2:
                        fb_second(i, (2, 3))

                transpose_xn(0, 0)
                batch(0, 0)
                with pe.Fori(0, B // 2 - 1) as i:
                    for k in (1, 2):
                        batch(i, k)
                batch(B // 2 - 1, 1, last=True)
                fb_second(B // 2 - 1, range(TPB))
                for e in range(E):
                    a = e % 2
                    pe.wait_ge(s_el, e + 1)
                    pe.matmul(rank_bank(e), ones_bf[:, :], escan[:, a, :], start=True, stop=False)
                    pe.matmul(rank_bank(e), after_bf[:, :], elig[:, a, :], start=False, stop=True).then_inc(s_rk, 1)

        NS = H * 10 // 8
        HS = NS // 4
        TS = 17
        EX0 = (0, 10)
        FB1 = (1, 3, 5, 7)
        FB2 = 9

        def slot_bank(s):
            return 4 if s % 2 else 2 * (s // 2 % 2)

        cm = ExitStack()
        hT = sb("hT", [P, 2, FC, CAP], c=cm)
        hf = hT[:, :, :, :].rearrange("p j c t -> p (j c t)")[:, 0:FC * T].rearrange("p (c t) -> p c t", c=FC)
        w1_s = sb("w1_s", [P, 2, F], c=cm)
        w2_s = sb("w2_s", [P, 2, FC, P], c=cm)
        xg_s = sb("xg_s", [P, 2, 3, P], c=cm)
        xgT = sb("xgT", [P, 2, CAP], c=cm)
        y_s = sb("y_s", [P, 2, 3, P], c=cm)
        blkmax = sb("blkmax", [P, 2, H * 10], c=cm)
        cp = sb("cp", [P, 2, 8, P], BF16, c=cm)
        half = sb("half", [P, 2, HS, 8, P // 2], BF16, c=cm)
        quarter = sb("quarter", [P, HS, 8, P // 4], BF16, c=cm)
        eighth = sb("eighth", [P, HS, 8, P // 8], BF16, c=cm)
        negm = sb("negm", [P, H, TPB], c=cm)
        shift = sb("shift", [P, 2, H, TPB], BF16, c=cm)
        shT = sb("shT", [P, 2, P], BF16, c=cm)
        pm = banks("pm", 6, cm)
        ph = banks("ph2", 2, cm)
        py = ph[:, 0:1, :]
        p_turn = ph[:, 1, 0:CAP]
        p_shift = ph[:, 1, 0:P // 2].bitcast(BF16)

        b_i = sem("b_first_maxima_ready")
        b_s = sem("b_scores_in_psum")
        b_m = sem("b_block_maxima")
        b_cp = sem("b_odd_slot_copied")
        b_h = sem("b_odd_slot_halved")
        b_q = sem("b_odd_maxima_steps")
        b_n = sem("b_negated_maxima")
        b_hi = sem("b_shift_high")
        b_sh = sem("b_shift_ready")
        b_t = sem("b_shift_in_psum")
        b_tc = sem("b_shiftT_ready")
        b_st = [sem(f"b_shift_stored{i}") for i in range(2)]

        def slot_pieces(s):
            out, at = [], 0
            for h in range(H):
                for qt in range(TPB):
                    done, n = 0, TPB - qt
                    while done < n:
                        g = at // 8
                        m = min(n - done, 4 - at % 4)
                        if g == s:
                            out.append((h, qt, qt + done, m, at % 8))
                        at += m
                        done += m
            return out

        with cm, nc.Block() as block:

            @block.sync
            def _(sp):
                def next_qk(p, k):
                    sp.wait_ge(b_s, p * NS + NS)
                    sp.sem_inc(s_pass, 1)
                    load_qk(sp, B - 2 - p + 2 * k, k, b_ld[k])

                HB = B // 4
                with sp.Fori(1, HB) as i:
                    for k in range(2):
                        next_qk(2 * i + k, k)
                        sp.wait_ge(s_y, B // 2 - 1 + 2 * i + k)
                        sp.sem_inc(s_pass, 1)
                        sp.dma_start(xT1[:, k, :], xnT_d[:, bass.ds((4 * i + 2 * k) * T, T)]).then_inc(s_xl[k], 16)
                sp.wait_ge(s_sc, 16 * TOPK * NT)
                with sp.Fori(0, HB) as i:
                    for k in range(2):
                        next_qk(B // 2 + 2 * i + k, k)
                        for j in range(2):
                            e = 2 * (2 * i + k) + j
                            sp.wait_ge(s_y2, e + 1)
                            sp.sem_inc(s_pass, 1)
                            sp.dma_start(w1_s[:, j, :], W1.rearrange("e d f -> (e d) f")[bass.ds(e * P, P), :]).then_inc(s_we[j], 16)
                            sp.dma_start(w2_s[:, j, :, :],
                                         W2.rearrange("e f d -> (e f) d")[bass.ds(e * F, F), :].rearrange("(c p) n -> p c n", p=P)).then_inc(s_we[j], 16)
                            sp.dma_start(xg_s[:, j, 0:2, :],
                                         xg_d[bass.ds(e * CAP, 2 * P), :].rearrange("(s p) c -> p s c", p=P)).then_inc(s_we[j], 16)
                            sp.dma_start(xg_s[0:CAP - 2 * P, j, 2, :],
                                         xg_d[bass.ds(e * CAP + 2 * P, CAP - 2 * P), :]).then_inc(s_we[j], 16)
                sp.wait_ge(b_st[1], 16 * (B // 2) + 1)
                load_shifts(sp, 0, 0)

            @block.gpsimd
            def _(pool):
                pool.sem_inc(s_yst, 2)
                pool.memset(cp[:, 1, :, :], 0.0).then_inc(b_i, 1)
                pool.memset(half[:, 1, 0:HS - 1, :, :].bitcast(F32), 0.0).then_inc(b_i, 1)
                pool.memset(blkmax[:, 1, :], 0.0).then_inc(b_i, 1)
                for t in range(NT):
                    for a in range(TOPK):
                        pool.indirect_dma_start(
                            out=xg_d[:, :], out_offset=bass.IndirectOffsetOnAxis(ap=idx[:, a, t:t + 1], axis=0),
                            in_=xn_all[:, t, :], in_offset=None,
                            bounds_check=SLOTS - 1, oob_is_err=False).then_inc(s_sc, 16)
                with pool.Fori(0, E // 2) as i:
                    for k in range(2):
                        e = 2 * i + k
                        pool.wait_ge(s_y2c, e + 2)
                        pool.dma_start(y_d[bass.ds(e * CAP, 2 * P), :].rearrange("(s p) c -> p s c", p=P),
                                       y_s[:, k, 0:2, :]).then_inc(s_ys[k], 16)
                        pool.dma_start(y_d[bass.ds(e * CAP + 2 * P, CAP - 2 * P), :],
                                       y_s[0:CAP - 2 * P, k, 2, :]).then_inc(s_ys[k], 16)
                        pool.wait_ge(s_ys[k], 32 * i + 32)
                        pool.sem_inc(s_yst, 1)

            @block.vector
            def _(dve):
                dve.sem_inc(b_m, 2)
                dve.sem_inc(b_q, 1)
                dve.sem_inc(b_h, 1)
                dve.sem_inc(b_sh, 1)
                dve.sem_inc(s_y2c, 1)

                def odd_maxima(n, k, h, step):
                    dve.wait_ge(b_q, 3 * (2 * n + h) + step + 4)
                    if step == 0:
                        dve.wait_ge(b_h, 2 * HS * n + HS * (h + 1) + 2)
                        dve.tensor_tensor(quarter[:, :, :, :], half[:, h, :, :, 0:P // 4], half[:, h, :, :, P // 4:],
                                          ALU.max).then_inc(b_q, 1)
                    elif step == 1:
                        dve.tensor_tensor(eighth[:, :, :, :], quarter[:, :, :, 0:P // 8], quarter[:, :, :, P // 8:],
                                          ALU.max).then_inc(b_q, 1)
                    else:
                        odd = blkmax[:, k, :].rearrange("p (t o b) -> p t o b", o=2, b=8)[:, HS * h:HS * (h + 1), 1, :]
                        dve.tensor_reduce(odd, eighth[:, :, :, :], AX.X, ALU.max).then_inc(b_q, 1)

                def halve(n, j):
                    dve.wait_ge(b_cp, 2 * HS * n + j + 2)
                    dve.tensor_tensor(half[:, j // HS, j % HS, :, :], cp[:, j % 2, :, 0:P // 2],
                                      cp[:, j % 2, :, P // 2:], ALU.max).then_inc(b_h, 1)

                def row_maxima(n, k):
                    dve.wait_ge(b_q, 6 * n + 4)
                    dve.wait_ge(b_m, n * (NS // 2) + 2)
                    dve.wait_ge(b_sh, n + 1)
                    v, at = blkmax[:, 1 - k, :].rearrange("p (h b) -> p h b", h=H), 0
                    for qt in range(TPB):
                        ins = dve.tensor_reduce(negm[:, :, qt], v[:, :, at:at + TPB - qt], AX.X, ALU.max, negate=True)
                        at += TPB - qt
                        ins.then_inc(b_n, 1)

                def shift_parts(n):
                    dve.wait_ge(b_n, TPB * n + TPB)
                    dve.wait_ge(b_t, n + 1)
                    dve.tensor_copy(shift[:, 0, :, :], negm[:, :, :]).then_inc(b_hi, 1)
                    dve.wait_ge(b_hi, n + 1)
                    dve.tensor_tensor(shift[:, 1, :, :], negm[:, :, :], shift[:, 0, :, :], ALU.subtract).then_inc(b_sh, 1)

                def finish(n, k, s):
                    if s == 0:
                        dve.wait_ge(b_i, 3)
                        halve(n - 1, NS // 2 - 1)
                    elif s in (2, 4, 6):
                        odd_maxima(n - 1, 1 - k, 1, s // 2 - 1)
                    elif s == 8:
                        row_maxima(n, k)
                    elif s == 10:
                        shift_parts(n)

                def maxima(n, k, extra):
                    for s in range(NS):
                        if s % 2 == 0:
                            dve.wait_ge(b_s, 2 * NS + n * NS + s + 1)
                            dve.tensor_reduce(blkmax[:, k, s * 8:s * 8 + 8],
                                              pm[:, slot_bank(s):slot_bank(s) + 2, :].rearrange("p a (b c) -> p (a b) c", c=P),
                                              AX.X, ALU.max).then_inc(b_m, 1)
                            if s >= 2:
                                halve(n, s // 2 - 1)
                            finish(n, k, s)
                        if s in (12, 14, 16):
                            odd_maxima(n, k, 0, (s - 12) // 2)
                        if s in extra:
                            extra[s]()

                def expert_out(e, j):
                    dve.wait_ge(s_y2, e + 3)
                    dve.wait_ge(s_yst, e + 1)
                    dve.tensor_tensor(y_s[:, j, 0:2, :], py[:, 0, 0:2 * P].rearrange("p (s c) -> p s c", c=P),
                                      bc[:, bass.ds(e * P, P)].unsqueeze(1).to_broadcast([P, 2, P]), ALU.add)
                    dve.tensor_tensor(y_s[0:CAP - 2 * P, j, 2, :], py[0:CAP - 2 * P, 0, 2 * P:3 * P],
                                      bc[0:CAP - 2 * P, bass.ds(e * P, P)], ALU.add).then_inc(s_y2c, 1)

                def fallback_out(n):
                    dve.wait_ge(s_y, B // 2 + n + 1)
                    dve.tensor_tensor(yfb_all[:, bass.ds(2 * n * TPB, TPB), :],
                                      py[:, 0, :].rearrange("p (j c) -> p j c", c=P),
                                      bcast("fb2").unsqueeze(1).to_broadcast([P, TPB, P]), ALU.add).then_inc(s_yc, 1)

                with dve.Fori(0, B // 4) as i:
                    for k in range(2):
                        n = 2 * i + k
                        maxima(n, k, {18: lambda: fallback_out(n)})
                with dve.Fori(0, B // 4) as i:
                    for k in range(2):
                        n = 2 * i + k
                        maxima(B // 2 + n, k, {9: lambda: expert_out(2 * n, 0),
                                               19: lambda: expert_out(2 * n + 1, 1)})
                for s in range(0, 11, 2):
                    finish(B, 0, s)

            @block.scalar
            def _(act):
                act.sem_inc(b_tc, 1)
                act.sem_inc(b_cp, 1)
                act.sem_inc(s_g2, 1)
                act.sem_inc(b_st[0], 1)
                act.sem_inc(b_st[1], 1)

                def shift_rows(n, k, i):
                    act.wait_ge(b_t, n + 2)
                    act.activation(shT[:, k, :], p_shift, ACT.Copy).then_inc(b_tc, 1)
                    act.wait_ge(b_tc, n + 2)
                    act.dma_start(sh_d.rearrange("b r t -> (b r) t")[bass.ds((B + 1 - n - 2 * k) * P, P), :], shT[:, k, :]).then_inc(b_st[k], 16)

                def copy_odd(n, s):
                    act.wait_ge(b_s, 2 * NS + n * NS + s + 1)
                    act.wait_ge(b_h, 2 * HS * n + s // 2 + 1)
                    act.activation(cp[:, (s // 2) % 2, :, :],
                                   pm[:, 4:6, :].rearrange("p a (b c) -> p (a b) c", c=P), ACT.Copy).then_inc(b_cp, 1)

                def gelu(e, j, c):
                    act.wait_ge(s_h2, FC * e + c + 1)
                    act.activation(hT[:, j, c, :], ph[:, c % 2, 0:CAP], ACT.Gelu,
                                   bias=bT[:, bass.ds(B1C + e * FC + c, 1)]).then_inc(s_g2, 1)

                with act.Fori(0, B // 4) as i:
                    for k in range(2):
                        n = 2 * i + k
                        for s in range(1, NS, 2):
                            copy_odd(n, s)
                            if s in FB1:
                                c = FB1.index(s)
                                act.wait_ge(s_h, FC * (B // 2 + n) + c + 1)
                                act.activation(hf[:, c, :], ph[:, c % 2, :], ACT.Gelu,
                                               bias=bT[:, FB1C + c:FB1C + c + 1]).then_inc(s_g, 1)
                            if s == TS:
                                act.wait_ge(b_st[k], 16 * i + 1)
                                shift_rows(n, k, i)
                with act.Fori(0, B // 4) as i:
                    for k in range(2):
                        n = 2 * i + k
                        for s in range(NS):
                            if s % 2:
                                copy_odd(B // 2 + n, s)
                            for j in range(2):
                                o = s - EX0[j]
                                if o == 0:
                                    act.wait_ge(s_xt, 2 * n + j + 1)
                                    act.activation(xgT[:, j, :], p_turn, ACT.Copy).then_inc(s_xtc, 1)
                                if 1 <= o <= FC:
                                    gelu(2 * n + j, j, o - 1)
                            if s == TS:
                                act.wait_ge(b_st[k], 16 * (B // 4) + 16 * i + 1)
                                shift_rows(B // 2 + n, k, i)
                act.wait_ge(b_st[0], 16 * (B // 2) + 1)
                shift_rows(B, 0, 0)

            @block.tensor
            def _(pe):
                pe.sem_inc(b_s, 2 * NS)
                pe.sem_inc(b_t, 1)
                pe.sem_inc(s_y2, 2)
                pe.wait_ge(b_c, 2)

                def scores(n, k, s):
                    pe.wait_ge(b_cp if s % 2 else b_m, n * (NS // 2) + s // 2 + 1)
                    fresh = set()
                    for h, qt, kt, m, at in slot_pieces(s):
                        bank, c0 = slot_bank(s) + at // 4, (at % 4) * P
                        pe.matmul(pm[:, bank, c0:c0 + m * P], qT[0:QROWS, k, h, qt * P:(qt + 1) * P],
                                  kT[0:QROWS, k, h, kt * P:(kt + m) * P],
                                  start=bank not in fresh, stop=False, skip_group_check=True)
                        fresh.add(bank)
                    for h, qt, kt, m, at in slot_pieces(s):
                        bank, c0 = slot_bank(s) + at // 4, (at % 4) * P
                        if kt == qt:
                            mm = pe.matmul(pm[:, bank, c0:c0 + P], ident_bf[:, :], hide[:, :],
                                           start=False, stop=True, skip_group_check=True)
                    mm.then_inc(b_s, 1)

                def transpose_shifts(n):
                    pe.wait_ge(b_sh, n + 2)
                    pe.wait_ge(b_tc, n + 1)
                    pe.transpose(p_shift, shift[:, :, :, :].rearrange("p a h q -> p (a h q)"),
                                 ident_bf[:, :]).then_inc(b_t, 1)

                def batch_maxima(n, k, i, between):
                    pe.wait_ge(b_ld[k], 16 * 18 * (i + 1))
                    for s in range(NS):
                        scores(n, k, s)
                        for piece in between.get(s, ()):
                            piece()
                        if s == TS:
                            transpose_shifts(n)

                def fb_first(n, k, i, c):
                    if c == 0:
                        pe.wait_ge(s_xl[k], 16 * i + 16)
                        pe.wait_ge(s_yc, B // 2 + n + 1)
                    elif c == 1:
                        pe.wait_ge(b_tc, n + 1)
                    else:
                        pe.wait_ge(s_g, FC * (B // 2 + n) + c)
                    pe.matmul(ph[:, c % 2, :], fw1_s[:, c * P:(c + 1) * P], xT1[:, k, :],
                              start=True, stop=True).then_inc(s_h, 1)

                def fb_second(n, t, h):
                    if t == 0:
                        pe.wait_ge(s_g, FC * (B // 2 + n) + FC + h)
                    for c in range(FC // 2 * h, FC // 2 * (h + 1)):
                        mm = pe.matmul(py[:, 0, t * P:(t + 1) * P], hf[:, c, t * P:(t + 1) * P],
                                       fw2_s[:, c, :], start=(c == 0), stop=(c == FC - 1))
                    if t == TPB - 1 and h == 1:
                        mm.then_inc(s_y, 1)

                def ex_turn(e, j, n):
                    pe.wait_ge(s_we[j], 64 * n + 64)
                    pe.wait_ge(s_g2, FC * e + 1)
                    pe.wait_ge(b_tc, B // 2 + n + 1)
                    for s, (s0, rows) in enumerate(ST):
                        mm = pe.transpose(p_turn[:, s0:s0 + rows], xg_s[0:rows, j, s, :], ident[0:rows, 0:rows])
                    mm.then_inc(s_xt, 1)

                def ex_first(e, j, c):
                    if c == 0:
                        pe.wait_ge(s_xtc, e + 1)
                        pe.wait_ge(s_y2c, e + 1)
                    elif c >= 2:
                        pe.wait_ge(s_g2, FC * e + c)
                    pe.matmul(ph[:, c % 2, 0:CAP], w1_s[:, j, c * P:(c + 1) * P], xgT[:, j, :],
                              start=True, stop=True).then_inc(s_h2, 1)

                def ex_second(e, j, s, h):
                    if s == 0:
                        pe.wait_ge(s_g2, FC * e + FC + h)
                    s0, n = ST[s]
                    for c in range(FC // 2 * h, FC // 2 * (h + 1)):
                        mm = pe.matmul(py[0:n, 0, s * P:(s + 1) * P], hT[:, j, c, s0:s0 + n],
                                       w2_s[:, j, c, :], start=(c == 0), stop=(c == FC - 1))
                    if s == len(ST) - 1 and h == 1:
                        mm.then_inc(s_y2, 1)

                with pe.Fori(0, B // 4) as i:
                    for k in range(2):
                        n = 2 * i + k
                        between = {}
                        for c in range(FC):
                            between[FB1[c]] = [lambda n=n, k=k, i=i, c=c: fb_first(n, k, i, c)]
                        for t in range(TPB):
                            for h in range(2):
                                between.setdefault(FB2 + 2 * t + h, []).append(lambda n=n, t=t, h=h: fb_second(n, t, h))
                        batch_maxima(n, k, i, between)
                pe.wait_ge(s_yc, B + 1)
                with pe.Fori(0, B // 4) as i:
                    for k in range(2):
                        n = 2 * i + k
                        between = {}
                        for j in range(2):
                            e, o = 2 * n + j, EX0[j]
                            between.setdefault(o, []).append(lambda e=e, j=j: ex_turn(e, j, n))
                            for c in range(FC):
                                between.setdefault(o + 1 + c, []).append(lambda e=e, j=j, c=c: ex_first(e, j, c))
                            for s in range(len(ST)):
                                for h in range(2):
                                    at = min(o + 5 + 2 * s + h, o + 9)
                                    between.setdefault(at, []).append(lambda e=e, j=j, s=s, h=h: ex_second(e, j, s, h))
                        between.setdefault(TS, []).append(lambda: pe.wait_ge(s_g2, FC * (2 * n + 2) + 1))
                        batch_maxima(B // 2 + n, k, i + B // 4, between)
                transpose_shifts(B)

        c12.close()
        c2 = ExitStack()
        pb = sb("pb", [P, RING, UNIT], c=c2)
        o_raw = sb("o_raw", [P, 2, T], c=c2)
        rd = sb("rd", [P, 2, TPB, G], c=c2)
        oq = sb("oq", [P, 2, TPB, H, D], c=c2)
        oT = sb("oT", [P, T], c=c2)
        idx_s = sb("idx_s", [P, 2, TOPK, TPB], I32, c=c2)
        acc = sb("acc", [P, 2, TPB, P], c=c2)
        acc2 = sb("acc2", [P, 2, TPB, P], c=c2)
        res = sb("res", [P, 2, TPB, P], c=c2)
        ps = banks("ps", 4, c2)
        po = banks("po", 2, c2)
        pv = banks("pv", 1, c2)
        px = banks("px", 1, c2)

        a_v = sem("v_in_psum")
        a_vc = sem("v_ready")
        a_s = sem("scores_in_psum")
        a_e = sem("probs_ready")
        a_m = sem("probs_masked")
        a_pv = sem("pv_done")
        a_oc = sem("o_raw_ready")
        a_t = sem("o_transposed")
        a_rd = sem("recip_ready")
        a_oq = sem("o_normalised")
        a_ot = sem("oT_in_psum")
        a_otc = sem("oT_ready")
        a_op = sem("attn_in_psum")
        a_g = [sem(f"gathered{i}") for i in range(2)]
        a_pc = sem("pool_chain")
        a_acc = sem("rest_summed")
        a_res = sem("result_ready")
        a_ost = sem("results_stored")
        a_out = [sem(f"out_stored{i}") for i in range(2)]

        NU = 5
        NGR = H // G
        UB = NU * NGR

        PRE = [(0, g) for g in range(NGR)]
        BODY = [(k, g) for k in (1, 2) for g in range(NGR)]
        LAST = [(1, g) for g in range(NGR)]

        def ring(at):
            k, g, u = at
            return (k * UB + g * NU + u) % RING

        def pieces(u):
            if u < 2:
                return [(2 * u + a, 3, a * 512, 512) for a in range(2)]
            if u < 4:
                return [x for a in range(2) for x in ((2 * (u - 2) + a, 2, a * 512, 384),
                                                       (2 * (u - 2) + a, 0, a * 512 + 384, 128))]
            return [(a, 1, a * 256, 256) for a in range(4)]

        with c2, nc.Block() as block:

            @block.sync
            def _(sp):
                sp.wait_ge(b_st[0], 16 * (B // 2) + 17)
                load_shifts(sp, 1, 1)
                with sp.Fori(1, B // 2) as i:
                    for k in range(2):
                        n = 2 * i + k
                        sp.wait_ge(a_s, n * UB + UB)
                        sp.sem_inc(s_pass, 1)
                        sp.wait_ge(a_v, n + 1)
                        sp.sem_inc(s_pass, 1)
                        load_qk(sp, n, k, a_ld[k])
                        load_shifts(sp, n, k)
                        sp.dma_start(xT2[:, k, :], xnT_d[:, bass.ds(n * T, T)]).then_inc(a_ld[k], 16)

            @block.gpsimd
            def _(pool):
                pool.sem_inc(a_ost, 2)
                STEPS = 8

                def rest(i, k):
                    n, slot = 2 * i + k, k % 2
                    tiles = bass.ds(n * TPB, TPB)
                    ch = Count(a_pc, n * STEPS)

                    def step(ins):
                        ch.inc(ins)
                        ch.wait(pool)

                    def wb(a):
                        return wgt[:, a, tiles].unsqueeze(2).to_broadcast([P, TPB, P])

                    step(pool.tensor_copy(idx_s[:, slot, :, :], idx[:, :, tiles]))
                    pool.sem_inc(s_pass, 1)
                    for j in range(TPB):
                        for a in range(TOPK):
                            pool.indirect_dma_start(
                                out=g1[:, slot, a, j, :], out_offset=None,
                                in_=y_d[:, :],
                                in_offset=bass.IndirectOffsetOnAxis(ap=idx_s[:, slot, a, j:j + 1], axis=0),
                                bounds_check=SLOTS - 1, oob_is_err=False).then_inc(a_g[slot], 16)
                    pool.wait_ge(a_res, n + 1)
                    step(pool.tensor_tensor(acc[:, slot, :, :], yfb_all[:, tiles, :], wb(2), ALU.mult))
                    step(pool.tensor_tensor(acc[:, slot, :, :], acc[:, slot, :, :], x_all[:, tiles, :], ALU.add))
                    step(pool.tensor_tensor(acc[:, slot, :, :], acc[:, slot, :, :],
                                            bcast("bo").unsqueeze(1).to_broadcast([P, TPB, P]), ALU.add))
                    pool.wait_ge(a_g[slot], 16 * TOPK * TPB * (i + k // 2 + 1))
                    for a in range(TOPK):
                        step(pool.tensor_tensor(acc2[:, slot, :, :], g1[:, slot, a, :, :], wb(a), ALU.mult))
                        step(pool.tensor_tensor(acc[:, slot, :, :], acc[:, slot, :, :], acc2[:, slot, :, :], ALU.add))
                    assert ch.n == STEPS
                    pool.sem_inc(a_acc, 1)

                def store(i, k):
                    n = 2 * i + k
                    pool.wait_ge(a_res, n + 3)
                    pool.dma_start(out_rows[bass.ds(n * T, T), :].rearrange("(j p) c -> p j c", p=P),
                                   res[:, k, :, :]).then_inc(a_out[k], 16)
                    pool.wait_ge(a_out[k], 16 * i + 16)
                    pool.sem_inc(a_ost, 1)

                rest(0, 0)
                with pool.Fori(0, B // 2 - 1) as i:
                    for k in range(2):
                        rest(i, k + 1)
                        store(i, k)
                rest(B // 2 - 1, 1)
                for k in range(2):
                    store(B // 2 - 1, k)

            @block.scalar
            def _(act):
                act.sem_inc(a_e, 2)
                with act.Fori(0, B // 2) as i:
                    for k in range(2):
                        for u in range(UB):
                            n = i * 2 * UB + k * UB + u
                            act.wait_ge(a_s, 2 * UB + n + 1)
                            act.wait_ge(a_pv, n + 1)
                            r = (k * UB + u) % RING
                            s = 2 * (u % 2)
                            act.activation(pb[:, r, :], ps[:, s:s + 2, :].rearrange("p a c -> p (a c)"),
                                           ACT.Exp).then_inc(a_e, 1)

            @block.vector
            def _(dve):
                dve.sem_inc(a_res, 2)
                dve.sem_inc(a_oq, 1)
                dve.sem_inc(a_otc, 1)
                dve.sem_inc(a_oc, 2)

                def new_v(n, k):
                    dve.wait_ge(a_v, n + 3)
                    dve.tensor_tensor(v_s[:, k % 2, :, :, 0:D],
                                      pv[:, 0, :].rearrange("p (j h d) -> p j h d", h=H, d=D),
                                      bcast("bv").rearrange("p (h d) -> p h d", d=D).unsqueeze(1).to_broadcast([P, TPB, H, D]),
                                      ALU.add).then_inc(a_vc, 1)

                def hide_masked(un, u):
                    dve.wait_ge(a_e, un + 3)
                    r = ring(u)
                    if u[2] < 2:
                        v = pb[:, r, :].rearrange("p (a c) -> p a c", a=2)[:, :, 384:512]
                        m = keep_min[:, :].unsqueeze(1).to_broadcast([P, 2, P])
                    elif u[2] < 4:
                        v = pb[:, r, :].rearrange("p (a b c) -> p a b c", a=2, c=P)[:, :, 2:4, :]
                        m = keep_min[:, :].unsqueeze(1).unsqueeze(1).to_broadcast([P, 2, 2, P])
                    else:
                        v = pb[:, r, :].rearrange("p (a c) -> p a c", a=4)[:, :, P:2 * P]
                        m = keep_min[:, :].unsqueeze(1).to_broadcast([P, 4, P])
                    dve.tensor_tensor(v, v, m, ALU.min).then_inc(a_m, 1)

                def evacuate(gg, g):
                    dve.wait_ge(a_pv, RING + (gg + 1) * NU)
                    dve.wait_ge(a_t, gg + 1)
                    dve.tensor_copy(o_raw[:, g % 2, :], po[:, g % 2, :]).then_inc(a_oc, 1)

                def normalise(gg, k, g):
                    dve.wait_ge(a_t, gg + 3)
                    o4 = px[:, 0, :].rearrange("p (j h w) -> p j h w", h=G, w=W)
                    dve.wait_ge(a_oq, gg + 1)
                    dve.reciprocal(rd[:, g % 2, :, :], o4[:, :, :, D]).then_inc(a_rd, 1)
                    dve.wait_ge(a_rd, gg + 1)
                    for j in range(TPB):
                        ins = dve.tensor_tensor(oq[:, k % 2, j, g * G:(g + 1) * G, :], o4[:, j, :, 0:D],
                                                rd[:, g % 2, j, :].unsqueeze(2).to_broadcast([P, G, D]), ALU.mult)
                    ins.then_inc(a_oq, 1)

                def copy_oT(n):
                    dve.wait_ge(a_ot, n + 1)
                    dve.tensor_copy(oT[:, :], pv[:, 0, :]).then_inc(a_otc, 1)

                def result(n, k):
                    dve.wait_ge(a_op, n + 1)
                    dve.wait_ge(a_acc, n + 1)
                    dve.wait_ge(a_ost, n + 1)
                    dve.tensor_tensor(res[:, k % 2, :, :], pv[:, 0, :].rearrange("p (j c) -> p j c", c=P),
                                      acc[:, k % 2, :, :], ALU.add).then_inc(a_res, 1)

                def group(i, k, g, behind=NGR):
                    n = 2 * i + k
                    gg = n * NGR + g
                    for u in range(NU):
                        hide_masked(gg * NU + u, (k, g, u))
                        if u == 1 and behind > 1:
                            normalise(gg - 2, k - (g < 2), (g - 2) % NGR)
                        if u == 3 and behind > 0:
                            evacuate(gg - 1, (g - 1) % NGR)
                        if u == 2 and g == 0:
                            new_v(n, k)
                        if u == 3 and g == 2 and k > 0:
                            copy_oT(n - 1)
                        if u == 4 and g == 3 and k > 0:
                            result(n - 1, k - 1)

                for k, g in PRE:
                    group(0, k, g, behind=g)
                with dve.Fori(0, B // 2 - 1) as i:
                    for k, g in BODY:
                        group(i, k, g)
                for k, g in LAST:
                    group(B // 2 - 1, k, g)
                evacuate(B * NGR - 1, NGR - 1)
                for g in (NGR - 2, NGR - 1):
                    normalise((B - 1) * NGR + g, 1, g)
                copy_oT(B - 1)
                result(B - 1, 1)

            @block.tensor
            def _(pe):
                pe.sem_inc(a_s, 2 * UB)
                pe.sem_inc(a_v, 2)
                pe.sem_inc(a_pv, RING)
                pe.sem_inc(a_t, 2)

                def project_v(i, k):
                    pe.wait_ge(a_res, 2 * i + k + 1)
                    for j in range(TPB):
                        mm = pe.matmul(pv[:, 0, j * P:(j + 1) * P], xT2[:, k % 2, j * P:(j + 1) * P], wT[:, 2, :],
                                       start=True, stop=True)
                    mm.then_inc(a_v, 1)

                def scores(i, k, g, u):
                    pe.wait_ge(a_e, (2 * i + k) * UB + g * NU + u + 1)
                    s = 2 * ((g * NU + u) % 2)
                    for a, kt, c0, nq in pieces(u):
                        h = g * G + a
                        o = ps[:, s + c0 // 512, c0 % 512:c0 % 512 + nq]
                        mm = pe.matmul(o, kT[0:SROWS, k % 2, h, kt * P:(kt + 1) * P], qT[0:SROWS, k % 2, h, 0:nq],
                                       start=(c0 % 512 == 0), stop=True, skip_group_check=True)
                    mm.then_inc(a_s, 1)

                def weighted(i, k, g, kt):
                    gg = (2 * i + k) * NGR + g
                    us = {3: (0, 1), 2: (2, 3), 0: (2, 3), 1: (4,)}[kt]
                    if kt == 3:
                        pe.wait_ge(a_vc, 2 * i + k + 1)
                        pe.wait_ge(a_oc, gg + 1)
                    pe.wait_ge(a_m, gg * NU + us[-1] + 1)
                    for u in us:
                        for a, t, c0, nq in pieces(u):
                            if t == kt:
                                mm = pe.matmul(po[W * a:W * (a + 1), g % 2, 0:nq], v_s[:, k % 2, kt, g * G + a, :],
                                               pb[:, ring((k, g, u)), c0:c0 + nq], start=(kt == 3), stop=(kt == 1),
                                               skip_group_check=True)
                        if kt != 2:
                            mm.then_inc(a_pv, 1)

                def transposes(i, k, g):
                    gg = (2 * i + k) * NGR + g
                    pe.wait_ge(a_oc, gg + 3)
                    pe.wait_ge(a_oq, gg + 1)
                    for j in range(TPB):
                        mm = pe.transpose(px[:, 0, j * P:(j + 1) * P], o_raw[:, g % 2, j * P:(j + 1) * P], ident[:, :])
                    mm.then_inc(a_t, 1)

                def transpose_out(i, k):
                    n = 2 * i + k
                    pe.wait_ge(a_oq, NGR * n + NGR + 1)
                    pe.wait_ge(a_vc, min(n + 2, B) if isinstance(n, int) else n + 2)
                    for j in range(TPB):
                        mm = pe.transpose(pv[:, 0, j * P:(j + 1) * P],
                                          oq[:, k % 2, j, :, :].rearrange("p h d -> p (h d)"), ident[:, :])
                    mm.then_inc(a_ot, 1)

                def project_out(i, k):
                    pe.wait_ge(a_otc, 2 * i + k + 2)
                    for j in range(TPB):
                        mm = pe.matmul(pv[:, 0, j * P:(j + 1) * P], oT[:, j * P:(j + 1) * P], wT[:, 3, :],
                                       start=True, stop=True)
                    mm.then_inc(a_op, 1)

                def group(i, k, g, behind=NGR):
                    before = (i, k - (g == 0), (g - 1) % NGR)
                    if g == 0:
                        pe.wait_ge(a_ld[k % 2], 16 * 20 * (i + k // 2) + 32)
                    for u in range(NU):
                        scores(i, k, g, u)
                        if behind > 0 and u != 1:
                            weighted(*before, {0: 3, 2: 2, 3: 0, 4: 1}[u])
                        if behind > 1 and u == 1:
                            transposes(i, k - (g < 2), (g - 2) % NGR)
                        if u == 1 and g == 0:
                            project_v(i, k)
                        if u == 3:
                            if g == 2 and k > 0:
                                transpose_out(i, k - 1)
                            if g == 3 and k > 0:
                                project_out(i, k - 1)

                for k, g in PRE:
                    group(0, k, g, behind=g)
                with pe.Fori(0, B // 2 - 1) as i:
                    for k, g in BODY:
                        group(i, k, g)
                i = B // 2 - 1
                for k, g in LAST:
                    group(i, k, g)
                for kt in (3, 2, 0, 1):
                    weighted(i, 1, NGR - 1, kt)
                for g in (NGR - 2, NGR - 1):
                    transposes(i, 1, g)
                transpose_out(i, 1)
                project_out(i, 1)


_INS = ['L0_attn_x', 'L0_attn_Wq', 'L0_attn_bq', 'L0_attn_Wk', 'L0_attn_bk', 'L0_attn_Wv', 'L0_attn_bv',
        'L0_attn_Wo', 'L0_attn_bo', 'L0_attn_attn_scale', 'L0_ffn_Wr', 'L0_ffn_W1', 'L0_ffn_b1', 'L0_ffn_W2',
        'L0_ffn_b2', 'L0_ffn_fw1', 'L0_ffn_fb1', 'L0_ffn_fw2', 'L0_ffn_fb2']
_OUTS = [((B, T, P), 'float32')]


def kernel(**inputs):
    import numpy as _np
    import concourse.bacc as _bacc
    from concourse import mybir as _mybir
    from concourse.bass_utils import run_bass_kernel_spmd as _run

    nc = _bacc.Bacc("TRN2", target_bir_lowering=False, num_devices=1)
    arrays, args = {}, []
    for name in _INS:
        a = _np.ascontiguousarray(inputs[name])
        arrays[f"in_{name}_dram"] = a
        args.append(nc.dram_tensor(f"in_{name}_dram", a.shape, _mybir.dt.from_np(a.dtype), kind="ExternalInput").ap())
    for i, (shape, dtype) in enumerate(_OUTS):
        dt = _mybir.dt.from_np(_np.dtype(dtype))
        args.append(nc.dram_tensor(f"out_{i}_dram", shape, dt, kind="ExternalOutput").ap())
    moe_attention_kernel(nc, *args)
    r = _run(nc, [arrays], core_ids=[0])
    return r.results[0]["out_0_dram"]
```

```python
from contextlib import ExitStack

import concourse.bass as bass
from concourse import mybir

ALU = mybir.AluOpType
ACT = mybir.ActivationFunctionType
AX = mybir.AxisListType
F32 = mybir.dt.float32
BF16 = mybir.dt.bfloat16
I32 = mybir.dt.int32

P = 128
B, T = 8, 512
TOK = B * T
TPB = T // P
NT = TOK // P
H, D = 16, 8
G = 4
W = 32
CHUNK = 64
F = 512
FC = F // P
E, TOPK = 8, 2
CAP = max(int(1.25 * (1024 * TOPK / E)), 4)
SLOTS = E * CAP
ST = [(0, P), (P, P), (2 * P, CAP - 2 * P)]
NPARTS = 3
QROWS = 3 * 32
EPS = 1e-5
FAR = 1.0e6
HUGE = 3.0e38
MASKED = -1.0e30
SROWS = QROWS + 2
UNIT = 1024
RING = 10


class Count:

    def __init__(self, sem, base=0):
        self.sem, self.base, self.n = sem, base, 0

    def inc(self, ins):
        self.n += 1
        ins.then_inc(self.sem, 1)
        return ins

    def wait(self, eng):
        eng.wait_ge(self.sem, self.base + self.n)


def moe_attention_kernel(nc, x, Wq, bq, Wk, bk, Wv, bv, Wo, bo, attn_scale,
                         Wr, W1, b1, W2, b2, fw1, fb1, fw2, fb2, out):
    qp_d = nc.dram_tensor("qp_d", (B * NPARTS * P, T), BF16, kind="Internal").ap()
    kp_d = nc.dram_tensor("kp_d", (B * NPARTS * P, T), BF16, kind="Internal").ap()
    xnT_d = nc.dram_tensor("xnT_d", (P, TOK), F32, kind="Internal").ap()
    xg_d = nc.dram_tensor("xg_d", (SLOTS, P), F32, kind="Internal").ap()
    sh_d = nc.dram_tensor("sh_d", (B + 2, P, P), BF16, kind="Internal").ap()
    y_d = nc.dram_tensor("y_d", (SLOTS, P), F32, kind="Internal").ap()

    x_rows = x.rearrange("b t c -> (b t) c")
    out_rows = out.rearrange("b t c -> (b t) c")

    ctx = ExitStack()
    with ctx:
        def sb(name, shape, dt=F32, c=ctx):
            return c.enter_context(nc.sbuf_tensor(name, shape, dt))

        def banks(name, n, c, dt=F32):
            return c.enter_context(nc.psum_tensor(name, [P, n, 512], dt))

        def sem(name):
            return ctx.enter_context(nc.semaphore(name))

        s_pass = sem("waits_passed")

        x_all = sb("x_all", [P, NT, P])
        yfb_all = sb("yfb_all", [P, NT, P])
        wT = sb("wT", [P, 4, P])
        ident = sb("ident", [P, P])
        keep_min = sb("keep_min", [P, P])
        BC = [("b2", E * P), ("fb2", P), ("bv", P), ("bo", P)]
        bc_at, w0 = {}, 0
        for name, n in BC:
            bc_at[name] = w0
            w0 += n
        NBC = w0
        bc = sb("bc", [P, NBC])
        scale_s = sb("scale_s", [P, 1])
        NBR = E * FC + FC + 2
        bT = sb("bT", [P, NBR])
        idx = sb("idx", [P, TOPK, NT], I32)
        wgt = sb("wgt", [P, TOPK + 1, NT])

        qT = sb("qT", [P, 2, H, T], BF16)
        kT = sb("kT", [P, 2, H, T], BF16)
        v_s = sb("v_s", [P, 2, TPB, H, W])
        g1 = sb("g1", [P, 2, TOPK, TPB, P])


        xT2 = sb("xT2", [P, 2, T])

        c12 = ctx.enter_context(ExitStack())
        xn_all = sb("xn_all", [P, NT, P], c=c12)
        fw1_s = sb("fw1_s", [P, F], c=c12)
        fw2_s = sb("fw2_s", [P, FC, P], c=c12)
        hide = sb("hide", [P, P], BF16, c=c12)
        ident_bf = sb("ident_bf", [P, P], BF16, c=c12)
        route = sb("route", [P, 3, NT * E], c=c12)
        logits, pr, tmp = (route[:, j, :].rearrange("p (n e) -> p n e", e=E) for j in range(3))
        ones_bf = sb("ones_bf", [P, P], BF16, c=c12)
        after_bf = sb("after_bf", [P, P], BF16, c=c12)
        tmp2 = sb("tmp2", [P, NT, E], c=c12)
        m1 = sb("m1", [P, NT, E], c=c12)
        m2 = sb("m2", [P, NT, E], c=c12)
        assign = sb("assign", [P, NT, E], c=c12)
        slotk = sb("slotk", [P, NT, E], c=c12)
        w8 = sb("w8", [P, E], c=c12)
        rsm = sb("rsm", [P, 8, NT], c=c12)
        elig = sb("elig", [P, 2, NT], BF16, c=c12)
        escan = sb("escan", [P, 2, NT], BF16, c=c12)
        ones_nt = sb("ones_nt", [P, NT], c=c12)
        ovf = sb("ovf", [P, NT], c=c12)
        mx, sm, p1, p2, fb, fbn, t1, t2 = (rsm[:, j, :] for j in range(8))
        c1 = ExitStack()
        hfb = sb("hfb", [P, FC, T], c=c1)
        xn_s = sb("xn_s", [P, 2, TPB, P], c=c1)
        xnT = sb("xnT", [P, 2, T], c=c1)
        wr_s = sb("wr_s", [P, E], c=c1)
        brows = sb("brows", [NBR, P], c=c1)
        stats = sb("stats", [P, NT, 6], c=c1)
        mv = sb("mv", [P, NT, 2], c=c1)
        vare = sb("vare", [P, NT], c=c1)
        rstd = sb("rstd", [P, NT], c=c1)
        mhalf = sb("mhalf", [P, NT], c=c1)
        qs = sb("qs", [P, 2, T], c=c1)
        rem = sb("rem", [P, 2, T], c=c1)
        wn = rem[:, 0, :].rearrange("p (w c) -> p w c", w=4)
        brows_dh = rem[0:NBR, 1, 0:P]
        parts = sb("parts", [P, 2, 2, NPARTS, T], BF16, c=c1)
        pt = banks("pt", 1, c1)
        pq = banks("pq", 2, c1)
        pl = banks("pl", 1, c1)
        ph = banks("ph", 2, c1)
        py = banks("py", 1, c1)

        s_x = [sem(f"x_loaded{i}") for i in range(4)]
        s_wn = sem("wn_loaded")
        s_wl = sem("weights_loaded")
        s_rows = sem("rows_loaded")
        s_scl = sem("scale_loaded")
        s_bcr = sem("broadcast_rows_loaded")
        s_const = sem("consts_ready")
        s_c0 = sem("const_chain")
        s_c1 = sem("mask_chain")
        s_clr = sem("buffers_cleared")
        s_clq = sem("spare_rows_filled")
        b_w = sem("b_weights_loaded")
        b_c = sem("b_consts")
        b_ld = [sem(f"b_qk_loaded{i}") for i in range(2)]
        a_ld = [sem(f"qkx_loaded{i}") for i in range(2)]
        s_zero = sem("zero_ready")
        s_xgz = sem("xg_zeroed")
        s_wt = sem("wt_in_psum")
        s_bp = sem("bias_rows_permuted")
        s_wtc = sem("wt_copied")
        s_dv = sem("dve_chain")
        s_bs = sem("x_statistics")
        s_rs = sem("rstd_ready")
        s_xn = sem("xn_ready")
        s_xnc = sem("xn_kept")
        s_tr = sem("xnT_in_psum")
        s_xnT = sem("xnT_ready")
        s_qk = sem("qk_in_psum")
        s_qs = sem("qs_ready")
        s_p1 = sem("part1_ready")
        s_r1 = sem("rem_ready")
        s_p2 = sem("part2_ready")
        s_p3 = sem("part3_ready")
        s_xst = [sem(f"xnT_stored{i}") for i in range(2)]
        s_xl = [sem(f"xnT_loaded{i}") for i in range(2)]
        s_st = [sem(f"parts_stored{i}") for i in range(2)]
        s_lg = sem("logits_in_psum")
        s_lc = sem("logits_copied")
        s_h = sem("h_in_psum")
        s_g = sem("gelu_done")
        s_y = sem("yfb_in_psum")
        s_yc = sem("yfb_copied")
        s_z = sem("shifted_logits")
        s_e = sem("exp_logits")
        s_el = sem("eligible_ready")
        s_rk = sem("rank_in_psum")
        s_ix = sem("slots_ready")
        s_rc = sem("routing_chain")
        s_rr = sem("ranks_read")
        s_sc = sem("rows_scattered")
        s_we = [sem(f"expert_loaded{i}") for i in range(2)]
        s_xt = sem("xgT_in_psum")
        s_xtc = sem("xgT_ready")
        s_h2 = sem("expert_h_in_psum")
        s_g2 = sem("expert_gelu_done")
        s_y2 = sem("expert_y_in_psum")
        s_y2c = sem("expert_y_ready")
        s_yst = sem("expert_y_stores_done")
        s_ys = [sem(f"expert_y_stored{i}") for i in range(2)]

        def bcast(name, n=P):
            return bc[:, bc_at[name]:bc_at[name] + n]

        def bc8(a):
            return a.unsqueeze(2).to_broadcast([P, NT, E])

        def load_qk(sp, nb, slot, sem):
            for a in range(NPARTS):
                rows = slice(32 * a, 32 * a + NPARTS * D)
                part = qp_d[bass.ds((nb * NPARTS + a) * P, P), :].rearrange("(d h) t -> d (h t)", h=H)
                sp.dma_start(qT[rows, slot, :, :].rearrange("r h t -> r (h t)"),
                             part.unsqueeze(0).to_broadcast([NPARTS, D, H * T])).then_inc(sem, 16)
                sp.dma_start(kT[rows, slot, :, :].rearrange("r h t -> r (h t)"),
                             kp_d[bass.ds(nb * NPARTS * P, NPARTS * P), :].rearrange("(r h) t -> r (h t)", h=H)).then_inc(sem, 16)

        def load_shifts(sp, n, k):
            sp.dma_start(qT[QROWS:SROWS, k, :, :],
                         sh_d.rearrange("b (a r) t -> (b a) (r t)", a=2)[bass.ds(2 * n, 2), :]
                         .rearrange("a (h t) -> a h t", h=H)).then_inc(a_ld[k], 16)

        B1C, FB1C, BQC, BKC = 0, E * FC, E * FC + FC, E * FC + FC + 1

        with c1, nc.Block() as block:

            @block.sync
            def _(sp):
                sp.sem_inc(s_st[0], 1)
                sp.sem_inc(s_st[1], 1)
                sp.sem_inc(s_xst[0], 1)
                sp.sem_inc(s_xst[1], 1)
                for c in range(4):
                    t0 = c * NT // 4
                    sp.dma_start(x_all[:, t0:t0 + NT // 4, :],
                                 x_rows[t0 * P:(t0 + NT // 4) * P, :].rearrange("(n p) c -> p n c", p=P)).then_inc(s_x[c], 16)
                    if c == 0:
                        for n, w in enumerate((Wq, Wk, Wv, Wo)):
                            sp.dma_start(wn[:, n, :], w).then_inc(s_wn, 16)
                        sp.dma_start(brows[0:E * FC, :], b1.rearrange("e (c p) -> (e c) p", p=P)).then_inc(s_rows, 16)
                        sp.dma_start(brows[FB1C:FB1C + FC, :], fb1.rearrange("(c p) -> c p", p=P)).then_inc(s_rows, 16)
                        sp.dma_start(brows[BQC:BQC + 1, :], bq.rearrange("(a p) -> a p", a=1)).then_inc(s_rows, 16)
                        sp.dma_start(brows[BKC:BKC + 1, :], bk.rearrange("(a p) -> a p", a=1)).then_inc(s_rows, 16)
                        sp.dma_start(scale_s[:, :],
                                     attn_scale.rearrange("(a p) -> a p", a=1).to_broadcast([P, 1])).then_inc(s_scl, 16)
                        sp.dma_start(wr_s[:, :], Wr).then_inc(s_wl, 16)
                sp.dma_start(bc[:, 0:E * P],
                             b2.rearrange("(a e) p -> a (e p)", a=1).to_broadcast([P, E * P])).then_inc(s_bcr, 16)
                for name, v in (("fb2", fb2), ("bv", bv), ("bo", bo)):
                    sp.dma_start(bc[:, bc_at[name]:bc_at[name] + P],
                                 v.rearrange("(a p) -> a p", a=1).to_broadcast([P, P])).then_inc(s_bcr, 16)
                sp.dma_start(fw1_s[:, :], fw1).then_inc(b_w, 16)
                sp.dma_start(fw2_s[:, :, :], fw2.rearrange("(c p) n -> p c n", p=P)).then_inc(b_w, 16)
                sp.wait_ge(s_zero, 1)
                for half in range(2):
                    sp.dma_start(xg_d.rearrange("(a p n) c -> a p (n c)", a=2, p=P)[half],
                                 g1[:, :, :, :, :].rearrange("p k a j c -> p (k a j c)")[:, 0:SLOTS // 2]).then_inc(s_xgz, 16)

                zeros = v_s[0:D, :, :, :, :].rearrange("p k j h w -> p (k j h w)").bitcast(BF16).rearrange("p (h t) -> p h t", t=T)
                sp.wait_ge(s_clr, 1)
                for buf in (qT, kT):
                    for a in range(NPARTS):
                        r = 32 * a + 3 * D
                        for k in range(2):
                            sp.dma_start(buf[r:r + D, k, :, :], zeros).then_inc(s_clq, 16)
                sp.wait_ge(s_const, 5)
                for k in range(2):
                    sp.dma_start(kT[QROWS:SROWS, k, :, :].rearrange("p h (a t) -> p (h a) t", t=P),
                                 ones_bf[0:2, :].unsqueeze(1).to_broadcast([2, H * T // P, P])).then_inc(s_clq, 16)

                with sp.Fori(0, B // 2) as i:
                    for k in range(2):
                        n = 2 * i + k
                        sp.wait_ge(s_xnT, n + 1)
                        sp.sem_inc(s_pass, 1)
                        sp.dma_start(xnT_d[:, bass.ds(n * T, T)], xnT[:, k, :]).then_inc(s_xst[k], 16)
                        sp.wait_ge(s_p3, 2 * n + 2)
                        sp.wait_ge(s_p2, 2 * n + 2)
                        sp.wait_ge(s_p1, 2 * n + 2)
                        sp.sem_inc(s_pass, 1)
                        for m, d in enumerate((qp_d, kp_d)):
                            sp.dma_start(d[bass.ds(n * NPARTS * P, NPARTS * P), :].rearrange("(j p) t -> p j t", p=P),
                                         parts[:, k, m, :, :]).then_inc(s_st[k], 16)
                for k in range(2):
                    sp.wait_ge(s_st[k], 32 * (B // 2) + 1)
                    sp.wait_ge(s_xst[k], 16 * (B // 2) + 1)
                for j in range(2):
                    sp.dma_start(xT2[:, j, :], xnT_d[:, 2 * j * T:(2 * j + 1) * T]).then_inc(s_xl[j], 16)
                sp.wait_ge(s_clq, 16 * (2 * NPARTS * 2 + 2))
                load_qk(sp, B - 2, 0, b_ld[0])
                sp.wait_ge(s_xgz, 32)

            @block.gpsimd
            def _(pool):
                ch = Count(s_c0)
                pool.sem_inc(s_xnc, 1)
                ch.inc(pool.memset(ident[:, :], 0.0))
                ch.inc(pool.memset(after_bf[:, :], 0.0))
                ch.inc(pool.memset(keep_min[:, :], HUGE))
                pool.memset(g1[:, :, :, :, :], 0.0).then_inc(s_zero, 1)
                pool.memset(ones_bf[:, :], 1.0).then_inc(s_const, 1)
                pool.memset(ones_nt[:, :], 1.0).then_inc(s_const, 1)
                ch.wait(pool)
                pool.affine_select(out=ident[:, :], in_=ident[:, :], compare_op=ALU.not_equal, fill=1.0,
                                   base=0, pattern=[[-1, P]], channel_multiplier=1).then_inc(s_const, 1)
                pool.affine_select(out=after_bf[:, :], in_=after_bf[:, :], compare_op=ALU.is_ge, fill=-1.0,
                                   base=0, pattern=[[1, P]], channel_multiplier=-1).then_inc(s_const, 1)
                for lo, base, step, channel, fill in ((CHUNK, -CHUNK, 0, 1, 0.0), (CHUNK, CHUNK, 1, -1, 0.0),
                                                      (0, 0, 1, -1, 0.0), (0, CHUNK - 1, 0, -1, HUGE)):
                    chunk = keep_min[:, lo:lo + CHUNK]
                    ch.inc(pool.affine_select(out=chunk, in_=chunk, compare_op=ALU.is_ge, fill=fill, base=base,
                                              pattern=[[step, CHUNK]], channel_multiplier=channel))
                    ch.wait(pool)
                for e in range(E):
                    ins = pool.memset(w8[:, e:e + 1], float(E - e))
                ins.then_inc(s_const, 1)
                ch.inc(pool.memset(mhalf[:, :], -0.5))
                ch.wait(pool)

                def reciprocal_root(c):
                    pool.wait_ge(s_bs, 3 * c + 3)
                    tiles = slice(c * NT // 4, (c + 1) * NT // 4)
                    pool.tensor_tensor(rstd[:, tiles], vare[:, tiles], mhalf[:, tiles], ALU.pow).then_inc(s_rs, 1)

                def keep(i, k):
                    n = 2 * i + k
                    pool.wait_ge(s_xn, n + 1)
                    pool.tensor_copy(xn_all[:, bass.ds(n * TPB, TPB), :], xn_s[:, k, :, :]).then_inc(s_xnc, 1)

                reciprocal_root(0)
                reciprocal_root(1)
                keep(0, 0)
                reciprocal_root(2)
                keep(0, 1)
                reciprocal_root(3)
                with pool.Fori(1, B // 2) as i:
                    for k in range(2):
                        keep(i, k)
                ch = Count(s_c1)
                ch.inc(pool.memset(hide[:, :], 0.0))
                ch.inc(pool.memset(ident_bf[:, :], 0.0))
                ch.wait(pool)
                pool.affine_select(out=ident_bf[:, :], in_=ident_bf[:, :], compare_op=ALU.not_equal, fill=1.0,
                                   base=0, pattern=[[-1, P]], channel_multiplier=1).then_inc(b_c, 1)
                for lo, base, step, channel, fill in ((0, 0, -1, 1, MASKED), (0, CHUNK - 1, 0, -1, MASKED),
                                                      (CHUNK, -CHUNK, -1, 1, MASKED), (CHUNK, -CHUNK, 0, 1, 0.0)):
                    chunk = hide[:, lo:lo + CHUNK]
                    ch.inc(pool.affine_select(out=chunk, in_=chunk, compare_op=ALU.is_ge, fill=fill, base=base,
                                              pattern=[[step, CHUNK]], channel_multiplier=channel))
                    ch.wait(pool)
                pool.sem_inc(b_c, 1)
                pool.wait_ge(s_clq, 16 * (2 * NPARTS * 2 + 2))
                pool.memset(v_s[:, :, :, :, D:D + 1], 1.0).then_inc(s_clr, 1)
                pool.wait_ge(s_clr, 2)
                pool.wait_ge(s_xnc, B + 1)

            @block.vector
            def _(dve):
                dve.sem_inc(s_qs, 1)
                dve.memset(v_s[:, :, :, :, :], 0.0).then_inc(s_clr, 1)
                dve.sem_inc(s_lc, 1)
                dve.sem_inc(s_yc, 1)

                def layer_norm(n, k, ch, first=False):
                    if not first:
                        dve.wait_ge(s_tr, n)
                        dve.wait_ge(s_xnc, n)
                    for j in range(TPB):
                        tile = bass.ds(n * TPB + j, 1)
                        ins = dve.tensor_scalar(xn_s[:, k, j, :], x_all[:, tile, :].rearrange("p a c -> p (a c)"),
                                                mv[:, tile, 0], rstd[:, tile], ALU.subtract, ALU.mult)
                        ch.inc(ins)
                    ch.wait(dve)
                    dve.sem_inc(s_xn, 1)

                def statistics(c):
                    tiles = range(c * NT // 4, (c + 1) * NT // 4)
                    dve.wait_ge(s_x[c], 16)
                    for t in tiles:
                        ins = dve.bn_stats(stats[:, t, :], x_all[:, t, :])
                    ins.then_inc(s_bs, 1)
                    dve.wait_ge(s_bs, 3 * c + 1)
                    for t in tiles:
                        ins = dve.bn_aggr(mv[:, t, :], stats[:, t, :])
                    ins.then_inc(s_bs, 1)
                    dve.wait_ge(s_bs, 3 * c + 2)
                    dve.tensor_scalar(vare[:, tiles[0]:tiles[-1] + 1], mv[:, tiles[0]:tiles[-1] + 1, 1], EPS, None,
                                      ALU.add).then_inc(s_bs, 1)

                def batch(i, k, ch, last=False):
                    n = 2 * i + k
                    for m, col in ((0, BQC), (1, BKC)):
                        dve.wait_ge(s_qk, 2 * n + m + 1)
                        if m == 0:
                            dve.tensor_scalar(qs[:, m, :], pq[:, m, :], bT[:, col:col + 1], scale_s[:, :],
                                              ALU.add, ALU.mult).then_inc(s_qs, 1)
                        else:
                            dve.tensor_scalar(qs[:, m, :], pq[:, m, :], bT[:, col:col + 1], None,
                                              ALU.add).then_inc(s_qs, 1)
                    if k == 1 and not last:
                        dve.wait_ge(s_rs, i + 2)
                    if not last:
                        layer_norm(n + 1, (k + 1) % 2, ch)
                    for m in range(2):
                        dve.wait_ge(s_p1, 2 * n + m + 1)
                        dve.tensor_tensor(rem[:, m, :], qs[:, m, :], parts[:, k % 2, m, 0, :], ALU.subtract).then_inc(s_r1, 1)
                    dve.wait_ge(s_lg, n + 1)
                    dve.tensor_copy(logits[:, bass.ds(n * TPB, TPB), :],
                                    pl[:, 0, 0:TPB * E].rearrange("p (j e) -> p j e", e=E)).then_inc(s_lc, 1)
                    for m in range(2):
                        dve.wait_ge(s_p2, 2 * n + m + 1)
                        dve.tensor_tensor(parts[:, k % 2, m, 2, :], rem[:, m, :], parts[:, k % 2, m, 1, :],
                                          ALU.subtract).then_inc(s_p3, 1)
                    if k == 2:
                        fallback_out(i)

                def fallback_out(f):
                    dve.wait_ge(s_y, f + 1)
                    dve.tensor_tensor(yfb_all[:, bass.ds((2 * f + 1) * TPB, TPB), :],
                                      py[:, 0, :].rearrange("p (j c) -> p j c", c=P),
                                      bcast("fb2").unsqueeze(1).to_broadcast([P, TPB, P]), ALU.add).then_inc(s_yc, 1)

                PER = 2 * TPB
                ch = Count(s_dv)
                statistics(0)
                dve.wait_ge(s_rs, 1)
                layer_norm(0, 0, ch, first=True)
                assert ch.n == PER // 2
                statistics(1)
                statistics(2)
                dve.wait_ge(s_wtc, 2)
                dve.wait_ge(s_scl, 16)
                batch(0, 0, Count(s_dv, PER // 2))
                statistics(3)
                dve.wait_ge(s_bcr, 16 * 4)
                with dve.Fori(0, B // 2 - 1) as i:
                    cl = Count(s_dv, PER + i * PER)
                    batch(i, 1, cl)
                    batch(i, 2, cl)
                    assert cl.n == PER
                batch(B // 2 - 1, 1, None, last=True)
                ch = Count(s_dv, PER * (B // 2))
                dve.wait_ge(s_lc, B + 1)
                dve.wait_ge(s_const, 5)

                w8b = w8[:, :].unsqueeze(1).to_broadcast([P, NT, E])

                def step(ins):
                    ch.inc(ins)
                    ch.wait(dve)

                ch.inc(dve.memset(fb, 0.0))
                step(dve.tensor_reduce(mx, logits[:, :, :], AX.X, ALU.max))
                dve.tensor_tensor(tmp[:, :, :], logits[:, :, :], bc8(mx), ALU.subtract).then_inc(s_z, 1)
                fallback_out(B // 2 - 1)
                dve.wait_ge(s_e, 1)
                step(dve.tensor_reduce(sm, pr[:, :, :], AX.X, ALU.add))
                step(dve.reciprocal(sm, sm))
                step(dve.tensor_tensor(pr[:, :, :], pr[:, :, :], bc8(sm), ALU.mult))
                for m, p, mask in ((0, p1, m1), (1, p2, m2)):
                    step(dve.tensor_reduce(p, pr[:, :, :], AX.X, ALU.max))
                    step(dve.tensor_tensor(tmp[:, :, :], pr[:, :, :], bc8(p), ALU.is_equal))
                    step(dve.tensor_tensor(tmp[:, :, :], tmp[:, :, :], w8b, ALU.mult))
                    step(dve.tensor_reduce(t1, tmp[:, :, :], AX.X, ALU.max))
                    step(dve.tensor_tensor(mask[:, :, :], tmp[:, :, :], bc8(t1), ALU.is_equal))
                    if m == 0:
                        step(dve.scalar_tensor_tensor(out=pr[:, :, :], in0=mask[:, :, :], scalar=-2.0,
                                                      in1=pr[:, :, :], op0=ALU.mult, op1=ALU.add))
                ch.inc(dve.tensor_tensor(assign[:, :, :], m1[:, :, :], m2[:, :, :], ALU.add))
                step(dve.tensor_tensor(t1, p1, p2, ALU.add))
                step(dve.tensor_scalar(t1, t1, 1e-9, None, ALU.max))
                step(dve.reciprocal(t1, t1))
                ch.inc(dve.tensor_tensor(p1, p1, t1, ALU.mult))
                step(dve.tensor_tensor(p2, p2, t1, ALU.mult))

            @block.scalar
            def _(act):
                act.wait_ge(s_rows, 16 * 4)
                act.activation(brows_dh.rearrange("r (d h) -> r h d", h=H), brows[:, :].rearrange("r (h d) -> r h d", d=D),
                               ACT.Copy).then_inc(s_bp, 1)
                act.wait_ge(s_wt, 1)
                act.activation(wT[:, 0:2, :].rearrange("p w (d h) -> p w h d", h=H),
                               pq[:, 0, 0:2 * P].rearrange("p (w h d) -> p w h d", w=2, d=D), ACT.Copy)
                act.activation(wT[:, 2:4, :], pq[:, 0, 2 * P:].rearrange("p (w c) -> p w c", c=P), ACT.Copy).then_inc(s_wtc, 1)
                act.wait_ge(s_wt, 2)
                act.activation(bT[:, 0:BQC], pl[:, 0, 0:BQC], ACT.Copy)
                act.activation(bT[:, BQC:], pl[:, 0, NBR + BQC:2 * NBR], ACT.Copy).then_inc(s_wtc, 1)
                act.sem_inc(s_g, 1)

                def copy_xnT(i, k):
                    act.wait_ge(s_tr, 2 * i + k + 2)
                    act.wait_ge(s_xst[k % 2], 16 * (i + k // 2) + 1)
                    act.activation(xnT[:, k % 2, :], pt[:, 0, :], ACT.Copy).then_inc(s_xnT, 1)

                def gelus(i, k, chunks):
                    for c in chunks if k == 1 else ():
                        act.wait_ge(s_h, FC * i + c + 1)
                        act.activation(hfb[:, c, :], ph[:, c % 2, :], ACT.Gelu,
                                       bias=bT[:, FB1C + c:FB1C + c + 1]).then_inc(s_g, 1)

                def batch(i, k, last=False):
                    n = 2 * i + k
                    act.wait_ge(s_st[k % 2], 32 * (i + k // 2) + 1)
                    for m in range(2):
                        act.wait_ge(s_qs, 2 * n + m + 2)
                        act.activation(parts[:, k % 2, m, 0, :], qs[:, m, :], ACT.Copy).then_inc(s_p1, 1)
                    gelus(i, k, (0, 1))
                    if not last:
                        copy_xnT(i, k + 1)
                    for m in range(2):
                        act.wait_ge(s_r1, 2 * n + m + 1)
                        act.activation(parts[:, k % 2, m, 1, :], rem[:, m, :], ACT.Copy).then_inc(s_p2, 1)
                    gelus(i, k, (2, 3))

                copy_xnT(0, 0)
                batch(0, 0)
                with act.Fori(0, B // 2 - 1) as i:
                    for k in (1, 2):
                        batch(i, k)
                batch(B // 2 - 1, 1, last=True)
                act.wait_ge(s_z, 1)
                act.activation(pr[:, :, :], tmp[:, :, :], ACT.Exp).then_inc(s_e, 1)

            @block.tensor
            def _(pe):
                pe.sem_inc(s_tr, 1)
                pe.wait_ge(s_const, 5)
                pe.wait_ge(s_wn, 64)
                for w in range(4):
                    mm = pe.transpose(pq[:, 0, w * P:(w + 1) * P], wn[:, w, :], ident[:, :])
                mm.then_inc(s_wt, 1)
                pe.wait_ge(s_rows, 16 * 4)
                pe.transpose(pl[:, 0, 0:NBR], brows[:, :], ident[0:NBR, 0:NBR])
                pe.wait_ge(s_bp, 1)
                pe.transpose(pl[:, 0, NBR:2 * NBR], brows_dh, ident[0:NBR, 0:NBR]).then_inc(s_wt, 1)

                def fb_first(f, chunks):
                    for c in chunks:
                        if c >= 2:
                            pe.wait_ge(s_g, FC * f + c)
                        pe.matmul(ph[:, c % 2, :], fw1_s[:, c * P:(c + 1) * P], xnT[:, 1, :],
                                  start=True, stop=True).then_inc(s_h, 1)

                def fb_second(f, tiles):
                    if 0 in tiles:
                        pe.wait_ge(s_g, FC * f + FC + 1)
                        pe.wait_ge(s_yc, f + 1)
                    for t in tiles:
                        for c in range(FC):
                            mm = pe.matmul(py[:, 0, t * P:(t + 1) * P], hfb[:, c, t * P:(t + 1) * P],
                                           fw2_s[:, c, :], start=(c == 0), stop=(c == FC - 1))
                    if TPB - 1 in tiles:
                        mm.then_inc(s_y, 1)

                def transpose_xn(n, k):
                    pe.wait_ge(s_xn, n + 1)
                    for j in range(TPB):
                        mm = pe.transpose(pt[:, 0, j * P:(j + 1) * P], xn_s[:, k % 2, j, :], ident[:, :])
                    mm.then_inc(s_tr, 1)

                def batch(i, k, last=False):
                    n = 2 * i + k
                    pe.wait_ge(s_xnT, n + 1)
                    pe.wait_ge(s_qs, 2 * n + 1)
                    for m in range(2):
                        pe.matmul(pq[:, m, :], wT[:, m, :], xnT[:, k % 2, :], start=True, stop=True).then_inc(s_qk, 1)
                    pe.wait_ge(s_lc, n + 1)
                    for j in range(TPB):
                        mm = pe.matmul(pl[:, 0, j * E:(j + 1) * E], xnT[:, k % 2, j * P:(j + 1) * P], wr_s[:, :],
                                       start=True, stop=True)
                    mm.then_inc(s_lg, 1)
                    if k == 1:
                        fb_first(i, (0, 1))
                    elif k == 2:
                        fb_second(i, (0, 1))
                    if not last:
                        transpose_xn(n + 1, k + 1)
                    if k == 1:
                        fb_first(i, (2, 3))
                    elif k == 2:
                        fb_second(i, (2, 3))

                transpose_xn(0, 0)
                pe.wait_ge(s_wl, 16)
                pe.wait_ge(s_wtc, 2)
                batch(0, 0)
                pe.wait_ge(b_w, 32)
                with pe.Fori(0, B // 2 - 1) as i:
                    for k in (1, 2):
                        batch(i, k)
                batch(B // 2 - 1, 1, last=True)
                fb_second(B // 2 - 1, range(TPB))

        NS = H * 10 // 8
        HS = NS // 4
        TS = 17
        EX0 = (0, 10)
        FB1, FB2 = (1, 3, 5, 7), (9, 10, 11, 12, 13, 14, 15, 16)
        CAP0 = 0
        FB1_0, FB2_0 = (9, 11, 12, 13), (14, 15, 16, 17, 18, 18, 19, 19)

        def slot_bank(s):
            return 4 if s % 2 else 2 * (s // 2 % 2)

        cm = ExitStack()
        hT = sb("hT", [P, 2, FC, CAP], c=cm)
        hf = hT[:, :, :, :].rearrange("p j c t -> p (j c t)")[:, 0:FC * T].rearrange("p (c t) -> p c t", c=FC)
        w1_s = sb("w1_s", [P, 2, F], c=cm)
        w2_s = sb("w2_s", [P, 2, FC, P], c=cm)
        assert NT * E == 2 * P
        xg_s = route[:, :, :].rearrange("p j n -> p (j n)").rearrange("p (k s c) -> p k s c", s=3, c=P)
        xgT = sb("xgT", [P, 2, CAP], c=cm)
        y_s = sb("y_s", [P, 2, 3, P], c=cm)
        blkmax = sb("blkmax", [P, 2, H * 10], c=cm)
        cp = sb("cp", [P, 2, 8, P], BF16, c=cm)
        half = sb("half", [P, 2, HS, 8, P // 2], BF16, c=cm)
        quarter = sb("quarter", [P, HS, 8, P // 4], BF16, c=cm)
        eighth = sb("eighth", [P, HS, 8, P // 8], BF16, c=cm)
        negm = sb("negm", [P, H, TPB], c=cm)
        shift = sb("shift", [P, 2, H, TPB], BF16, c=cm)
        shT = sb("shT", [P, 2, P], BF16, c=cm)
        pm = banks("pm", 6, cm)
        ph = banks("ph2", 2, cm)
        py = ph[:, 0:1, :]
        p_turn = ph[:, 1, 0:CAP]
        p_rank = ph[:, 1, 0:NT]
        p_shift = ph[:, 1, 0:P // 2].bitcast(BF16)

        b_i = sem("b_first_maxima_ready")
        b_s = sem("b_scores_in_psum")
        b_m = sem("b_block_maxima")
        b_cp = sem("b_odd_slot_copied")
        b_h = sem("b_odd_slot_halved")
        b_q = sem("b_odd_maxima_steps")
        b_n = sem("b_negated_maxima")
        b_hi = sem("b_shift_high")
        b_sh = sem("b_shift_ready")
        b_t = sem("b_shift_in_psum")
        b_tc = sem("b_shiftT_ready")
        b_st = [sem(f"b_shift_stored{i}") for i in range(2)]

        def slot_pieces(s):
            out, at = [], 0
            for h in range(H):
                for qt in range(TPB):
                    done, n = 0, TPB - qt
                    while done < n:
                        g = at // 8
                        m = min(n - done, 4 - at % 4)
                        if g == s:
                            out.append((h, qt, qt + done, m, at % 8))
                        at += m
                        done += m
            return out

        with cm, nc.Block() as block:

            @block.sync
            def _(sp):
                def next_qk(p, k):
                    sp.wait_ge(b_s, p * NS + NS)
                    sp.sem_inc(s_pass, 1)
                    load_qk(sp, B - 2 - p + 2 * k, k, b_ld[k])

                load_qk(sp, B - 1, 1, b_ld[1])
                HB = B // 4
                with sp.Fori(1, HB) as i:
                    for k in range(2):
                        next_qk(2 * i + k, k)
                        sp.wait_ge(s_y, B // 2 - 1 + 2 * i + k)
                        sp.sem_inc(s_pass, 1)
                        sp.dma_start(xT2[:, k, :], xnT_d[:, bass.ds((4 * i + 2 * k) * T, T)]).then_inc(s_xl[k], 16)
                next_qk(B // 2, 0)
                sp.wait_ge(s_sc, 16 * TOPK * NT)
                def next_experts(i, k):
                    for j in range(2):
                        e = 2 * (2 * i + k) + j
                        sp.wait_ge(s_y2, e + 1)
                        sp.sem_inc(s_pass, 1)
                        sp.dma_start(w1_s[:, j, :], W1.rearrange("e d f -> (e d) f")[bass.ds(e * P, P), :]).then_inc(s_we[j], 16)
                        sp.dma_start(w2_s[:, j, :, :],
                                     W2.rearrange("e f d -> (e f) d")[bass.ds(e * F, F), :].rearrange("(c p) n -> p c n", p=P)).then_inc(s_we[j], 16)
                        sp.dma_start(xg_s[:, j, 0:2, :],
                                     xg_d[bass.ds(e * CAP, 2 * P), :].rearrange("(s p) c -> p s c", p=P)).then_inc(s_we[j], 16)
                        sp.dma_start(xg_s[0:CAP - 2 * P, j, 2, :],
                                     xg_d[bass.ds(e * CAP + 2 * P, CAP - 2 * P), :]).then_inc(s_we[j], 16)

                next_experts(0, 0)
                next_qk(B // 2 + 1, 1)
                next_experts(0, 1)
                for k in range(2):
                    sp.wait_ge(s_y, B - 1 + k)
                    sp.dma_start(xT2[:, k, :], xnT_d[:, k * T:(k + 1) * T]).then_inc(a_ld[k], 16)
                with sp.Fori(1, HB) as i:
                    for k in range(2):
                        next_qk(B // 2 + 2 * i + k, k)
                        next_experts(i, k)
                sp.wait_ge(b_st[1], 16 * (B // 2) + 1)
                load_shifts(sp, 0, 0)

            @block.gpsimd
            def _(pool):
                pool.sem_inc(s_yst, 2)
                pool.memset(cp[:, 1, :, :], 0.0).then_inc(b_i, 1)
                pool.memset(half[:, 1, 0:HS - 1, :, :].bitcast(F32), 0.0).then_inc(b_i, 1)
                pool.memset(blkmax[:, 1, :], 0.0).then_inc(b_i, 1)
                pool.wait_ge(s_ix, 1)
                for t in range(NT):
                    for a in range(TOPK):
                        pool.indirect_dma_start(
                            out=xg_d[:, :], out_offset=bass.IndirectOffsetOnAxis(ap=idx[:, a, t:t + 1], axis=0),
                            in_=xn_all[:, t, :], in_offset=None,
                            bounds_check=SLOTS - 1, oob_is_err=False).then_inc(s_sc, 16)
                with pool.Fori(0, E // 2) as i:
                    for k in range(2):
                        e = 2 * i + k
                        pool.wait_ge(s_y2c, e + 2)
                        pool.dma_start(y_d[bass.ds(e * CAP, 2 * P), :].rearrange("(s p) c -> p s c", p=P),
                                       y_s[:, k, 0:2, :]).then_inc(s_ys[k], 16)
                        pool.dma_start(y_d[bass.ds(e * CAP + 2 * P, CAP - 2 * P), :],
                                       y_s[0:CAP - 2 * P, k, 2, :]).then_inc(s_ys[k], 16)
                        pool.wait_ge(s_ys[k], 32 * i + 32)
                        pool.sem_inc(s_yst, 1)

            @block.vector
            def _(dve):
                dve.sem_inc(b_m, 2)
                dve.sem_inc(b_q, 1)
                dve.sem_inc(b_h, 1)
                dve.sem_inc(b_sh, 1)
                dve.sem_inc(s_y2c, 1)

                def odd_maxima(n, k, h, step):
                    dve.wait_ge(b_q, 3 * (2 * n + h) + step + 4)
                    if step == 0:
                        dve.wait_ge(b_h, 2 * HS * n + HS * (h + 1) + 2)
                        dve.tensor_tensor(quarter[:, :, :, :], half[:, h, :, :, 0:P // 4], half[:, h, :, :, P // 4:],
                                          ALU.max).then_inc(b_q, 1)
                    elif step == 1:
                        dve.tensor_tensor(eighth[:, :, :, :], quarter[:, :, :, 0:P // 8], quarter[:, :, :, P // 8:],
                                          ALU.max).then_inc(b_q, 1)
                    else:
                        odd = blkmax[:, k, :].rearrange("p (t o b) -> p t o b", o=2, b=8)[:, HS * h:HS * (h + 1), 1, :]
                        dve.tensor_reduce(odd, eighth[:, :, :, :], AX.X, ALU.max).then_inc(b_q, 1)

                def halve(n, j):
                    dve.wait_ge(b_cp, 2 * HS * n + j + 2)
                    dve.tensor_tensor(half[:, j // HS, j % HS, :, :], cp[:, j % 2, :, 0:P // 2],
                                      cp[:, j % 2, :, P // 2:], ALU.max).then_inc(b_h, 1)

                def row_maxima(n, k):
                    dve.wait_ge(b_q, 6 * n + 4)
                    dve.wait_ge(b_m, n * (NS // 2) + 2)
                    dve.wait_ge(b_sh, n + 1)
                    v, at = blkmax[:, 1 - k, :].rearrange("p (h b) -> p h b", h=H), 0
                    for qt in range(TPB):
                        ins = dve.tensor_reduce(negm[:, :, qt], v[:, :, at:at + TPB - qt], AX.X, ALU.max, negate=True)
                        at += TPB - qt
                        ins.then_inc(b_n, 1)

                def shift_parts(n):
                    dve.wait_ge(b_n, TPB * n + TPB)
                    dve.wait_ge(b_t, n + 1)
                    dve.tensor_copy(shift[:, 0, :, :], negm[:, :, :]).then_inc(b_hi, 1)
                    dve.wait_ge(b_hi, n + 1)
                    dve.tensor_tensor(shift[:, 1, :, :], negm[:, :, :], shift[:, 0, :, :], ALU.subtract).then_inc(b_sh, 1)

                def finish(n, k, s):
                    if s == 0:
                        dve.wait_ge(b_i, 3)
                        halve(n - 1, NS // 2 - 1)
                    elif s in (2, 4, 6):
                        odd_maxima(n - 1, 1 - k, 1, s // 2 - 1)
                    elif s == 8:
                        row_maxima(n, k)
                    elif s == 10:
                        shift_parts(n)

                def maxima(n, k, extra):
                    for s in range(NS):
                        if s % 2 == 0:
                            dve.wait_ge(b_s, 2 * NS + n * NS + s + 1)
                            dve.tensor_reduce(blkmax[:, k, s * 8:s * 8 + 8],
                                              pm[:, slot_bank(s):slot_bank(s) + 2, :].rearrange("p a (b c) -> p (a b) c", c=P),
                                              AX.X, ALU.max).then_inc(b_m, 1)
                            if s >= 2:
                                halve(n, s // 2 - 1)
                            finish(n, k, s)
                        if s in (12, 14, 16):
                            odd_maxima(n, k, 0, (s - 12) // 2)
                        if s in extra:
                            extra[s]()

                def expert_out(e, j):
                    dve.wait_ge(s_y2, e + 3)
                    dve.wait_ge(s_yst, e + 1)
                    dve.tensor_tensor(y_s[:, j, 0:2, :], py[:, 0, 0:2 * P].rearrange("p (s c) -> p s c", c=P),
                                      bc[:, bass.ds(e * P, P)].unsqueeze(1).to_broadcast([P, 2, P]), ALU.add)
                    dve.tensor_tensor(y_s[0:CAP - 2 * P, j, 2, :], py[0:CAP - 2 * P, 0, 2 * P:3 * P],
                                      bc[0:CAP - 2 * P, bass.ds(e * P, P)], ALU.add).then_inc(s_y2c, 1)

                def fallback_out(n):
                    dve.wait_ge(s_y, B // 2 + n + 1)
                    dve.tensor_tensor(yfb_all[:, bass.ds(2 * n * TPB, TPB), :],
                                      py[:, 0, :].rearrange("p (j c) -> p j c", c=P),
                                      bcast("fb2").unsqueeze(1).to_broadcast([P, TPB, P]), ALU.add).then_inc(s_yc, 1)

                ch = Count(s_rc)

                def step(ins):
                    ch.inc(ins)
                    ch.wait(dve)

                def overflow(e):
                    dve.wait_ge(s_rk, e + 1)
                    ch.inc(dve.scalar_tensor_tensor(out=ovf[:, :], in0=p_rank, scalar=float(CAP),
                                                    in1=elig[:, e % 2, :], op0=ALU.is_gt, op1=ALU.mult))
                    dve.tensor_scalar(slotk[:, :, e], p_rank, float(e * CAP - 1), None, ALU.add).then_inc(s_rr, 1)
                    ch.wait(dve)
                    step(dve.tensor_tensor(fb, fb, ovf[:, :], ALU.max))

                def eligible(e):
                    step(dve.scalar_tensor_tensor(out=elig[:, e % 2, :], in0=fb, scalar=0.0, in1=assign[:, :, e],
                                                  op0=ALU.is_equal, op1=ALU.mult))
                    dve.tensor_tensor_scan(escan[:, e % 2, :], ones_nt[:, :], elig[:, e % 2, :], 0.0,
                                           ALU.mult, ALU.add).then_inc(s_el, 1)

                both = ((0, p1, m1, tmp, t1), (1, p2, m2, tmp2, t2))

                def chosen_slots():
                    dve.wait_ge(s_rr, E)
                    ch.inc(dve.tensor_scalar(fbn, fb, -1.0, 1.0, ALU.mult, ALU.add))
                    ch.inc(dve.tensor_copy(wgt[:, 2, :], fb))
                    for m, p, mask, prod, t in both:
                        ch.inc(dve.tensor_tensor(prod[:, :, :], slotk[:, :, :], mask[:, :, :], ALU.mult))
                    ch.wait(dve)

                def kept_slots():
                    for m, p, mask, prod, t in both:
                        ch.inc(dve.tensor_reduce(t, prod[:, :, :], AX.X, ALU.add))
                        ch.inc(dve.tensor_tensor(wgt[:, m, :], p, fbn, ALU.mult))
                    ch.wait(dve)

                def skip_others():
                    for m, p, mask, prod, t in both:
                        ch.inc(dve.tensor_tensor(t, t, fbn, ALU.mult))
                    ch.wait(dve)
                    for m, p, mask, prod, t in both:
                        ch.inc(dve.scalar_tensor_tensor(out=t, in0=fb, scalar=FAR, in1=t, op0=ALU.mult, op1=ALU.add))
                    ch.wait(dve)
                    for m, p, mask, prod, t in both:
                        ch.inc(dve.tensor_copy(idx[:, m, :], t))
                    ch.wait(dve)
                    dve.sem_inc(s_ix, 1)

                def routing(s):
                    if CAP0 < s <= CAP0 + E:
                        overflow(s - CAP0 - 1)
                    if CAP0 <= s < CAP0 + E:
                        eligible(s - CAP0)
                    if s >= CAP0 + E:
                        for at, piece in enumerate((chosen_slots, kept_slots, skip_others)):
                            if s == CAP0 + E + at:
                                piece()

                first = {s: lambda s=s: routing(s) for s in range(NS - 1)}
                first[NS - 1] = lambda: fallback_out(0)
                maxima(0, 0, first)
                maxima(1, 1, {18: lambda: fallback_out(1)})
                with dve.Fori(1, B // 4) as i:
                    for k in range(2):
                        n = 2 * i + k
                        maxima(n, k, {18: lambda: fallback_out(n)})
                with dve.Fori(0, B // 4) as i:
                    for k in range(2):
                        n = 2 * i + k
                        maxima(B // 2 + n, k, {9: lambda: expert_out(2 * n, 0),
                                               19: lambda: expert_out(2 * n + 1, 1)})
                for s in range(0, 11, 2):
                    finish(B, 0, s)

            @block.scalar
            def _(act):
                act.sem_inc(b_tc, 1)
                act.sem_inc(b_cp, 1)
                act.sem_inc(s_g2, 1)
                act.sem_inc(b_st[0], 1)
                act.sem_inc(b_st[1], 1)

                def shift_rows(n, k, i):
                    act.wait_ge(b_t, n + 2)
                    act.activation(shT[:, k, :], p_shift, ACT.Copy).then_inc(b_tc, 1)
                    act.wait_ge(b_tc, n + 2)
                    act.dma_start(sh_d.rearrange("b r t -> (b r) t")[bass.ds((B + 1 - n - 2 * k) * P, P), :], shT[:, k, :]).then_inc(b_st[k], 16)

                def copy_odd(n, s):
                    act.wait_ge(b_s, 2 * NS + n * NS + s + 1)
                    act.wait_ge(b_h, 2 * HS * n + s // 2 + 1)
                    act.activation(cp[:, (s // 2) % 2, :, :],
                                   pm[:, 4:6, :].rearrange("p a (b c) -> p (a b) c", c=P), ACT.Copy).then_inc(b_cp, 1)

                def gelu(e, j, c):
                    act.wait_ge(s_h2, FC * e + c + 1)
                    act.activation(hT[:, j, c, :], ph[:, c % 2, 0:CAP], ACT.Gelu,
                                   bias=bT[:, bass.ds(B1C + e * FC + c, 1)]).then_inc(s_g2, 1)

                def with_fallback(i, k, slots):
                    n = 2 * i + k
                    for s in range(NS):
                        if s % 2:
                            copy_odd(n, s)
                        if s in slots:
                            c = slots.index(s)
                            act.wait_ge(s_h, FC * (B // 2 + n) + c + 1)
                            act.activation(hf[:, c, :], ph[:, c % 2, :], ACT.Gelu,
                                           bias=bT[:, FB1C + c:FB1C + c + 1]).then_inc(s_g, 1)
                        if s == TS:
                            act.wait_ge(b_st[k], 16 * i + 1)
                            shift_rows(n, k, i)

                with_fallback(0, 0, FB1_0)
                with_fallback(0, 1, FB1)
                with act.Fori(1, B // 4) as i:
                    for k in range(2):
                        with_fallback(i, k, FB1)
                with act.Fori(0, B // 4) as i:
                    for k in range(2):
                        n = 2 * i + k
                        for s in range(NS):
                            if s % 2:
                                copy_odd(B // 2 + n, s)
                            for j in range(2):
                                o = s - EX0[j]
                                if o == 0:
                                    act.wait_ge(s_xt, 2 * n + j + 1)
                                    act.activation(xgT[:, j, :], p_turn, ACT.Copy).then_inc(s_xtc, 1)
                                if 1 <= o <= FC:
                                    gelu(2 * n + j, j, o - 1)
                            if s == TS:
                                act.wait_ge(b_st[k], 16 * (B // 4) + 16 * i + 1)
                                shift_rows(B // 2 + n, k, i)
                act.wait_ge(b_st[0], 16 * (B // 2) + 1)
                shift_rows(B, 0, 0)

            @block.tensor
            def _(pe):
                pe.sem_inc(b_s, 2 * NS)
                pe.sem_inc(b_t, 1)
                pe.sem_inc(s_y2, 2)
                pe.wait_ge(b_c, 2)

                def scores(n, k, s):
                    pe.wait_ge(b_cp if s % 2 else b_m, n * (NS // 2) + s // 2 + 1)
                    fresh = set()
                    for h, qt, kt, m, at in slot_pieces(s):
                        bank, c0 = slot_bank(s) + at // 4, (at % 4) * P
                        pe.matmul(pm[:, bank, c0:c0 + m * P], qT[0:QROWS, k, h, qt * P:(qt + 1) * P],
                                  kT[0:QROWS, k, h, kt * P:(kt + m) * P],
                                  start=bank not in fresh, stop=False, skip_group_check=True)
                        fresh.add(bank)
                    for h, qt, kt, m, at in slot_pieces(s):
                        bank, c0 = slot_bank(s) + at // 4, (at % 4) * P
                        if kt == qt:
                            mm = pe.matmul(pm[:, bank, c0:c0 + P], ident_bf[:, :], hide[:, :],
                                           start=False, stop=True, skip_group_check=True)
                    mm.then_inc(b_s, 1)

                def transpose_shifts(n):
                    pe.wait_ge(b_sh, n + 2)
                    pe.wait_ge(b_tc, n + 1)
                    pe.transpose(p_shift, shift[:, :, :, :].rearrange("p a h q -> p (a h q)"),
                                 ident_bf[:, :]).then_inc(b_t, 1)

                def batch_maxima(n, k, i, between):
                    pe.wait_ge(b_ld[k], 16 * 6 * (i + 1))
                    for s in range(NS):
                        scores(n, k, s)
                        for piece in between.get(s, ()):
                            piece()
                        if s == TS:
                            transpose_shifts(n)

                def fb_first(n, k, i, c):
                    if c == 0:
                        pe.wait_ge(s_xl[k], 16 * i + 16)
                        pe.wait_ge(s_yc, B // 2 + n + 1)
                    elif c == 1:
                        pe.wait_ge(b_tc, n + 1)
                    else:
                        pe.wait_ge(s_g, FC * (B // 2 + n) + c)
                    pe.matmul(ph[:, c % 2, :], fw1_s[:, c * P:(c + 1) * P], xT2[:, k, :],
                              start=True, stop=True).then_inc(s_h, 1)

                def fb_second(n, t, h):
                    if t == 0:
                        pe.wait_ge(s_g, FC * (B // 2 + n) + FC + h)
                    for c in range(FC // 2 * h, FC // 2 * (h + 1)):
                        mm = pe.matmul(py[:, 0, t * P:(t + 1) * P], hf[:, c, t * P:(t + 1) * P],
                                       fw2_s[:, c, :], start=(c == 0), stop=(c == FC - 1))
                    if t == TPB - 1 and h == 1:
                        mm.then_inc(s_y, 1)

                def ex_turn(e, j, n):
                    pe.wait_ge(s_we[j], 64 * n + 64)
                    pe.wait_ge(s_g2, FC * e + 1)
                    pe.wait_ge(b_tc, B // 2 + n + 1)
                    for s, (s0, rows) in enumerate(ST):
                        mm = pe.transpose(p_turn[:, s0:s0 + rows], xg_s[0:rows, j, s, :], ident[0:rows, 0:rows])
                    mm.then_inc(s_xt, 1)

                def ex_first(e, j, c):
                    if c == 0:
                        pe.wait_ge(s_xtc, e + 1)
                        pe.wait_ge(s_yc, B + 1)
                        pe.wait_ge(s_y2c, e + 1)
                    elif c >= 2:
                        pe.wait_ge(s_g2, FC * e + c)
                    pe.matmul(ph[:, c % 2, 0:CAP], w1_s[:, j, c * P:(c + 1) * P], xgT[:, j, :],
                              start=True, stop=True).then_inc(s_h2, 1)

                def ex_second(e, j, s, h):
                    if s == 0:
                        pe.wait_ge(s_g2, FC * e + FC + h)
                    s0, n = ST[s]
                    for c in range(FC // 2 * h, FC // 2 * (h + 1)):
                        mm = pe.matmul(py[0:n, 0, s * P:(s + 1) * P], hT[:, j, c, s0:s0 + n],
                                       w2_s[:, j, c, :], start=(c == 0), stop=(c == FC - 1))
                    if s == len(ST) - 1 and h == 1:
                        mm.then_inc(s_y2, 1)

                def rank(e):
                    pe.wait_ge(s_el, e + 1)
                    pe.matmul(p_rank, ones_bf[:, :], escan[:, e % 2, :], start=True, stop=False)
                    pe.matmul(p_rank, after_bf[:, :], elig[:, e % 2, :], start=False, stop=True).then_inc(s_rk, 1)

                def with_fallback(i, k, between, first=FB1, second=FB2):
                    n = 2 * i + k
                    for c in range(FC):
                        between.setdefault(first[c], []).append(lambda c=c: fb_first(n, k, i, c))
                    for t in range(TPB):
                        for h in range(2):
                            between.setdefault(second[2 * t + h], []).append(lambda t=t, h=h: fb_second(n, t, h))
                    batch_maxima(n, k, i, between)

                capacities = {CAP0 + 2 + e: [lambda e=e: rank(e)] for e in range(E)}
                capacities.setdefault(FB1_0[1], []).append(lambda: pe.wait_ge(s_rr, E))
                with_fallback(0, 0, capacities, FB1_0, FB2_0)
                with_fallback(0, 1, {})
                with pe.Fori(1, B // 4) as i:
                    for k in range(2):
                        with_fallback(i, k, {})
                with pe.Fori(0, B // 4) as i:
                    for k in range(2):
                        n = 2 * i + k
                        between = {}
                        for j in range(2):
                            e, o = 2 * n + j, EX0[j]
                            between.setdefault(o, []).append(lambda e=e, j=j: ex_turn(e, j, n))
                            for c in range(FC):
                                between.setdefault(o + 1 + c, []).append(lambda e=e, j=j, c=c: ex_first(e, j, c))
                            for s in range(len(ST)):
                                for h in range(2):
                                    at = min(o + 5 + 2 * s + h, o + 9)
                                    between.setdefault(at, []).append(lambda e=e, j=j, s=s, h=h: ex_second(e, j, s, h))
                        between.setdefault(TS, []).append(lambda: pe.wait_ge(s_g2, FC * (2 * n + 2) + 1))
                        batch_maxima(B // 2 + n, k, i + B // 4, between)
                transpose_shifts(B)

        c12.close()
        c2 = ExitStack()
        pb = sb("pb", [P, RING, UNIT], c=c2)
        o_raw = sb("o_raw", [P, 2, T], c=c2)
        rd = sb("rd", [P, 2, TPB, G], c=c2)
        oq = sb("oq", [P, 2, TPB, H, D], c=c2)
        oT = sb("oT", [P, T], c=c2)
        idx_s = sb("idx_s", [P, 2, TOPK, TPB], I32, c=c2)
        acc = sb("acc", [P, 2, TPB, P], c=c2)
        acc2 = sb("acc2", [P, 2, TPB, P], c=c2)
        res = sb("res", [P, 2, TPB, P], c=c2)
        ps = banks("ps", 4, c2)
        po = banks("po", 2, c2)
        pv = banks("pv", 1, c2)
        px = banks("px", 1, c2)

        a_v = sem("v_in_psum")
        a_vc = sem("v_ready")
        a_s = sem("scores_in_psum")
        a_e = sem("probs_ready")
        a_m = sem("probs_masked")
        a_pv = sem("pv_done")
        a_oc = sem("o_raw_ready")
        a_t = sem("o_transposed")
        a_rd = sem("recip_ready")
        a_oq = sem("o_normalised")
        a_ot = sem("oT_in_psum")
        a_otc = sem("oT_ready")
        a_op = sem("attn_in_psum")
        a_g = [sem(f"gathered{i}") for i in range(2)]
        a_pc = sem("pool_chain")
        a_acc = sem("rest_summed")
        a_res = sem("result_ready")
        a_ost = sem("results_stored")
        a_last = sem("last_out_stored")
        a_out = [sem(f"out_stored{i}") for i in range(2)]

        NU = 5
        NGR = H // G
        UB = NU * NGR

        PRE = [(0, g) for g in range(NGR)]
        BODY = [(k, g) for k in (1, 2) for g in range(NGR)]
        LAST = [(1, g) for g in range(NGR)]

        def ring(at):
            k, g, u = at
            return (k * UB + g * NU + u) % RING

        def pieces(u):
            if u < 2:
                return [(2 * u + a, 3, a * 512, 512) for a in range(2)]
            if u < 4:
                return [x for a in range(2) for x in ((2 * (u - 2) + a, 2, a * 512, 384),
                                                       (2 * (u - 2) + a, 0, a * 512 + 384, 128))]
            return [(a, 1, a * 256, 256) for a in range(4)]

        with c2, nc.Block() as block:

            @block.sync
            def _(sp):
                sp.wait_ge(b_st[0], 16 * (B // 2) + 17)
                load_shifts(sp, 1, 1)
                with sp.Fori(1, B // 2) as i:
                    for k in range(2):
                        n = 2 * i + k
                        sp.wait_ge(a_s, n * UB + UB)
                        sp.sem_inc(s_pass, 1)
                        sp.wait_ge(a_v, n + 1)
                        sp.sem_inc(s_pass, 1)
                        load_qk(sp, n, k, a_ld[k])
                        load_shifts(sp, n, k)
                        sp.dma_start(xT2[:, k, :], xnT_d[:, bass.ds(n * T, T)]).then_inc(a_ld[k], 16)
                sp.wait_ge(a_res, B + 2)
                sp.dma_start(out_rows[(B - 1) * T:B * T, :].rearrange("(j p) c -> p j c", p=P),
                             res[:, 1, :, :]).then_inc(a_last, 16)
                sp.wait_ge(a_last, 16)

            @block.gpsimd
            def _(pool):
                pool.sem_inc(a_ost, 2)
                STEPS = 8

                def rest(i, k):
                    n, slot = 2 * i + k, k % 2
                    tiles = bass.ds(n * TPB, TPB)
                    ch = Count(a_pc, n * STEPS)

                    def step(ins):
                        ch.inc(ins)
                        ch.wait(pool)

                    def wb(a):
                        return wgt[:, a, tiles].unsqueeze(2).to_broadcast([P, TPB, P])

                    step(pool.tensor_copy(idx_s[:, slot, :, :], idx[:, :, tiles]))
                    pool.sem_inc(s_pass, 1)
                    for j in range(TPB):
                        for a in range(TOPK):
                            pool.indirect_dma_start(
                                out=g1[:, slot, a, j, :], out_offset=None,
                                in_=y_d[:, :],
                                in_offset=bass.IndirectOffsetOnAxis(ap=idx_s[:, slot, a, j:j + 1], axis=0),
                                bounds_check=SLOTS - 1, oob_is_err=False).then_inc(a_g[slot], 16)
                    pool.wait_ge(a_res, n + 1)
                    step(pool.tensor_tensor(acc[:, slot, :, :], yfb_all[:, tiles, :], wb(2), ALU.mult))
                    step(pool.tensor_tensor(acc[:, slot, :, :], acc[:, slot, :, :], x_all[:, tiles, :], ALU.add))
                    step(pool.tensor_tensor(acc[:, slot, :, :], acc[:, slot, :, :],
                                            bcast("bo").unsqueeze(1).to_broadcast([P, TPB, P]), ALU.add))
                    pool.wait_ge(a_g[slot], 16 * TOPK * TPB * (i + k // 2 + 1))
                    for a in range(TOPK):
                        step(pool.tensor_tensor(acc2[:, slot, :, :], g1[:, slot, a, :, :], wb(a), ALU.mult))
                        step(pool.tensor_tensor(acc[:, slot, :, :], acc[:, slot, :, :], acc2[:, slot, :, :], ALU.add))
                    assert ch.n == STEPS
                    pool.sem_inc(a_acc, 1)

                def store(i, k):
                    n = 2 * i + k
                    pool.wait_ge(a_res, n + 3)
                    pool.dma_start(out_rows[bass.ds(n * T, T), :].rearrange("(j p) c -> p j c", p=P),
                                   res[:, k, :, :]).then_inc(a_out[k], 16)
                    pool.wait_ge(a_out[k], 16 * i + 16)
                    pool.sem_inc(a_ost, 1)

                rest(0, 0)
                with pool.Fori(0, B // 2 - 1) as i:
                    for k in range(2):
                        rest(i, k + 1)
                        store(i, k)
                rest(B // 2 - 1, 1)
                store(B // 2 - 1, 0)

            @block.scalar
            def _(act):
                act.sem_inc(a_e, 2)
                with act.Fori(0, B // 2) as i:
                    for k in range(2):
                        for u in range(UB):
                            n = i * 2 * UB + k * UB + u
                            act.wait_ge(a_s, 2 * UB + n + 1)
                            act.wait_ge(a_pv, n + 1)
                            r = (k * UB + u) % RING
                            s = 2 * (u % 2)
                            act.activation(pb[:, r, :], ps[:, s:s + 2, :].rearrange("p a c -> p (a c)"),
                                           ACT.Exp).then_inc(a_e, 1)

            @block.vector
            def _(dve):
                dve.sem_inc(a_res, 2)
                dve.sem_inc(a_oq, 1)
                dve.sem_inc(a_otc, 1)
                dve.sem_inc(a_oc, 2)

                def new_v(n, k):
                    dve.wait_ge(a_v, n + 3)
                    dve.tensor_tensor(v_s[:, k % 2, :, :, 0:D],
                                      pv[:, 0, :].rearrange("p (j h d) -> p j h d", h=H, d=D),
                                      bcast("bv").rearrange("p (h d) -> p h d", d=D).unsqueeze(1).to_broadcast([P, TPB, H, D]),
                                      ALU.add).then_inc(a_vc, 1)

                def hide_masked(un, u):
                    dve.wait_ge(a_e, un + 3)
                    r = ring(u)
                    if u[2] < 2:
                        v = pb[:, r, :].rearrange("p (a c) -> p a c", a=2)[:, :, 384:512]
                        m = keep_min[:, :].unsqueeze(1).to_broadcast([P, 2, P])
                    elif u[2] < 4:
                        v = pb[:, r, :].rearrange("p (a b c) -> p a b c", a=2, c=P)[:, :, 2:4, :]
                        m = keep_min[:, :].unsqueeze(1).unsqueeze(1).to_broadcast([P, 2, 2, P])
                    else:
                        v = pb[:, r, :].rearrange("p (a c) -> p a c", a=4)[:, :, P:2 * P]
                        m = keep_min[:, :].unsqueeze(1).to_broadcast([P, 4, P])
                    dve.tensor_tensor(v, v, m, ALU.min).then_inc(a_m, 1)

                def evacuate(gg, g):
                    dve.wait_ge(a_pv, RING + (gg + 1) * NU)
                    dve.wait_ge(a_t, gg + 1)
                    dve.tensor_copy(o_raw[:, g % 2, :], po[:, g % 2, :]).then_inc(a_oc, 1)

                def normalise(gg, k, g):
                    dve.wait_ge(a_t, gg + 3)
                    o4 = px[:, 0, :].rearrange("p (j h w) -> p j h w", h=G, w=W)
                    dve.wait_ge(a_oq, gg + 1)
                    dve.reciprocal(rd[:, g % 2, :, :], o4[:, :, :, D]).then_inc(a_rd, 1)
                    dve.wait_ge(a_rd, gg + 1)
                    for j in range(TPB):
                        ins = dve.tensor_tensor(oq[:, k % 2, j, g * G:(g + 1) * G, :], o4[:, j, :, 0:D],
                                                rd[:, g % 2, j, :].unsqueeze(2).to_broadcast([P, G, D]), ALU.mult)
                    ins.then_inc(a_oq, 1)

                def copy_oT(n):
                    dve.wait_ge(a_ot, n + 1)
                    dve.tensor_copy(oT[:, :], pv[:, 0, :]).then_inc(a_otc, 1)

                def result(n, k):
                    dve.wait_ge(a_op, n + 1)
                    dve.wait_ge(a_acc, n + 1)
                    dve.wait_ge(a_ost, n + 1)
                    dve.tensor_tensor(res[:, k % 2, :, :], pv[:, 0, :].rearrange("p (j c) -> p j c", c=P),
                                      acc[:, k % 2, :, :], ALU.add).then_inc(a_res, 1)

                def group(i, k, g, behind=NGR):
                    n = 2 * i + k
                    gg = n * NGR + g
                    for u in range(NU):
                        hide_masked(gg * NU + u, (k, g, u))
                        if u == 1 and behind > 1:
                            normalise(gg - 2, k - (g < 2), (g - 2) % NGR)
                        if u == 3 and behind > 0:
                            evacuate(gg - 1, (g - 1) % NGR)
                        if u == 2 and g == 0:
                            new_v(n, k)
                        if u == 3 and g == 2 and k > 0:
                            copy_oT(n - 1)
                        if u == 4 and g == 3 and k > 0:
                            result(n - 1, k - 1)

                for k, g in PRE:
                    group(0, k, g, behind=g)
                with dve.Fori(0, B // 2 - 1) as i:
                    for k, g in BODY:
                        group(i, k, g)
                for k, g in LAST:
                    group(B // 2 - 1, k, g)
                normalise(B * NGR - 2, 1, NGR - 2)
                evacuate(B * NGR - 1, NGR - 1)
                normalise(B * NGR - 1, 1, NGR - 1)
                copy_oT(B - 1)
                result(B - 1, 1)

            @block.tensor
            def _(pe):
                pe.sem_inc(a_s, 2 * UB)
                pe.sem_inc(a_v, 2)
                pe.sem_inc(a_pv, RING)
                pe.sem_inc(a_t, 2)

                def project_v(i, k):
                    pe.wait_ge(a_res, 2 * i + k + 1)
                    for j in range(TPB):
                        mm = pe.matmul(pv[:, 0, j * P:(j + 1) * P], xT2[:, k % 2, j * P:(j + 1) * P], wT[:, 2, :],
                                       start=True, stop=True)
                    mm.then_inc(a_v, 1)

                def scores(i, k, g, u):
                    pe.wait_ge(a_e, (2 * i + k) * UB + g * NU + u + 1)
                    s = 2 * ((g * NU + u) % 2)
                    for a, kt, c0, nq in pieces(u):
                        h = g * G + a
                        o = ps[:, s + c0 // 512, c0 % 512:c0 % 512 + nq]
                        mm = pe.matmul(o, kT[0:SROWS, k % 2, h, kt * P:(kt + 1) * P], qT[0:SROWS, k % 2, h, 0:nq],
                                       start=(c0 % 512 == 0), stop=True, skip_group_check=True)
                    mm.then_inc(a_s, 1)

                def weighted(i, k, g, kt):
                    gg = (2 * i + k) * NGR + g
                    us = {3: (0, 1), 2: (2, 3), 0: (2, 3), 1: (4,)}[kt]
                    if kt == 3:
                        pe.wait_ge(a_vc, 2 * i + k + 1)
                        pe.wait_ge(a_oc, gg + 1)
                    pe.wait_ge(a_m, gg * NU + us[-1] + 1)
                    for u in us:
                        for a, t, c0, nq in pieces(u):
                            if t == kt:
                                mm = pe.matmul(po[W * a:W * (a + 1), g % 2, 0:nq], v_s[:, k % 2, kt, g * G + a, :],
                                               pb[:, ring((k, g, u)), c0:c0 + nq], start=(kt == 3), stop=(kt == 1),
                                               skip_group_check=True)
                        if kt != 2:
                            mm.then_inc(a_pv, 1)

                def transposes(i, k, g):
                    gg = (2 * i + k) * NGR + g
                    pe.wait_ge(a_oc, gg + 3)
                    pe.wait_ge(a_oq, gg + 1)
                    for j in range(TPB):
                        mm = pe.transpose(px[:, 0, j * P:(j + 1) * P], o_raw[:, g % 2, j * P:(j + 1) * P], ident[:, :])
                    mm.then_inc(a_t, 1)

                def transpose_out(i, k, v_ahead=1):
                    n = 2 * i + k
                    pe.wait_ge(a_oq, NGR * n + NGR + 1)
                    pe.wait_ge(a_vc, n + 1 + v_ahead)
                    for j in range(TPB):
                        mm = pe.transpose(pv[:, 0, j * P:(j + 1) * P],
                                          oq[:, k % 2, j, :, :].rearrange("p h d -> p (h d)"), ident[:, :])
                    mm.then_inc(a_ot, 1)

                def project_out(i, k):
                    pe.wait_ge(a_otc, 2 * i + k + 2)
                    for j in range(TPB):
                        mm = pe.matmul(pv[:, 0, j * P:(j + 1) * P], oT[:, j * P:(j + 1) * P], wT[:, 3, :],
                                       start=True, stop=True)
                    mm.then_inc(a_op, 1)

                def group(i, k, g, behind=NGR):
                    before = (i, k - (g == 0), (g - 1) % NGR)
                    if g == 0:
                        pe.wait_ge(a_ld[k % 2], 16 * 8 * (i + k // 2) + 32)
                    for u in range(NU):
                        scores(i, k, g, u)
                        if behind > 0 and u != 1:
                            weighted(*before, {0: 3, 2: 2, 3: 0, 4: 1}[u])
                        if behind > 1 and u == 1:
                            transposes(i, k - (g < 2), (g - 2) % NGR)
                        if u == 1 and g == 0:
                            project_v(i, k)
                        if u == 3:
                            if g == 2 and k > 0:
                                transpose_out(i, k - 1)
                            if g == 3 and k > 0:
                                project_out(i, k - 1)

                for k, g in PRE:
                    group(0, k, g, behind=g)
                with pe.Fori(0, B // 2 - 1) as i:
                    for k, g in BODY:
                        group(i, k, g)
                i = B // 2 - 1
                for k, g in LAST:
                    group(i, k, g)
                for kt in (3, 2, 0, 1):
                    weighted(i, 1, NGR - 1, kt)
                    if kt == 3:
                        transposes(i, 1, NGR - 2)
                transposes(i, 1, NGR - 1)
                transpose_out(i, 1, v_ahead=0)
                project_out(i, 1)


_INS = ['L0_attn_x', 'L0_attn_Wq', 'L0_attn_bq', 'L0_attn_Wk', 'L0_attn_bk', 'L0_attn_Wv', 'L0_attn_bv',
        'L0_attn_Wo', 'L0_attn_bo', 'L0_attn_attn_scale', 'L0_ffn_Wr', 'L0_ffn_W1', 'L0_ffn_b1', 'L0_ffn_W2',
        'L0_ffn_b2', 'L0_ffn_fw1', 'L0_ffn_fb1', 'L0_ffn_fw2', 'L0_ffn_fb2']
_OUTS = [((B, T, P), 'float32')]


def kernel(**inputs):
    import numpy as _np
    import concourse.bacc as _bacc
    from concourse import mybir as _mybir
    from concourse.bass_utils import run_bass_kernel_spmd as _run

    nc = _bacc.Bacc("TRN2", target_bir_lowering=False, num_devices=1)
    arrays, args = {}, []
    for name in _INS:
        a = _np.ascontiguousarray(inputs[name])
        arrays[f"in_{name}_dram"] = a
        args.append(nc.dram_tensor(f"in_{name}_dram", a.shape, _mybir.dt.from_np(a.dtype), kind="ExternalInput").ap())
    for i, (shape, dtype) in enumerate(_OUTS):
        dt = _mybir.dt.from_np(_np.dtype(dtype))
        args.append(nc.dram_tensor(f"out_{i}_dram", shape, dt, kind="ExternalOutput").ap())
    moe_attention_kernel(nc, *args)
    r = _run(nc, [arrays], core_ids=[0])
    return r.results[0]["out_0_dram"]
```
